# Optimizing a Trainium2 kernel written in Bass

```python
import numpy as np
import jax
import jax.numpy as jnp

def _softmax(x, axis=-1):
    return jax.nn.softmax(x, axis=axis)

def _gelu(x):
    return jax.nn.gelu(x, approximate=True)

def _silu(x):
    return jax.nn.silu(x)

def _sigmoid(x):
    return jax.nn.sigmoid(x)

def _layernorm(x, axis=-1, eps=1e-05):
    m = jnp.mean(x, axis=axis, keepdims=True)
    v = jnp.var(x, axis=axis, keepdims=True)
    return (x - m) / jnp.sqrt(v + eps)

def _scatter_add(tgt, idx, src, axis=0):
    return tgt.at[idx].add(src)

def _segment_sum(src, seg, n):
    return jax.ops.segment_sum(src, seg, n)
kernel_name = 'mk_lm_tower_d2_tok_ids1024_r4_b1ab86'

def setup_inputs(seed: int=0):
    np.random.seed(seed)
    _w = jnp.asarray

    def _rec_inputs():
        import jax
        import jax.numpy as jnp
        _rk = jax.random.key(seed)
        x = jax.random.randint(jax.random.fold_in(_rk, 1), (2, 1024), 0, 12564, jnp.int32)
        return x
    x = _rec_inputs()

    def _L0_tok_setup():
        import jax, jax.numpy as jnp
        import numpy as np
        VOCAB = 50257
        DIM = 256
        R = 16
        ALPHA = 32
        SCALING = ALPHA / R
        key = jax.random.key(seed)
        k1, k2, k3, k4 = jax.random.split(key, 4)
        input_ids = jax.random.randint(k1, (4, 1024), 0, VOCAB)
        emb_weight = jax.random.normal(k2, (VOCAB, DIM), dtype=jnp.float32)
        lora_A = jax.random.normal(k3, (R, VOCAB), dtype=jnp.float32) * (1.0 / R)
        lora_B = jax.random.normal(k4, (DIM, R), dtype=jnp.float32) * 0.02
        return {'input': input_ids, 'emb_weight': emb_weight, 'lora_A': lora_A, 'lora_B': lora_B}
    _L0_tok_all = _L0_tok_setup()
    _L0_tok_in = {k: v for k, v in _L0_tok_all.items() if k in ('emb_weight', 'lora_A', 'lora_B')}
    del _L0_tok_all

    def _L0_attn_setup():
        import jax, jax.numpy as jnp
        import numpy as np
        import math
        D_MODEL = 256
        N_HEADS = 16
        SPARSITY = 0.3
        key = jax.random.key(seed)
        ks = jax.random.split(key, 12)
        B, S, D = (4, 512, D_MODEL)
        Dh = D // 2
        sc = 0.02
        inp = {'x': jax.random.normal(ks[0], (B, S, D), dtype=jnp.float32), 'wq': jax.random.normal(ks[1], (D, D), dtype=jnp.float32) * sc, 'bq': jnp.zeros((D,), jnp.float32), 'wk': jax.random.normal(ks[2], (D, D), dtype=jnp.float32) * sc, 'bk': jnp.zeros((D,), jnp.float32), 'wv': jax.random.normal(ks[3], (D, D), dtype=jnp.float32) * sc, 'bv': jnp.zeros((D,), jnp.float32), 'wo': jax.random.normal(ks[4], (D, D), dtype=jnp.float32) * sc, 'bo': jnp.zeros((D,), jnp.float32), 'wi1': jax.random.normal(ks[5], (Dh, D), dtype=jnp.float32) * sc, 'bi1': jnp.zeros((Dh,), jnp.float32), 'wi2': jax.random.normal(ks[6], (1, Dh), dtype=jnp.float32) * sc, 'bi2': jnp.zeros((1,), jnp.float32)}
        return inp
    _L0_attn_all = _L0_attn_setup()
    _L0_attn_in = {k: v for k, v in _L0_attn_all.items() if k in ('wq', 'bq', 'wk', 'bk', 'wv', 'bv', 'wo', 'bo', 'wi1', 'bi1', 'wi2', 'bi2')}
    del _L0_attn_all

    def _L0_ffn_setup():
        import jax, jax.numpy as jnp
        import numpy as np
        BS, SLEN, DIM = (1, 512, 256)
        NUM_EXPERTS, TOP_K = (8, 2)
        HID = 352

        def _masked_grouped_mm(x, w, onehot):
            g = jnp.einsum('tk,gnk->tgn', x, w, preferred_element_type=jnp.float32)
            return jnp.einsum('tgn,tg->tn', g, onehot)

        def moe_forward(x, gate_w, expert_bias, w_up, w_down, shared_w_up, shared_w_down):
            bs, slen, dim = x.shape
            xf = x.reshape(-1, dim)
            scores = jax.nn.sigmoid((xf @ gate_w.T).astype(jnp.float32))
            biased = scores + expert_bias
            _, sel = jax.lax.top_k(biased, TOP_K)
            top_scores = jnp.take_along_axis(scores, sel, axis=-1)
            flat_sel = sel.reshape(-1)
            counts = jnp.bincount(flat_sel, length=NUM_EXPERTS)
            order = jnp.argsort(flat_sel, stable=True)
            scores_sorted = top_scores.reshape(-1)[order]
            token_ids = order // TOP_K
            routed_in = (xf[token_ids] * scores_sorted[:, None]).astype(x.dtype)
            seg = jnp.repeat(jnp.arange(NUM_EXPERTS), counts, total_repeat_length=flat_sel.shape[0])
            onehot = jax.nn.one_hot(seg, NUM_EXPERTS, dtype=jnp.float32)
            h = _masked_grouped_mm(routed_in.astype(jnp.bfloat16), w_up.astype(jnp.bfloat16), onehot)
            h = jnp.square(jax.nn.relu(h.astype(jnp.bfloat16)))
            routed_out = _masked_grouped_mm(h.astype(jnp.bfloat16), w_down.astype(jnp.bfloat16), onehot)
            routed_out = routed_out.astype(jnp.bfloat16).astype(x.dtype)
            hs = jnp.square(jax.nn.relu(xf @ shared_w_up.T))
            shared_out = hs @ shared_w_down.T
            combined = jnp.zeros((flat_sel.shape[0], dim), routed_out.dtype).at[order].set(routed_out)
            out = combined.reshape(-1, TOP_K, dim).sum(axis=1) + shared_out
            return out.reshape(bs, slen, dim)
        key = jax.random.key(seed)
        k = jax.random.split(key, 6)
        s = 0.02
        return {'x': jax.random.normal(k[0], (BS, SLEN, DIM), jnp.float32), 'gate_w': jax.random.normal(k[1], (NUM_EXPERTS, DIM), jnp.float32) * s, 'expert_bias': jnp.zeros((NUM_EXPERTS,), jnp.float32), 'w_up': jax.random.normal(k[2], (NUM_EXPERTS, HID, DIM), jnp.float32) * s, 'w_down': jax.random.normal(k[3], (NUM_EXPERTS, DIM, HID), jnp.float32) * s, 'shared_w_up': jax.random.normal(k[4], (HID, DIM), jnp.float32) * s, 'shared_w_down': jax.random.normal(k[5], (DIM, HID), jnp.float32) * s}
    _L0_ffn_all = _L0_ffn_setup()
    _L0_ffn_in = {k: v for k, v in _L0_ffn_all.items() if k in ('gate_w', 'expert_bias', 'w_up', 'w_down', 'shared_w_up', 'shared_w_down')}
    del _L0_ffn_all

    def _L1_attn_setup():
        import jax, jax.numpy as jnp
        import numpy as np
        B, T, C = (2, 512, 256)
        LAT = 64
        N_HEAD = 16
        HEAD_DIM = C // N_HEAD
        SCALE = 1.0 / np.sqrt(HEAD_DIM).astype(np.float32)
        key = jax.random.key(seed)
        ks = jax.random.split(key, 9)
        s_in = 0.02
        return {'x': jax.random.normal(ks[0], (B, T, C), dtype=jnp.float32), 'wq_lat': jax.random.normal(ks[1], (C, LAT), dtype=jnp.float32) * s_in, 'wk_lat': jax.random.normal(ks[2], (C, LAT), dtype=jnp.float32) * s_in, 'wv_lat': jax.random.normal(ks[3], (C, LAT), dtype=jnp.float32) * s_in, 'wq_heads': jax.random.normal(ks[4], (LAT, C), dtype=jnp.float32) * s_in, 'wk_heads': jax.random.normal(ks[5], (LAT, C), dtype=jnp.float32) * s_in, 'wv_heads': jax.random.normal(ks[6], (LAT, C), dtype=jnp.float32) * s_in, 'w_proj': jax.random.normal(ks[7], (C, C), dtype=jnp.float32) * s_in, 'b_proj': jnp.zeros((C,), dtype=jnp.float32)}
    _L1_attn_all = _L1_attn_setup()
    _L1_attn_in = {k: v for k, v in _L1_attn_all.items() if k in ('wq_lat', 'wk_lat', 'wv_lat', 'wq_heads', 'wk_heads', 'wv_heads', 'w_proj', 'b_proj')}
    del _L1_attn_all

    def _L1_ffn_setup():
        import jax, jax.numpy as jnp
        import numpy as np
        DMODEL = 256
        N_EXPERTS = 32
        EXPERT_SIZE = 128
        N_HEADS = 4
        WEIGHT_SCALE = 1.0
        key = jax.random.key(seed)
        k0, k1, k2, k3 = jax.random.split(key, 4)
        x = jax.random.normal(k0, (2, 512, DMODEL), dtype=jnp.float32)
        expert_sel = jax.random.normal(k1, (N_EXPERTS, DMODEL), dtype=jnp.float32) * DMODEL ** (-0.5)
        keys = jax.random.normal(k2, (N_EXPERTS, DMODEL, EXPERT_SIZE), dtype=jnp.float32) * DMODEL ** (-0.5)
        values = jax.random.normal(k3, (N_EXPERTS, EXPERT_SIZE, DMODEL), dtype=jnp.float32) * (N_EXPERTS * EXPERT_SIZE) ** (-0.5)
        return {'x': x, 'expert_sel': expert_sel, 'keys': keys, 'values': values}
    _L1_ffn_all = _L1_ffn_setup()
    _L1_ffn_in = {k: v for k, v in _L1_ffn_all.items() if k in ('expert_sel', 'keys', 'values')}
    del _L1_ffn_all
    return {'x': x, 'L0_tok_emb_weight': _L0_tok_in['emb_weight'], 'L0_tok_lora_A': _L0_tok_in['lora_A'], 'L0_tok_lora_B': _L0_tok_in['lora_B'], 'L0_attn_wq': _L0_attn_in['wq'], 'L0_attn_bq': _L0_attn_in['bq'], 'L0_attn_wk': _L0_attn_in['wk'], 'L0_attn_bk': _L0_attn_in['bk'], 'L0_attn_wv': _L0_attn_in['wv'], 'L0_attn_bv': _L0_attn_in['bv'], 'L0_attn_wo': _L0_attn_in['wo'], 'L0_attn_bo': _L0_attn_in['bo'], 'L0_attn_wi1': _L0_attn_in['wi1'], 'L0_attn_bi1': _L0_attn_in['bi1'], 'L0_attn_wi2': _L0_attn_in['wi2'], 'L0_attn_bi2': _L0_attn_in['bi2'], 'L0_ffn_gate_w': _L0_ffn_in['gate_w'], 'L0_ffn_expert_bias': _L0_ffn_in['expert_bias'], 'L0_ffn_w_up': _L0_ffn_in['w_up'], 'L0_ffn_w_down': _L0_ffn_in['w_down'], 'L0_ffn_shared_w_up': _L0_ffn_in['shared_w_up'], 'L0_ffn_shared_w_down': _L0_ffn_in['shared_w_down'], 'L1_attn_wq_lat': _L1_attn_in['wq_lat'], 'L1_attn_wk_lat': _L1_attn_in['wk_lat'], 'L1_attn_wv_lat': _L1_attn_in['wv_lat'], 'L1_attn_wq_heads': _L1_attn_in['wq_heads'], 'L1_attn_wk_heads': _L1_attn_in['wk_heads'], 'L1_attn_wv_heads': _L1_attn_in['wv_heads'], 'L1_attn_w_proj': _L1_attn_in['w_proj'], 'L1_attn_b_proj': _L1_attn_in['b_proj'], 'L1_ffn_expert_sel': _L1_ffn_in['expert_sel'], 'L1_ffn_keys': _L1_ffn_in['keys'], 'L1_ffn_values': _L1_ffn_in['values']}

def reference(x, L0_tok_emb_weight, L0_tok_lora_A, L0_tok_lora_B, L0_attn_wq, L0_attn_bq, L0_attn_wk, L0_attn_bk, L0_attn_wv, L0_attn_bv, L0_attn_wo, L0_attn_bo, L0_attn_wi1, L0_attn_bi1, L0_attn_wi2, L0_attn_bi2, L0_ffn_gate_w, L0_ffn_expert_bias, L0_ffn_w_up, L0_ffn_w_down, L0_ffn_shared_w_up, L0_ffn_shared_w_down, L1_attn_wq_lat, L1_attn_wk_lat, L1_attn_wv_lat, L1_attn_wq_heads, L1_attn_wk_heads, L1_attn_wv_heads, L1_attn_w_proj, L1_attn_b_proj, L1_ffn_expert_sel, L1_ffn_keys, L1_ffn_values):
    import jax
    import jax.numpy as jnp

    def _L0_tok_ref(input, emb_weight, lora_A, lora_B):
        import jax, jax.numpy as jnp
        import numpy as np
        VOCAB = 50257
        DIM = 256
        R = 16
        ALPHA = 32
        SCALING = ALPHA / R
        orig_out = jnp.take(emb_weight, input, axis=0)
        a_rows = jnp.take(lora_A, input, axis=1)
        a_rows = jnp.moveaxis(a_rows, 0, -1)
        lora_out = jnp.einsum('bsr,dr->bsd', a_rows, lora_B) * SCALING
        return orig_out + lora_out

    def _L0_attn_ref(x, wq, bq, wk, bk, wv, bv, wo, bo, wi1, bi1, wi2, bi2):
        import jax, jax.numpy as jnp
        import numpy as np
        import math
        D_MODEL = 256
        N_HEADS = 16
        SPARSITY = 0.3
        B, S, D = x.shape
        H = N_HEADS
        hd = D // H
        k = max(1, int(S * SPARSITY))
        Q = (x @ wq.T + bq).reshape(B, S, H, hd).transpose(0, 2, 1, 3)
        K = (x @ wk.T + bk).reshape(B, S, H, hd).transpose(0, 2, 1, 3)
        V = (x @ wv.T + bv).reshape(B, S, H, hd).transpose(0, 2, 1, 3)
        h = jnp.maximum(x @ wi1.T + bi1, 0.0)
        importance = (h @ wi2.T + bi2)[..., 0]
        _, top_idx = jax.lax.top_k(importance, k)
        sparse_mask = jnp.zeros((B, S), dtype=x.dtype).at[jnp.arange(B)[:, None], top_idx].set(1.0)
        scores = jnp.einsum('bhqd,bhkd->bhqk', Q, K) / math.sqrt(hd)
        scores = jnp.where(sparse_mask[:, None, None, :] == 0, -jnp.inf, scores)
        attn = jax.nn.softmax(scores, axis=-1)
        out = jnp.einsum('bhqk,bhkd->bhqd', attn, V)
        out = out.transpose(0, 2, 1, 3).reshape(B, S, D)
        return out @ wo.T + bo

    def _L0_ffn_ref(x, gate_w, expert_bias, w_up, w_down, shared_w_up, shared_w_down):
        import jax, jax.numpy as jnp
        import numpy as np
        BS, SLEN, DIM = (1, 512, 256)
        NUM_EXPERTS, TOP_K = (8, 2)
        HID = 352

        def _masked_grouped_mm(x, w, onehot):
            g = jnp.einsum('tk,gnk->tgn', x, w, preferred_element_type=jnp.float32)
            return jnp.einsum('tgn,tg->tn', g, onehot)

        def moe_forward(x, gate_w, expert_bias, w_up, w_down, shared_w_up, shared_w_down):
            bs, slen, dim = x.shape
            xf = x.reshape(-1, dim)
            scores = jax.nn.sigmoid((xf @ gate_w.T).astype(jnp.float32))
            biased = scores + expert_bias
            _, sel = jax.lax.top_k(biased, TOP_K)
            top_scores = jnp.take_along_axis(scores, sel, axis=-1)
            flat_sel = sel.reshape(-1)
            counts = jnp.bincount(flat_sel, length=NUM_EXPERTS)
            order = jnp.argsort(flat_sel, stable=True)
            scores_sorted = top_scores.reshape(-1)[order]
            token_ids = order // TOP_K
            routed_in = (xf[token_ids] * scores_sorted[:, None]).astype(x.dtype)
            seg = jnp.repeat(jnp.arange(NUM_EXPERTS), counts, total_repeat_length=flat_sel.shape[0])
            onehot = jax.nn.one_hot(seg, NUM_EXPERTS, dtype=jnp.float32)
            h = _masked_grouped_mm(routed_in.astype(jnp.bfloat16), w_up.astype(jnp.bfloat16), onehot)
            h = jnp.square(jax.nn.relu(h.astype(jnp.bfloat16)))
            routed_out = _masked_grouped_mm(h.astype(jnp.bfloat16), w_down.astype(jnp.bfloat16), onehot)
            routed_out = routed_out.astype(jnp.bfloat16).astype(x.dtype)
            hs = jnp.square(jax.nn.relu(xf @ shared_w_up.T))
            shared_out = hs @ shared_w_down.T
            combined = jnp.zeros((flat_sel.shape[0], dim), routed_out.dtype).at[order].set(routed_out)
            out = combined.reshape(-1, TOP_K, dim).sum(axis=1) + shared_out
            return out.reshape(bs, slen, dim)
        return moe_forward(x, gate_w, expert_bias, w_up, w_down, shared_w_up, shared_w_down)

    def _L1_attn_ref(x, wq_lat, wk_lat, wv_lat, wq_heads, wk_heads, wv_heads, w_proj, b_proj):
        import jax, jax.numpy as jnp
        import numpy as np
        B, T, C = (2, 512, 256)
        LAT = 64
        N_HEAD = 16
        HEAD_DIM = C // N_HEAD
        SCALE = 1.0 / np.sqrt(HEAD_DIM).astype(np.float32)
        Bx, Tx, Cx = x.shape
        q = x @ wq_lat @ wq_heads
        k = x @ wk_lat @ wk_heads
        v = x @ wv_lat @ wv_heads
        q = q.reshape(Bx, Tx, N_HEAD, HEAD_DIM).transpose(0, 2, 1, 3)
        k = k.reshape(Bx, Tx, N_HEAD, HEAD_DIM).transpose(0, 2, 1, 3)
        v = v.reshape(Bx, Tx, N_HEAD, HEAD_DIM).transpose(0, 2, 1, 3)
        att = jnp.einsum('bhqd,bhkd->bhqk', q, k) * SCALE
        causal = jnp.tril(jnp.ones((Tx, Tx), dtype=bool))
        att = jnp.where(causal[None, None], att, -jnp.inf)
        att = jax.nn.softmax(att, axis=-1)
        y = jnp.einsum('bhqk,bhkd->bhqd', att, v)
        y = y.transpose(0, 2, 1, 3).reshape(Bx, Tx, Cx)
        return y @ w_proj + b_proj

    def _L1_ffn_ref(x, expert_sel, keys, values):
        import jax, jax.numpy as jnp
        import numpy as np
        DMODEL = 256
        N_EXPERTS = 32
        EXPERT_SIZE = 128
        N_HEADS = 4
        WEIGHT_SCALE = 1.0
        B, S, D = x.shape
        xt = x.reshape(-1, D)
        N = xt.shape[0]
        sel_logits = jnp.einsum('nd,ed->ne', xt, expert_sel)
        gates = jax.nn.sigmoid(sel_logits)
        sel_val, sel_idx = jax.lax.top_k(gates, N_HEADS)
        gate_full = jnp.zeros_like(gates).at[jnp.arange(N)[:, None], sel_idx].set(sel_val)
        scores = jax.nn.relu(jnp.einsum('nd,edf->nef', xt, keys))
        scores = scores * gate_full[:, :, None]
        out = jnp.einsum('nef,efv->nv', scores, values)
        return out.reshape(B, S, -1)
    h = _L0_tok_ref(x, L0_tok_emb_weight, L0_tok_lora_A, L0_tok_lora_B)
    h = h + _L0_attn_ref(_layernorm(h, axis=-1), L0_attn_wq, L0_attn_bq, L0_attn_wk, L0_attn_bk, L0_attn_wv, L0_attn_bv, L0_attn_wo, L0_attn_bo, L0_attn_wi1, L0_attn_bi1, L0_attn_wi2, L0_attn_bi2)
    h = h + _L0_ffn_ref(_layernorm(h, axis=-1), L0_ffn_gate_w, L0_ffn_expert_bias, L0_ffn_w_up, L0_ffn_w_down, L0_ffn_shared_w_up, L0_ffn_shared_w_down)
    h = h + _L1_attn_ref(_layernorm(h, axis=-1), L1_attn_wq_lat, L1_attn_wk_lat, L1_attn_wv_lat, L1_attn_wq_heads, L1_attn_wk_heads, L1_attn_wv_heads, L1_attn_w_proj, L1_attn_b_proj)
    h = h + _L1_ffn_ref(_layernorm(h, axis=-1), L1_ffn_expert_sel, L1_ffn_keys, L1_ffn_values)
    return h

_drawn_inputs = setup_inputs


def setup_inputs(seed=0):
    import zlib

    import numpy as np

    out = dict(_drawn_inputs(seed))
    spreads = {'L0_attn_bq': (0.0, 0.8),
     'L0_attn_bk': (0.0, 2.0),
     'L0_attn_bv': (0.0, 0.1),
     'L0_attn_bo': (0.0, 0.1),
     'L0_attn_bi1': (0.0, 0.586),
     'L0_ffn_expert_bias': (0.0, 0.1),
     'L1_attn_b_proj': (0.0, 0.484)}
    factors = {'L0_tok_lora_A': 2.822,
     'L0_tok_lora_B': 2.673,
     'L0_attn_wq': 8.0,
     'L0_attn_wk': 8.0,
     'L0_attn_wv': 3.13,
     'L0_attn_wi1': 2.83,
     'L1_attn_wq_lat': 8.0,
     'L1_attn_wk_lat': 8.0,
     'L1_attn_wv_lat': 7.237,
     'L1_attn_wq_heads': 8.0,
     'L1_attn_wk_heads': 8.0,
     'L1_attn_wv_heads': 8.0,
     'L1_attn_w_proj': 7.749}
    for name, (base, spread) in spreads.items():
        noise = np.random.default_rng([zlib.crc32(name.encode()), seed]).standard_normal(out[name].shape)
        drawn = base * np.exp(spread * noise) if base else spread * noise
        out[name] = jnp.asarray(drawn.astype(out[name].dtype))
    for name, factor in factors.items():
        out[name] = (out[name] * factor).astype(out[name].dtype)
    return out
```

```python
from contextlib import ExitStack

import concourse.bass as bass
from concourse import mybir
from concourse.bass import ds

F32 = mybir.dt.float32
BF16 = mybir.dt.bfloat16
I32 = mybir.dt.int32
U32 = mybir.dt.uint32
ALU = mybir.AluOpType
ACT = mybir.ActivationFunctionType
AX = mybir.AxisListType

P = 128
B, S, D = 2, 1024, 256
N = B * S
NT = N // P
KD = D // P
QW = 512
NQ = N // QW
TQ = QW // P
R = 16
H, HD = 16, 16
G4 = 4
NU = B * H // G4
TOPK = int(S * 0.3)
CK = 103
KCH = [(c, min(CK, TOPK - c)) for c in range(0, TOPK, CK)]
QROWS = 96
E0, HID = 8, 352
HCH = [(c, min(P, HID - c)) for c in range(0, HID, P)]
LAT = 64
E1, F1, TOP1 = 32, 128, 4
EPS = 1e-5
MASKED = -1.0e30
QPART = [0, 0, 1, 1, 0, 2]
KPART = [0, 1, 0, 1, 2, 0]


def unit_plan(layer):
    if layer == 0:
        exps = [(qh, c, n, 0, QW) for qh in range(2) for c, (_, n) in enumerate(KCH)]
        maxes = [(qt, 0, TOPK, h, 1) for qt in range(S // P) for h in range(G4)]
    else:
        exps = []
        for qh in range(2):
            for c in range(4 * (qh + 1)):
                first = max(0, c * P - qh * QW)
                exps.append((qh, c, P, first, QW - first))
        maxes = []
        for qt in range(S // P):
            for k0 in range(0, (qt + 1) * P, QW):
                w = min(QW, (qt + 1) * P - k0)
                per = min(G4, QW // w)
                maxes += [(qt, k0, w, h, per) for h in range(0, G4, per)]
    plan, s = [], 0
    for g in range(len(exps)):
        plan += [("scores", g, 0), ("scores", g, 1)]
        upto = (g + 1) * len(maxes) // len(exps)
        half = (s + upto) // 2
        plan += [("max", i, 0) for i in range(s, half)]
        if g:
            plan.append(("values", g - 1, 0))
            if exps[g - 1][0] != exps[g][0]:
                plan.append(("norm", exps[g - 1][0], 0))
        plan += [("max", i, 0) for i in range(half, upto)]
        s = upto
    plan += [("maxrow", 0, 0), ("values", len(exps) - 1, 0), ("norm", 1, 0)]
    return exps, maxes, plan


def lm_tower(nc, ids, table, loraB, wq, wk, wv, wo, wi1, wi2, bq, bk, bv, bo, bi1, bi2,
             gate_w, e_bias, w_up, w_down, sh_up, sh_down,
             wq_lat, wk_lat, wv_lat, wq_heads, wk_heads, wv_heads, w_proj, b_proj,
             e_sel, e_keys, e_values, out):
    with ExitStack() as ctx:
        def sb(name, shape, dt=F32):
            return ctx.enter_context(nc.sbuf_tensor(name, shape, dt))

        def sem(name):
            return ctx.enter_context(nc.semaphore(name))

        ps = ctx.enter_context(nc.psum_tensor("ps", [P, 8, 512], F32))

        h = sb("h", [P, NT, D])
        xn = sb("xn", [P, NT, D])
        xT = sb("xT", [P, KD, N])
        oT = sb("oT", [P, NU, S])
        vaug = sb("vaug", [P, NU, 8, G4, 32])
        arena = sb("arena", [P, 16384])

        qs = arena[:, 0:4096].bitcast(BF16).rearrange("p (a h t) -> p a h t", a=2, h=G4)
        ks = arena[:, 4096:8192].bitcast(BF16).rearrange("p (a h t) -> p a h t", a=2, h=G4)
        pT = arena[:, 8192:12288].rearrange("p (a h t) -> p a h t", a=2, h=G4)
        rcp = arena[:, 12288:12800]
        rcb = arena[:, 12800:13312]
        vst = arena[:, 13312:15360].rearrange("p (a c j r) -> p a c j r", a=2, c=8, j=G4)
        rows = arena[:, 0:NT * (D + R)].rearrange("p (t d) -> p t d", t=NT)
        aT = arena[0:R, 8192:8192 + N]
        hi = arena[:, 0:1024].rearrange("p (a t) -> p a t", a=2)
        sel = arena[:, 1024:1024 + 8 * TOPK].rearrange("p (t k) -> p t k", t=8)
        xcT = arena[:, 4096:4096 + KD * TOPK].rearrange("p (k n) -> p k n", k=KD)
        junk = arena[:, 5120:6144]
        qf = arena[:, 6144:7168].rearrange("p (a t) -> p a t", a=2)
        rem = arena[:, 7168:8192].rearrange("p (a t) -> p a t", a=2)
        parts = arena[:, 8192:9728].bitcast(BF16).rearrange("p (a s t) -> p a s t", a=2, s=3)
        latqk = arena[:, 9728:10752].rearrange("p (a t) -> p a t", a=2)
        latv = arena[:, 10752:11776].rearrange("p (a t) -> p a t", a=2)
        up_sb = arena[:, 0:2816].bitcast(BF16).rearrange("p (k e f) -> p k e f", k=KD, e=E0)
        dn_sb = arena[:, 2816:5888].bitcast(BF16).rearrange("p (m e d) -> p m e d", m=3, e=E0)
        shu_sb = arena[:, 5888:6592].rearrange("p (k f) -> p k f", k=KD)
        shd_sb = arena[:, 6592:7360].rearrange("p (m d) -> p m d", m=3)
        hsf = arena[:, 7360:8896].rearrange("p (m t) -> p m t", m=3)
        hs = arena[:, 8896:10432].rearrange("p (m t) -> p m t", m=3)
        xs = arena[:, 10432:10944].bitcast(BF16).rearrange("p (t d) -> p t d", t=TQ)
        xeT = arena[:, 10944:11968].bitcast(BF16).rearrange("p (a k t) -> p a k t", a=2, k=KD)
        hr = arena[:, 11968:12736].bitcast(BF16).rearrange("p (m t) -> p m t", m=3)
        hq = arena[:, 12736:14272].bitcast(BF16).rearrange("p (a m t) -> p a m t", a=2, m=3)
        ge, sc, eq, hit = (arena[:, 14336 + 512 * i:14848 + 512 * i].rearrange("p (t e) -> p t e", t=NT)
                           for i in range(4))
        ek = arena[:, 0:512].rearrange("p (a k f) -> p a k f", a=2, k=KD)
        ev = arena[:, 512:1024].rearrange("p (a d) -> p a d", a=2)
        hx = arena[:, 1024:5120].rearrange("p (a t) -> p a t", a=2)

        ids_sb = sb("ids_sb", [P, NT], I32)
        loraB_sb = sb("loraB_sb", [R, D])
        wq_sb = sb("wq_sb", [P, KD, D])
        wk_sb = sb("wk_sb", [P, KD, D])
        wv_sb = sb("wv_sb", [P, KD, D])
        wi1_sb = sb("wi1_sb", [P, KD, P])
        wi2_sb = sb("wi2_sb", [P, 1])
        wpad = sb("wpad", [P, G4, D])
        gw_sb = sb("gw_sb", [P, KD, E0])
        es_sb = sb("es_sb", [P, KD, E1])
        wl_sb = sb("wl_sb", [P, KD, 4, LAT])
        wh_sb = sb("wh_sb", [P, 3, D])
        bq_sb = sb("bq_sb", [P, KD])
        bq4 = sb("bq4", [P, KD])
        bk_sb = sb("bk_sb", [P, KD])
        bi1_sb = sb("bi1_sb", [P, 1])
        bi2_sb = sb("bi2_sb", [P, 1])
        bv_sb = sb("bv_sb", [P, D])
        bo_sb = sb("bo_sb", [P, D])
        bp_sb = sb("bp_sb", [P, D])
        eb_sb = sb("eb_sb", [P, E0])
        ident = sb("ident", [P, P])
        identb = sb("identb", [P, P], BF16)
        causal = sb("causal", [P, P], BF16)
        before = sb("before", [P, P])
        iota = sb("iota", [P, TOPK])
        eps = sb("eps", [P, 1])
        post = sb("post", [P, 2])
        st = sb("st", [P, TQ, 6])
        mv = sb("mv", [P, TQ, 2])
        sd = sb("sd", [P, TQ])
        rstd = sb("rstd", [P, TQ])
        impc = sb("impc", [P, B, 8])
        rkp = sb("rkp", [P, 8, 4])
        rank = sb("rank", [P, 8])
        mA = sb("mA", [P, G4, 8])
        mB = sb("mB", [P, G4, 4])
        mbf = sb("mbf", [P, G4, 8], BF16)
        mT = sb("mT", [32, 2, P], BF16)
        bi = sb("bi", [P, NT, E0])
        mx8 = sb("mx8", [P, NT, 8])
        ix8 = sb("ix8", [P, NT, 8], U32)
        ixf = sb("ixf", [P, NT, 8])
        g0 = sb("g0", [P, NT, E0])
        g1 = sb("g1", [P, NT, E1])

        qd = nc.dram_tensor("q_parts", [3, B, D, S], BF16, kind="Internal").ap()
        kd = nc.dram_tensor("k_parts", [3, B, D, S], BF16, kind="Internal").ap()

        ids_in, table_in = sem("ids_in"), [sem(f"rows_in{c}") for c in range(NQ)]
        w_emb, w_l0, w_l0b, w_pad, w_l1 = sem("w_emb"), sem("w_l0"), sem("w_l0b"), sem("w_pad"), sem("w_l1")
        w_moe, w_moeb = sem("w_moe"), sem("w_moeb")
        consts = sem("consts")
        vlink = sem("vlink")
        plink = sem("plink")
        act_left, dve_left = sem("act_left_psum"), sem("dve_left_psum")
        aT_mm, aT_sb = sem("aT_mm"), sem("aT_sb")
        prod, taken = sem("quad_product"), sem("quad_taken")
        var_in, sd_in, xn_in = sem("var_ready"), sem("sd_ready"), sem("xn_ready")
        tr_mm, xT_in = sem("xn_transposed"), sem("xT_ready")
        biased = sem("bias_in_residual")
        ih_mm, hi_in, imp_mm, imp_in = sem("ih_mm"), sem("hi_ready"), sem("imp_mm"), sem("imp_ready")
        impb_mm, sel_in, xc_mm, xc_in = sem("impb_mm"), sem("sel_ready"), sem("xc_mm"), sem("xc_ready")
        pc_mm, pc_f, pc_12, pc_3 = sem("piece_mm"), sem("piece_f"), sem("piece_12"), sem("piece_3")
        pc_out = [sem("piece_out0"), sem("piece_out1")]
        v_mm, v_in = sem("v_mm"), sem("v_ready")
        lat_mm, lat_in = sem("lat_mm"), sem("lat_ready")
        gate_mm, gate_e, gate_in = sem("gate_mm"), sem("gate_e"), sem("gate_ready")
        qk_in = [[sem(f"qk_in{l}{a}") for a in range(2)] for l in range(2)]
        mrow_in = [[sem(f"mrow_in{l}{a}") for a in range(2)] for l in range(2)]
        st_mm = [sem(f"scores_ready{l}") for l in range(2)]
        p_in = [sem(f"probs_ready{l}") for l in range(2)]
        p_cut = [sem(f"probs_masked{l}") for l in range(2)]
        p_free = [sem(f"probs_free{l}") for l in range(2)]
        o_free = [sem(f"out_bank_free{l}") for l in range(2)]
        mx_mm = [sem(f"max_scores{l}") for l in range(2)]
        mx_free = [sem(f"max_bank_free{l}") for l in range(2)]
        m_in = [sem(f"max_ready{l}") for l in range(2)]
        mT_in = [sem(f"max_row_ready{l}") for l in range(2)]
        vst_in = [sem(f"unit_values{l}") for l in range(2)]
        sh_mm, sh_f, sh_in, sh_dn = sem("sh_mm"), sem("sh_relu"), sem("sh_square"), sem("sh_down")
        xs_in, xe_mm, xe_in = sem("xs_ready"), sem("xe_mm"), sem("xe_ready")
        up_mm, up_f, up_in, dn_mm = sem("up_mm"), sem("up_relu"), sem("up_square"), sem("down_done")
        ew_in = [sem("expert_weights0"), sem("expert_weights1")]
        ex_mm, ex_f, ey_mm, ey_add = sem("ex_up"), sem("ex_relu"), sem("ex_down"), sem("ex_added")
        stored = sem("stored")

        NCONST = 9
        PLANS = [unit_plan(0), unit_plan(1)]
        NPC0 = 12

        def kparts(w, k=KD):
            return w.rearrange("(k p) n -> p k n", k=k)

        def arena_free(eng, layer):
            eng.wait_ge(v_mm, 6 if layer == 0 else 6 + NT)
            eng.wait_ge(act_left, 2 if layer == 0 else 6)
            eng.wait_ge(dve_left, 2 if layer == 0 else 6)

        block = ctx.enter_context(nc.Block())

        @block.sync
        def _(sp):
            sp.dma_start(ids_sb[:], ids).then_inc(ids_in, 16)
            sp.dma_start(loraB_sb[:], loraB).then_inc(w_emb, 16)
            for dst, src in ((wi1_sb[:], kparts(wi1)), (wi2_sb[:], wi2), (bi1_sb[:], bi1),
                             (bi2_sb[:], bi2.partition_broadcast(P)),
                             (wq_sb[:], kparts(wq)), (bq_sb[:], bq)):
                sp.dma_start(dst, src).then_inc(w_l0, 16)
            for dst, src in ((wk_sb[:], kparts(wk)), (wv_sb[:], kparts(wv)), (bk_sb[:], bk),
                             (bv_sb[:], bv.partition_broadcast(P)),
                             (bo_sb[:], bo.partition_broadcast(P))):
                sp.dma_start(dst, src).then_inc(w_l0b, 16)
            sp.wait_ge(consts, NCONST)
            for j in range(G4):
                sp.dma_start(wpad[32 * j:32 * j + HD, :, :],
                             wo.rearrange("(g j r) n -> j r g n", g=G4, j=G4)[j]).then_inc(w_pad, 16)
            for i, w in enumerate((wq_lat, wk_lat, wv_lat, wv_lat)):
                sp.dma_start(wl_sb[:, :, i, :], kparts(w)).then_inc(w_l1, 16)
            for i, (w, r) in enumerate(((wq_heads, 0), (wk_heads, LAT), (wv_heads, 0))):
                sp.dma_start(wh_sb[r:r + LAT, i, :], w).then_inc(w_l1, 16)
            for dst, src in ((bp_sb[:], b_proj.partition_broadcast(P)), (gw_sb[:], kparts(gate_w)),
                             (eb_sb[:], e_bias.partition_broadcast(P)), (es_sb[:], kparts(e_sel))):
                sp.dma_start(dst, src).then_inc(w_l1, 16)

            def store_pieces(first, n, where):
                for s in range(first, first + n):
                    sp.wait_ge(pc_3, s + 1)
                    sp.wait_ge(pc_12, s + 1)
                    dst, b, cg, c0, w = where(s - first)
                    sp.dma_start(dst[:, b, cg * P:(cg + 1) * P, c0:c0 + w].rearrange("s p t -> p s t"),
                                 parts[:, s % 2, :, 0:w]).then_inc(pc_out[s % 2], 16)

            def attention_dma(layer):
                nk = TOPK if layer == 0 else S

                def load(u, a):
                    for src, dst, sel_, w in ((qd, qs, QPART, S), (kd, ks, KPART, nk)):
                        for r, part in enumerate(sel_):
                            rows_ = src[part].rearrange("b (g j r) t -> (b g) r j t", g=G4, j=G4)
                            sp.dma_start(dst[16 * r:16 * r + 16, a, :, 0:w],
                                         rows_[ds(u, 1), :, :, 0:w].rearrange("o r j t -> (o r) j t"))\
                              .then_inc(qk_in[layer][a], 16)

                def mrow(u, a):
                    sp.wait_ge(mT_in[layer], u + 1)
                    sp.dma_start(qs[QROWS:QROWS + 1, a, :, :].rearrange("o h (q j) -> o (h q) j", j=P),
                                 mT[:, a, :]).then_inc(mrow_in[layer][a], 16)

                last = len(PLANS[layer][0])
                arena_free(sp, layer)
                load(0, 0)
                load(1, 1)
                mrow(0, 0)
                with sp.Fori(0, NU - 3, 2) as u:
                    for a in range(2):
                        mrow(u + a + 1, 1 - a)
                        sp.wait_ge(p_free[layer], 2 + last * (u + a + 1))
                        load(u + a + 2, a)
                mrow(NU - 1, 1)

            def q0(i):
                b, i = divmod(i, 6)
                return (qd, b, i // 2, (i % 2) * QW, QW) if i < 4 else (kd, b, i - 4, 0, TOPK)

            store_pieces(0, NPC0, q0)
            for a in range(2):
                sp.wait_ge(pc_out[a], 16 * NPC0 // 2)
            attention_dma(0)

            sp.wait_ge(dve_left, 3)
            sp.wait_ge(act_left, 3)
            sp.dma_start(shu_sb[:, :, :], kparts(sh_up)).then_inc(w_moe, 16)
            for m, (c, n) in enumerate(HCH):
                sp.dma_start(shd_sb[0:n, m, :], sh_down[c:c + n, :]).then_inc(w_moe, 16)
            sp.wait_ge(prod, 8)
            for j in range(G4):
                sp.dma_start(wpad[32 * j:32 * j + HD, :, :],
                             w_proj.rearrange("(g j r) n -> j r g n", g=G4, j=G4)[j]).then_inc(w_pad, 16)

            def q1(i):
                c, i = divmod(i, 4)
                return (qd if i < 2 else kd, c // 2, i % 2, (c % 2) * QW, QW)

            store_pieces(NPC0, 16, q1)
            for a in range(2):
                sp.wait_ge(pc_out[a], 16 * (NPC0 + 16) // 2)
            attention_dma(1)

            def expert(e, a):
                sp.dma_start(ek[:, a, :, :], e_keys.rearrange("e (k p) f -> e p k f", k=KD)[ds(e, 1), :, :, :]
                             .rearrange("o p k f -> (o p) k f")).then_inc(ew_in[a], 16)
                sp.dma_start(ev[:, a, :], e_values[ds(e, 1), :, :].rearrange("o p n -> (o p) n")).then_inc(ew_in[a], 16)

            sp.wait_ge(dve_left, 7)
            sp.wait_ge(act_left, 7)
            expert(0, 0)
            expert(1, 1)
            with sp.Fori(0, E1 - 3, 2) as e:
                for a in range(2):
                    sp.wait_ge(ey_mm, NT // 2 * (e + a + 1))
                    expert(e + a + 2, a)
            for c in range(NQ):
                sp.wait_ge(ey_add, 8 + NT * (E1 - 1) + (c + 1) * TQ)
                sp.dma_start(out[c * QW:(c + 1) * QW, :].rearrange("(t p) d -> p t d", p=P),
                             h[:, c * TQ:(c + 1) * TQ, :]).then_inc(stored, 16)
            sp.wait_ge(stored, 16 * NQ)

        @block.gpsimd
        def _(pool):
            own = [0]

            def link(ins):
                own[0] += 1
                ins.then_inc(plink, 1)
                pool.wait_ge(plink, own[0])

            pool.wait_ge(ids_in, 16)
            for t in range(NT):
                nc.gpsimd.indirect_dma_start(
                    rows[:, t, :], None, table,
                    bass.IndirectOffsetOnAxis(ids_sb[:, t:t + 1].bitcast(U32), 0)).then_inc(table_in[t // TQ], 16)
            link(nc.gpsimd.memset(ident[:], 0.0))
            nc.gpsimd.affine_select(out=ident[:], in_=ident[:], compare_op=ALU.not_equal, fill=1.0, base=0,
                                    pattern=[[-1, P]], channel_multiplier=1).then_inc(consts, 1)
            pool.wait_ge(consts, 1)
            nc.gpsimd.tensor_copy(identb[:], ident[:]).then_inc(consts, 1)
            link(nc.gpsimd.memset(causal[:], 0.0))
            nc.gpsimd.affine_select(out=causal[:], in_=causal[:], compare_op=ALU.is_ge, fill=MASKED, base=0,
                                    pattern=[[-1, P]], channel_multiplier=1).then_inc(consts, 1)
            link(nc.gpsimd.memset(before[:], 1.0))
            nc.gpsimd.affine_select(out=before[:], in_=before[:], compare_op=ALU.is_gt, fill=0.0, base=0,
                                    pattern=[[-1, P]], channel_multiplier=1).then_inc(consts, 1)
            nc.gpsimd.iota(iota[:], pattern=[[1, TOPK]], base=0, channel_multiplier=0,
                           allow_small_or_imprecise_dtypes=True).then_inc(consts, 1)
            nc.gpsimd.memset(eps[:], EPS).then_inc(consts, 1)
            nc.gpsimd.memset(wpad[:], 0.0).then_inc(consts, 1)
            nc.gpsimd.memset(wh_sb[:], 0.0).then_inc(consts, 1)
            nc.gpsimd.memset(vaug[:], 1.0).then_inc(consts, 1)

            def add_bias(first, bias):
                for c in range(NQ):
                    pool.wait_ge(xn_in, first + c + 1)
                    hc = h[:, c * TQ:(c + 1) * TQ, :]
                    nc.gpsimd.tensor_tensor(hc, hc, bias[:].unsqueeze(1).broadcast_to([P, TQ, D]), ALU.add)\
                      .then_inc(biased, 1)

            def third_parts(first, n, width):
                for s in range(first, first + n):
                    w = width(s - first)
                    pool.wait_ge(pc_12, s + 1)
                    if s >= 2:
                        pool.wait_ge(pc_out[s % 2], 16 * (s // 2))
                    nc.gpsimd.tensor_tensor(parts[:, s % 2, 2, 0:w], rem[:, s % 2, 0:w], parts[:, s % 2, 1, 0:w],
                                            ALU.subtract).then_inc(pc_3, 1)

            def attention_pool(layer):
                exps, _, plan = PLANS[layer]
                nch = len(KCH) if layer == 0 else 8
                rows_ = CK if layer == 0 else P
                cuts = [g for g, e in enumerate(exps) if layer == 1 and e[1] * P >= e[0] * QW]

                def stage_values(u, a):
                    nc.gpsimd.tensor_copy(vst[0:rows_, a, 0:nch, :, :].rearrange("p c j r -> p (c j r)"),
                                          vaug[0:rows_, ds(u, 1), 0:nch, :, :].rearrange("p u c j r -> p (u c j r)"))\
                      .then_inc(vst_in[layer], 1)

                def unit(u, a):
                    for i, g in enumerate(cuts):
                        pool.wait_ge(p_in[layer], 2 * len(exps) * u + 2 * g + 2)
                        pool.wait_ge(p_cut[layer], len(cuts) * u + i + 1)
                        nc.gpsimd.tensor_tensor(post[:, 0:1], eps[:], eps[:], ALU.add)
                        d = pT[:, g % 2, :, 0:P]
                        nc.gpsimd.affine_select(out=d, in_=d, compare_op=ALU.is_ge, fill=0.0, base=0,
                                                pattern=[[0, G4], [1, P]], channel_multiplier=-1)\
                          .then_inc(p_cut[layer], 1)

                arena_free(pool, layer)
                for a in range(2):
                    nc.gpsimd.memset(ks[QROWS:QROWS + 1, a, :, :], -1.0).then_inc(vst_in[layer], 1)
                pool.sem_inc(p_cut[layer], 1)
                pool.wait_ge(vst_in[layer], 2)
                pool.wait_ge(v_in, 6 if layer == 0 else 6 + NT)
                stage_values(0, 0)
                stage_values(1, 1)
                with pool.Fori(0, NU - 3, 2) as u:
                    for a in range(2):
                        unit(u + a, a)
                        pool.wait_ge(p_free[layer], 2 + len(exps) * (u + a + 1))
                        stage_values(u + a + 2, a)
                unit(NU - 2, 0)
                unit(NU - 1, 1)

            pool.wait_ge(w_l0b, 16 * 5)
            add_bias(0, bo_sb)
            third_parts(0, NPC0, lambda i: QW if i % 6 < 4 else TOPK)
            pool.wait_ge(pc_out[0], 16 * NPC0 // 2)
            pool.wait_ge(pc_out[1], 16 * NPC0 // 2)
            attention_pool(0)
            pool.wait_ge(dve_left, 3)
            pool.wait_ge(act_left, 3)
            for k in range(KD):
                nc.gpsimd.dma_start(up_sb[:, k, :, :], w_up[k * P:(k + 1) * P, :].rearrange("p (e f) -> p e f", e=E0))\
                  .then_inc(w_moeb, 16)
            for m, (c, n) in enumerate(HCH):
                nc.gpsimd.dma_start(dn_sb[0:n, m, :, :], w_down[c:c + n, :].rearrange("p (e d) -> p e d", e=E0))\
                  .then_inc(w_moeb, 16)
            pool.wait_ge(w_l1, 16 * 11)
            add_bias(8, bp_sb)
            third_parts(NPC0, 16, lambda i: QW)
            pool.wait_ge(pc_out[0], 16 * (NPC0 + 16) // 2)
            pool.wait_ge(pc_out[1], 16 * (NPC0 + 16) // 2)
            attention_pool(1)

        @block.vector
        def _(dve):
            own = [0]

            def link(ins):
                own[0] += 1
                ins.then_inc(vlink, 1)
                dve.wait_ge(vlink, own[0])

            def layernorm(i, c):
                for t in range(TQ):
                    ins = nc.vector.bn_stats(st[:, t, :], h[:, c * TQ + t, :])
                link(ins)
                for t in range(TQ):
                    ins = nc.vector.bn_aggr(mv[:, t, :], st[:, t, :])
                ins.then_inc(var_in, 1)
                dve.wait_ge(sd_in, 4 * i + c + 1)
                link(nc.vector.reciprocal(rstd[:], sd[:]))
                for t in range(TQ):
                    ins = nc.vector.tensor_scalar(xn[:, c * TQ + t, :], h[:, c * TQ + t, :], mv[:, t, 0:1],
                                                  rstd[:, t:t + 1], ALU.subtract, ALU.mult)
                ins.then_inc(xn_in, 1)

            def quad_banks(c):
                return ps[:, 2 * (c % 2):2 * (c % 2) + 2, :].rearrange("p a (b d) -> p (a b) d", d=D)

            def split_piece(s, w, first_of_stage=2):
                a = s % 2
                dve.wait_ge(pc_f, s + 1)
                if s >= 2:
                    dve.wait_ge(pc_out[a], 16 * (s // 2))
                    dve.wait_ge(pc_3, s - 1)
                link(nc.vector.tensor_copy(parts[:, a, 0, 0:w], qf[:, a, 0:w]))
                link(nc.vector.tensor_tensor(rem[:, a, 0:w], qf[:, a, 0:w], parts[:, a, 0, 0:w], ALU.subtract))
                nc.vector.tensor_copy(parts[:, a, 1, 0:w], rem[:, a, 0:w]).then_inc(pc_12, 1)

            def attention_dve(layer):
                exps, maxes, plan = PLANS[layer]
                ne, nm = len(exps), len(maxes) + 1
                half_end = [max(g for g, e in enumerate(exps) if e[0] == qh) for qh in range(2)]

                def max_step(i, u, a):
                    qt, k0, w, hd, per = maxes[i]
                    bank = 4 + (a * nm + i) % 2
                    dve.wait_ge(mx_mm[layer], nm * u + i + 1)
                    if layer == 0:
                        o = mbf[:, hd:hd + per, qt]
                    else:
                        o = mA[:, hd:hd + per, qt] if k0 == 0 else mB[:, hd:hd + per, qt - 4]
                    nc.vector.tensor_reduce(o, ps[:, bank, 0:per * w].rearrange("p (j k) -> p j k", j=per),
                                            AX.X, ALU.max).then_inc(mx_free[layer], 1)
                    if i < len(maxes) - 1:
                        return
                    dve.wait_ge(mx_free[layer], 2 + nm * u + nm - 1)
                    if layer == 0:
                        nc.vector.tensor_copy(mbf[:, :, 0:1], mbf[:, :, 0:1]).then_inc(m_in[layer], 1)
                    else:
                        nc.vector.tensor_copy(mbf[:, :, 0:4], mA[:, :, 0:4])
                        nc.vector.tensor_tensor(mbf[:, :, 4:8], mA[:, :, 4:8], mB[:, :, :], ALU.max)\
                          .then_inc(m_in[layer], 1)

                def max_row(u, a):
                    bank = 4 + (a * nm + nm - 1) % 2
                    dve.wait_ge(mx_mm[layer], nm * u + nm)
                    nc.vector.tensor_copy(mT[:, a, :], ps[0:32, bank, 0:64].bitcast(BF16))\
                      .then_inc(mx_free[layer], 1)
                    dve.wait_ge(mx_free[layer], 2 + nm * (u + 1))
                    dve.sem_inc(mT_in[layer], 1)

                def norm(qh, u):
                    o = ps[:, 6 + qh, :]
                    dve.wait_ge(p_free[layer], 2 + ne * u + half_end[qh] + 1)
                    nc.vector.reciprocal(rcp, o).then_inc(o_free[layer], 1)
                    dve.wait_ge(o_free[layer], 2 + 6 * u + 3 * qh + 1)
                    nc.vector.tensor_copy(post[:, 1:2], eps[:])
                    nc.vector.stream_shuffle(rcb, rcp, [HD] * 32).then_inc(o_free[layer], 1)
                    dve.wait_ge(o_free[layer], 2 + 6 * u + 3 * qh + 2)
                    nc.vector.tensor_tensor(oT[:, ds(u, 1), qh * QW:(qh + 1) * QW].rearrange("p u t -> p (u t)"),
                                            o, rcb, ALU.mult).then_inc(o_free[layer], 1)

                def unit(u, a, more):
                    for what, i, _ in plan:
                        if what == "max" and more:
                            max_step(i, u + 1, 1 - a)
                        elif what == "maxrow" and more:
                            max_row(u + 1, 1 - a)
                        elif what == "norm":
                            norm(i, u)

                dve.sem_inc(mx_free[layer], 2)
                dve.sem_inc(o_free[layer], 2)
                for i in range(len(maxes)):
                    max_step(i, 0, 0)
                max_row(0, 0)
                with dve.Fori(0, NU - 3, 2) as u:
                    unit(u, 0, True)
                    unit(u + 1, 1, True)
                unit(NU - 2, 0, True)
                unit(NU - 1, 1, False)

            def pick(scores, ne, ntop, values, gates, n8):
                for t in range(NT):
                    ins = nc.vector.max(mx8[:, t, :], values[:, t, :])
                link(ins)
                for t in range(NT):
                    ins = nc.vector.max_index(ix8[:, t, :], mx8[:, t, :], values[:, t, :])
                link(ins)
                link(nc.vector.tensor_copy(ixf[:], ix8[:]))
                io = iota[:, 0:ne].unsqueeze(1).broadcast_to([P, NT, ne])
                for j in range(ntop):
                    dst = hit if j == 0 else eq
                    link(nc.vector.tensor_tensor(dst[:, :, 0:ne], io, ixf[:, :, j:j + 1].broadcast_to([P, NT, ne]),
                                                 ALU.is_equal))
                    if j:
                        link(nc.vector.tensor_tensor(hit[:, :, 0:ne], hit[:, :, 0:ne], eq[:, :, 0:ne], ALU.add))
                nc.vector.tensor_tensor(gates[:], scores, hit[:, :, 0:ne], ALU.mult).then_inc(gate_in, 1)

            dve.wait_ge(consts, NCONST)
            for c in range(NQ):
                dve.wait_ge(table_in[c], 16 * TQ)
                dve.wait_ge(prod, c + 1)
                for half in range(2):
                    t0 = c * TQ + 2 * half
                    ins = nc.vector.scalar_tensor_tensor(
                        h[:, t0:t0 + 2, :], quad_banks(c)[:, 2 * half:2 * half + 2, :], 2.0,
                        rows[:, t0:t0 + 2, 0:D], ALU.mult, ALU.add)
                ins.then_inc(taken, 1)
                dve.wait_ge(taken, c + 1)
                layernorm(0, c)
            dve.sem_inc(dve_left, 1)

            dve.wait_ge(w_l0, 16 * 6)
            link(nc.vector.tensor_scalar(bq4[:], bq_sb[:], 0.25, None, ALU.mult))
            dve.sem_inc(consts, 1)
            for b in range(B):
                dve.wait_ge(imp_mm, b + 1)
                nc.vector.tensor_scalar(impc[:, b, :], ps[:, 6 + b, 0:8], bi2_sb[:], None, ALU.add)\
                  .then_inc(imp_in, 1)
            dve.wait_ge(imp_in, B)
            dve.wait_ge(w_l0b, 16 * 5)
            for b in range(B):
                dve.wait_ge(impb_mm, b + 1)
                row = ps[:, 4:6, :].rearrange("p a n -> p (a n)")
                for t in range(8):
                    me = impc[:, b, t:t + 1]
                    lo, hi_ = t * P, (t + 1) * P
                    if t > 0:
                        nc.vector.tensor_scalar(junk[:, 0:lo], row[:, 0:lo], me, None, ALU.is_ge, ALU.add,
                                                accum_out=rkp[:, t, 0:1])
                    else:
                        nc.vector.memset(rkp[:, t, 0:1], 0.0)
                    if t < 7:
                        nc.vector.tensor_scalar(junk[:, hi_:S], row[:, hi_:S], me, None, ALU.is_gt, ALU.add,
                                                accum_out=rkp[:, t, 1:2])
                    else:
                        nc.vector.memset(rkp[:, t, 1:2], 0.0)
                    link(nc.vector.tensor_scalar(junk[:, lo:hi_], row[:, lo:hi_], me, None, ALU.is_gt, ALU.add,
                                                 accum_out=rkp[:, t, 2:3]))
                    link(nc.vector.scalar_tensor_tensor(junk[:, lo:hi_], row[:, lo:hi_], me, before[:], ALU.is_equal,
                                                        ALU.mult, accum_out=rkp[:, t, 3:4]))
                link(nc.vector.tensor_reduce(rank[:], rkp[:], AX.X, ALU.add))
                if b:
                    dve.wait_ge(xc_mm, b)
                for t in range(8):
                    ins = nc.vector.tensor_scalar(sel[:, t, :], iota[:], rank[:, t:t + 1], None, ALU.is_equal)
                ins.then_inc(sel_in, 1)
                dve.wait_ge(sel_in, b + 1)
                for i in range(4):
                    split_piece(6 * b + i, QW)
                for i in range(4, 6):
                    split_piece(6 * b + i, TOPK)
                for c, (_, n) in enumerate(KCH):
                    dve.wait_ge(v_mm, 3 * b + c + 1)
                    nc.vector.tensor_tensor(
                        vaug[0:n, 4 * b:4 * b + 4, c, :, 0:HD],
                        ps[0:n, 2 + (3 * b + c) % 2, 0:D].rearrange("p (g j r) -> p g j r", g=G4, j=G4),
                        bv_sb[0:n, :].rearrange("p (g j r) -> p g j r", g=G4, j=G4), ALU.add).then_inc(v_in, 1)
            dve.wait_ge(v_in, 6)
            dve.sem_inc(dve_left, 1)

            attention_dve(0)
            dve.wait_ge(o_free[0], 2 + 6 * NU)
            dve.sem_inc(dve_left, 1)

            def project(i):
                for c in range(NQ):
                    hc = h[:, c * TQ:(c + 1) * TQ, :]
                    dve.wait_ge(prod, 4 * (i if i == 1 else 2) + c + 1)
                    dve.wait_ge(biased, 4 * (0 if i == 1 else 1) + c + 1)
                    nc.vector.tensor_tensor(hc, quad_banks(c), hc, ALU.add).then_inc(taken, 1)
                    dve.wait_ge(taken, 4 * i + c + 1)
                    layernorm(i, c)
                dve.sem_inc(dve_left, 1)

            def sigmoid(ne, n):
                dve.wait_ge(gate_e, n)
                link(nc.vector.tensor_scalar(sc[:, :, 0:ne], ge[:, :, 0:ne], 1.0, None, ALU.add))
                link(nc.vector.reciprocal(sc[:, :, 0:ne], sc[:, :, 0:ne]))

            project(1)
            sigmoid(E0, 1)
            link(nc.vector.tensor_tensor(bi[:], sc[:, :, 0:E0], eb_sb[:].unsqueeze(1).broadcast_to([P, NT, E0]), ALU.add))
            pick(sc[:, :, 0:E0], E0, 2, bi, g0, E0)
            dve.wait_ge(gate_in, 1)
            for c in range(NQ):
                def scaled(e, first):
                    if not first:
                        dve.wait_ge(xe_mm, E0 * c + e)
                    for t in range(TQ):
                        tt = c * TQ + t
                        ins = nc.vector.tensor_scalar(xs[:, t, :], xn[:, tt, :],
                                                      g0[:, tt, ds(e, 1)], None, ALU.mult)
                    ins.then_inc(xs_in, 1)

                def squares(e, a):
                    for m, (_, n) in enumerate(HCH):
                        dve.wait_ge(up_f, 3 * (E0 * c + e) + m + 1)
                        ins = nc.vector.tensor_tensor(hq[0:n, a, m, :], hr[0:n, m, :], hr[0:n, m, :], ALU.mult)
                        ins.then_inc(up_in, 1)

                for m, (_, n) in enumerate(HCH):
                    dve.wait_ge(sh_f, 3 * c + m + 1)
                    if c:
                        dve.wait_ge(sh_dn, c)
                    nc.vector.tensor_tensor(hs[0:n, m, :], hsf[0:n, m, :], hsf[0:n, m, :], ALU.mult).then_inc(sh_in, 1)
                if c:
                    dve.wait_ge(xe_mm, E0 * c)
                scaled(0, True)
                scaled(1, False)
                if c:
                    dve.wait_ge(dn_mm, E0 * c + 1)
                squares(0, 0)
                with dve.Fori(0, E0 - 3, 2) as e:
                    for a in range(2):
                        scaled(e + a + 2, False)
                        dve.wait_ge(dn_mm, E0 * c + e + a + 1)
                        squares(e + a + 1, 1 - a)
                dve.wait_ge(dn_mm, E0 * c + E0 - 1)
                squares(E0 - 1, 1)
                hc = h[:, c * TQ:(c + 1) * TQ, :]
                dve.wait_ge(dn_mm, E0 * (c + 1) + 1)
                nc.vector.tensor_tensor(hc, ps[:, 0:2, :].rearrange("p a (b d) -> p (a b) d", d=D), hc, ALU.add)\
                  .then_inc(taken, 1)
            dve.wait_ge(taken, 12)
            dve.sem_inc(dve_left, 1)

            for c in range(NQ):
                layernorm(2, c)
            for c in range(NQ):
                for i in range(4):
                    split_piece(NPC0 + 4 * c + i, QW)
                for t in range(TQ):
                    n = c * TQ + t
                    dve.wait_ge(v_mm, 6 + n + 1)
                    nc.vector.tensor_copy(
                        vaug[:, 4 * (n // 8):4 * (n // 8) + 4, n % 8, :, 0:HD],
                        ps[:, 6 + n % 2, 0:D].rearrange("p (g j r) -> p g j r", g=G4, j=G4)).then_inc(v_in, 1)
            dve.wait_ge(v_in, 6 + NT)
            dve.sem_inc(dve_left, 1)
            attention_dve(1)
            dve.wait_ge(o_free[1], 2 + 6 * NU)
            dve.sem_inc(dve_left, 1)
            project(3)
            sigmoid(E1, 2)
            pick(sc[:, :, :], E1, TOP1, sc, g1, E1)
            dve.wait_ge(gate_in, 2)
            dve.sem_inc(ey_add, 8)
            with dve.Fori(0, E1) as e:
                for t in range(NT):
                    dve.wait_ge(ey_mm, NT // 2 * e + t // 2 + 1)
                    nc.vector.scalar_tensor_tensor(h[:, t, :], ps[:, 4 + (t // 2) % 4, (t % 2) * D:(t % 2 + 1) * D],
                                                   g1[:, t, ds(e, 1)], h[:, t, :], ALU.mult, ALU.add)\
                      .then_inc(ey_add, 1)

        @block.scalar
        def _(act):
            def ln_scalar(i, c):
                act.wait_ge(var_in, 4 * i + c + 1)
                nc.scalar.activation(sd[:], mv[:, :, 1], ACT.Sqrt, bias=eps[:]).then_inc(sd_in, 1)
                act.wait_ge(tr_mm, 4 * i + c + 1)
                nc.scalar.activation(xT[:, :, c * QW:(c + 1) * QW], ps[:, 4 + 2 * (c % 2):6 + 2 * (c % 2), :],
                                     ACT.Copy).then_inc(xT_in, 1)

            def piece(s, w, scale, bias):
                a = s % 2
                act.wait_ge(pc_mm, s + 1)
                if s >= 2:
                    act.wait_ge(pc_12, s - 1)
                nc.scalar.activation(qf[:, a, 0:w], ps[:, a, 0:w], ACT.Identity, bias=bias, scale=scale)\
                  .then_inc(pc_f, 1)

            def attention_act(layer):
                exps, _, plan = PLANS[layer]
                ne = len(exps)

                def unit(u, a):
                    for g, (qh, c, n, first, w) in enumerate(exps):
                        for pair in range(2):
                            k = 2 * g + pair
                            act.wait_ge(st_mm[layer], 2 * ne * u + k + 1)
                            if pair == 0:
                                act.wait_ge(p_free[layer], ne * u + g + 1)
                            nc.scalar.activation(pT[0:n, g % 2, 2 * pair:2 * pair + 2, 0:w],
                                                 ps[0:n, 2 * pair:2 * pair + 2, 0:w], ACT.Exp)\
                              .then_inc(p_in[layer], 1)

                with act.Fori(0, NU - 1, 2) as u:
                    unit(u, 0)
                    unit(u + 1, 1)

            act.wait_ge(consts, NCONST)
            for c in range(NQ):
                act.wait_ge(aT_mm, c + 1)
                nc.scalar.activation(aT[:, c * QW:(c + 1) * QW], ps[0:R, 4 + c, :], ACT.Copy).then_inc(aT_sb, 1)
            for c in range(NQ):
                ln_scalar(0, c)
            act.wait_ge(xT_in, 4)
            act.sem_inc(act_left, 1)
            act.wait_ge(w_l0, 16 * 6)
            act.wait_ge(consts, NCONST + 1)
            for b in range(B):
                for c in range(2 * b, 2 * b + 2):
                    act.wait_ge(ih_mm, c + 1)
                    if c >= 2:
                        act.wait_ge(imp_mm, b)
                    nc.scalar.activation(hi[:, c % 2, :], ps[:, 2 + c % 2, :], ACT.Relu, bias=bi1_sb[:])\
                      .then_inc(hi_in, 1)
            for b in range(B):
                for i in range(4):
                    piece(6 * b + i, QW, 0.25, bq4[:, i // 2:i // 2 + 1])
                act.wait_ge(xc_mm, b + 1)
                nc.scalar.activation(xcT, ps[:, 6:8, 0:TOPK], ACT.Copy).then_inc(xc_in, 1)
                for i in range(2):
                    piece(6 * b + 4 + i, TOPK, 1.0, bk_sb[:, i:i + 1])
            act.wait_ge(pc_f, NPC0)
            act.sem_inc(act_left, 1)
            attention_act(0)
            act.wait_ge(p_in[0], 2 * len(PLANS[0][0]) * NU)
            act.sem_inc(act_left, 1)
            for c in range(NQ):
                ln_scalar(1, c)
            act.wait_ge(xT_in, 8)
            act.sem_inc(act_left, 1)
            act.wait_ge(gate_mm, 1)
            nc.scalar.activation(ge[:, :, 0:E0], ps[:, 7, 0:NT * E0].rearrange("p (t e) -> p t e", e=E0),
                                 ACT.Exp, scale=-1.0).then_inc(gate_e, 1)
            for c in range(NQ):
                def relus(e, a):
                    for m, (_, n) in enumerate(HCH):
                        act.wait_ge(up_mm, 3 * (E0 * c + e) + m + 1)
                        nc.scalar.activation(hr[0:n, m, :], ps[0:n, 2 + m, :], ACT.Relu).then_inc(up_f, 1)

                def columns(e, a):
                    act.wait_ge(xe_mm, E0 * c + e + 1)
                    nc.scalar.activation(xeT[:, a, :, :].rearrange("p k t -> p (k t)"),
                                         ps[:, 5 + a, :].bitcast(BF16), ACT.Copy).then_inc(xe_in, 1)

                for m, (_, n) in enumerate(HCH):
                    act.wait_ge(sh_mm, 3 * c + m + 1)
                    if c:
                        act.wait_ge(sh_in, 3 * c)
                    nc.scalar.activation(hsf[0:n, m, :], ps[0:n, 2 + m, :], ACT.Relu).then_inc(sh_f, 1)
                columns(0, 0)
                if c:
                    act.wait_ge(up_in, 3 * E0 * c)
                relus(0, 0)
                with act.Fori(0, E0 - 3, 2) as e:
                    for a in range(2):
                        columns(e + a + 1, 1 - a)
                        act.wait_ge(up_in, 3 * (E0 * c + e + a + 1))
                        relus(e + a + 1, 1 - a)
                columns(E0 - 1, 1)
                act.wait_ge(up_in, 3 * (E0 * c + E0 - 1))
                relus(E0 - 1, 1)
            act.wait_ge(up_f, 3 * E0 * NQ)
            act.sem_inc(act_left, 1)
            for c in range(NQ):
                ln_scalar(2, c)
            for c in range(NQ):
                a = c % 2
                for i, lat in enumerate((latqk, latv)):
                    act.wait_ge(lat_mm, 2 * c + i + 1)
                    nc.scalar.activation(lat[:, a, :], ps[:, 2 + i, :], ACT.Copy).then_inc(lat_in, 1)
                for i in range(4):
                    piece(NPC0 + 4 * c + i, QW, 0.25 if i < 2 else 1.0, 0.0)
            act.wait_ge(pc_f, NPC0 + 16)
            act.sem_inc(act_left, 1)
            attention_act(1)
            act.wait_ge(p_in[1], 2 * len(PLANS[1][0]) * NU)
            act.sem_inc(act_left, 1)
            for c in range(NQ):
                ln_scalar(3, c)
            act.wait_ge(xT_in, 16)
            act.sem_inc(act_left, 1)
            act.wait_ge(gate_mm, 2)
            nc.scalar.activation(ge[:, :, :], ps[:, 7, :].rearrange("p (t e) -> p t e", e=E1),
                                 ACT.Exp, scale=-1.0).then_inc(gate_e, 1)
            act.wait_ge(xn_in, 16)
            with act.Fori(0, E1 - 1, 2) as e:
                for a in range(2):
                    for c in range(NQ):
                        act.wait_ge(ex_mm, NQ * (e + a) + c + 1)
                        nc.scalar.activation(hx[:, a, c * QW:(c + 1) * QW], ps[:, c % 2, :], ACT.Relu)\
                          .then_inc(ex_f, 1)

        @block.tensor
        def _(pe):
            def stage(n):
                pe.wait_ge(act_left, n)
                pe.wait_ge(dve_left, n)

            def transposes(i, c):
                pe.wait_ge(xn_in, 4 * i + c + 1)
                if c >= 2:
                    pe.wait_ge(xT_in, 4 * i + c - 1)
                for t in range(TQ):
                    for k in range(KD):
                        mm = pe.transpose(ps[:, 4 + 2 * (c % 2) + k, t * P:(t + 1) * P],
                                          xn[:, c * TQ + t, k * P:(k + 1) * P], ident[:])
                mm.then_inc(tr_mm, 1)

            def attention_pe(layer):
                exps, maxes, plan = PLANS[layer]
                ne, nm = len(exps), len(maxes) + 1
                starts = [min(g for g, e in enumerate(exps) if e[0] == qh) for qh in range(2)]
                ends = [max(g for g, e in enumerate(exps) if e[0] == qh) for qh in range(2)]
                cuts = [g for g, e in enumerate(exps) if layer == 1 and e[1] * P >= e[0] * QW]
                step = CK if layer == 0 else P

                def scores(g, pair, u, a):
                    qh, c, n, first, w = exps[g]
                    k = 2 * g + pair
                    if k >= 2:
                        pe.wait_ge(p_in[layer], 2 * ne * u + k - 1)
                    for j in range(2):
                        hd = 2 * pair + j
                        mm = pe.matmul(ps[0:n, 2 * pair + j, 0:w], ks[0:QROWS + 1, a, hd, c * step:c * step + n],
                                       qs[0:QROWS + 1, a, hd, qh * QW + first:qh * QW + first + w],
                                       start=True, stop=True)
                    mm.then_inc(st_mm[layer], 1)

                def values(g, u, a):
                    qh, c, n, first, w = exps[g]
                    pe.wait_ge(p_in[layer], 2 * ne * u + 2 * g + 2)
                    if g in cuts:
                        pe.wait_ge(p_cut[layer], len(cuts) * u + cuts.index(g) + 2)
                    if g in starts:
                        pe.wait_ge(o_free[layer], 6 * u + 2)
                    for j in range(G4):
                        mm = pe.matmul(ps[32 * j:32 * j + 32, 6 + qh, first:first + w], vst[0:n, a, c, j, :],
                                       pT[0:n, g % 2, j, 0:w], start=(g in starts), stop=(g in ends),
                                       skip_group_check=True)
                    mm.then_inc(p_free[layer], 1)

                def max_scores(i, u, a):
                    qt, k0, w, hd, per = maxes[i]
                    bank = 4 + (a * nm + i) % 2
                    pe.wait_ge(mx_free[layer], nm * u + i + 1)
                    diagonal = layer == 1 and k0 + w == (qt + 1) * P
                    for j in range(per):
                        mm = pe.matmul(ps[:, bank, j * w:(j + 1) * w], qs[0:QROWS, a, hd + j, qt * P:(qt + 1) * P],
                                       ks[0:QROWS, a, hd + j, k0:k0 + w], start=(j == 0),
                                       stop=not diagonal, skip_group_check=True)
                    if diagonal:
                        for j in range(per):
                            mm = pe.matmul(ps[:, bank, (j + 1) * w - P:(j + 1) * w], identb[:], causal[:],
                                           start=False, stop=True, skip_group_check=True)
                    mm.then_inc(mx_mm[layer], 1)

                def max_row(u, a):
                    bank = 4 + (a * nm + nm - 1) % 2
                    pe.wait_ge(m_in[layer], u + 1)
                    pe.wait_ge(mx_free[layer], nm * u + nm)
                    pe.transpose(ps[0:32, bank, 0:64].bitcast(BF16), mbf[:].rearrange("p j q -> p (j q)"),
                                 identb[:]).then_inc(mx_mm[layer], 1)

                def unit(u, a, more):
                    pe.wait_ge(mrow_in[layer][a], 8 * (u - a) + 16)
                    for what, i, j in plan:
                        if what == "scores":
                            scores(i, j, u, a)
                            if more and i == 0 and j == 1:
                                pe.wait_ge(qk_in[layer][1 - a], 96 * (u + a) + 192)
                        elif what == "values":
                            values(i, u, a)
                        elif more and what == "max":
                            max_scores(i, u + 1, 1 - a)
                        elif more and what == "maxrow":
                            max_row(u + 1, 1 - a)

                pe.sem_inc(p_free[layer], 2)
                pe.wait_ge(vst_in[layer], 2 + 2)
                pe.wait_ge(qk_in[layer][0], 192)
                for i in range(len(maxes)):
                    max_scores(i, 0, 0)
                max_row(0, 0)
                with pe.Fori(0, NU - 3, 2) as u:
                    for a in range(2):
                        pe.wait_ge(vst_in[layer], u + a + 3)
                        unit(u + a, a, True)
                pe.wait_ge(vst_in[layer], NU + 2)
                unit(NU - 2, 0, True)
                unit(NU - 1, 1, False)

            def project(i):
                for c in range(NQ):
                    if c >= 2:
                        pe.wait_ge(taken, 4 * i + c - 1)
                    for t in range(TQ):
                        tt = c * TQ + t
                        for g in range(G4):
                            mm = pe.matmul(ps[:, 2 * (c % 2) + t // 2, (t % 2) * D:(t % 2 + 1) * D],
                                           oT[:, 4 * (tt // 8) + g, (tt % 8) * P:(tt % 8 + 1) * P], wpad[:, g, :],
                                           start=(g == 0), stop=(g == G4 - 1))
                    mm.then_inc(prod, 1)
                    if c:
                        transposes(i, c - 1)
                transposes(i, NQ - 1)

            def gates(w, ne):
                for t in range(NT):
                    for k in range(KD):
                        mm = pe.matmul(ps[:, 7, t * ne:(t + 1) * ne], xT[:, k, t * P:(t + 1) * P], w[:, k, :],
                                       start=(k == 0), stop=(k == KD - 1))
                mm.then_inc(gate_mm, 1)

            pe.wait_ge(consts, NCONST)
            pe.wait_ge(w_emb, 16)
            for c in range(NQ):
                pe.wait_ge(table_in[c], 16 * TQ)
                for t in range(TQ):
                    mm = pe.transpose(ps[0:R, 4 + c, t * P:(t + 1) * P], rows[:, c * TQ + t, D:D + R], ident[:])
                mm.then_inc(aT_mm, 1)
            for c in range(NQ):
                pe.wait_ge(aT_sb, NQ)
                if c >= 2:
                    pe.wait_ge(taken, c - 1)
                for t in range(TQ):
                    tt = c * TQ + t
                    mm = pe.matmul(ps[:, 2 * (c % 2) + t // 2, (t % 2) * D:(t % 2 + 1) * D],
                                   aT[:, tt * P:(tt + 1) * P], loraB_sb[:], start=True, stop=True)
                mm.then_inc(prod, 1)
                if c:
                    transposes(0, c - 1)
            transposes(0, NQ - 1)

            stage(1)
            pe.wait_ge(w_l0, 16 * 6)
            for b in range(B):
                for c in range(2 * b, 2 * b + 2):
                    pe.wait_ge(xT_in, c + 1)
                    if c >= 2:
                        pe.wait_ge(hi_in, c - 1)
                    for k in range(KD):
                        mm = pe.matmul(ps[:, 2 + c % 2, :], wi1_sb[:, k, :], xT[:, k, c * QW:(c + 1) * QW],
                                       start=(k == 0), stop=(k == KD - 1))
                    mm.then_inc(ih_mm, 1)
                pe.wait_ge(hi_in, 2 * b + 2)
                for t in range(8):
                    mm = pe.matmul(ps[:, 6 + b, t:t + 1], hi[:, t // 4, (t % 4) * P:(t % 4 + 1) * P],
                                   wi2_sb[:], start=True, stop=True)
                mm.then_inc(imp_mm, 1)
            pe.wait_ge(w_l0b, 16 * 5)
            for b in range(B):
                pe.wait_ge(imp_in, B)
                if b:
                    pe.wait_ge(sel_in, b)
                for t in range(8):
                    mm = pe.transpose(ps[:, 4 + t // 4, (t % 4) * P:(t % 4 + 1) * P],
                                      impc[:, b, t:t + 1].broadcast_to([P, P]), ident[:])
                mm.then_inc(impb_mm, 1)
                for i in range(4):
                    s = 6 * b + i
                    if s >= 2:
                        pe.wait_ge(pc_f, s - 1)
                    for k in range(KD):
                        mm = pe.matmul(ps[:, s % 2, :], wq_sb[:, k, (i // 2) * P:(i // 2 + 1) * P],
                                       xT[:, k, b * S + (i % 2) * QW:b * S + (i % 2 + 1) * QW],
                                       start=(k == 0), stop=(k == KD - 1))
                    mm.then_inc(pc_mm, 1)
                pe.wait_ge(sel_in, b + 1)
                for k in range(KD):
                    for t in range(8):
                        mm = pe.matmul(ps[:, 6 + k, 0:TOPK], xn[:, 8 * b + t, k * P:(k + 1) * P], sel[:, t, :],
                                       start=(t == 0), stop=(t == 7))
                mm.then_inc(xc_mm, 1)
                pe.wait_ge(xc_in, b + 1)
                for i in range(2):
                    s = 6 * b + 4 + i
                    pe.wait_ge(pc_f, s - 1)
                    for k in range(KD):
                        mm = pe.matmul(ps[:, s % 2, 0:TOPK], wk_sb[:, k, i * P:(i + 1) * P], xcT[:, k, :],
                                       start=(k == 0), stop=(k == KD - 1))
                    mm.then_inc(pc_mm, 1)
                for c, (c0, n) in enumerate(KCH):
                    if 3 * b + c >= 2:
                        pe.wait_ge(v_in, 3 * b + c - 1)
                    for k in range(KD):
                        mm = pe.matmul(ps[0:n, 2 + (3 * b + c) % 2, 0:D], xcT[:, k, c0:c0 + n], wv_sb[:, k, :],
                                       start=(k == 0), stop=(k == KD - 1))
                    mm.then_inc(v_mm, 1)

            stage(2)
            attention_pe(0)
            stage(3)
            pe.wait_ge(w_pad, 16 * 4)
            project(1)
            stage(4)
            pe.wait_ge(w_l1, 16 * 11)
            gates(gw_sb, E0)
            pe.wait_ge(w_moe, 16 * 4)
            pe.sem_inc(dn_mm, 1)
            for c in range(NQ):
                def turned(e, a):
                    pe.wait_ge(xs_in, E0 * c + e + 1)
                    for t in range(TQ):
                        for k in range(KD):
                            mm = pe.transpose(ps[:, 5 + a, :].bitcast(BF16)[:, k * QW + t * P:k * QW + (t + 1) * P],
                                              xs[:, t, k * P:(k + 1) * P], identb[:])
                    mm.then_inc(xe_mm, 1)

                def up(e, a):
                    pe.wait_ge(xe_in, E0 * c + e + 1)
                    for m, (c0, n) in enumerate(HCH):
                        for k in range(KD):
                            mm = pe.matmul(ps[0:n, 2 + m, :],
                                           up_sb[:, k, ds(e, 1), c0:c0 + n].rearrange("p e f -> p (e f)"),
                                           xeT[:, a, k, :], start=(k == 0), stop=(k == KD - 1))
                        mm.then_inc(up_mm, 1)

                def down(e, a, last):
                    for m, (_, n) in enumerate(HCH):
                        pe.wait_ge(up_in, 3 * (E0 * c + e) + m + 1)
                        for t in range(TQ):
                            mm = pe.matmul(ps[:, t // 2, (t % 2) * D:(t % 2 + 1) * D],
                                           hq[0:n, a, m, t * P:(t + 1) * P],
                                           dn_sb[0:n, m, ds(e, 1), :].rearrange("p e d -> p (e d)"),
                                           start=False, stop=last and m == 2, skip_group_check=True)
                    mm.then_inc(dn_mm, 1)

                if c:
                    pe.wait_ge(up_f, 3 * E0 * c)
                for m, (c0, n) in enumerate(HCH):
                    for k in range(KD):
                        mm = pe.matmul(ps[0:n, 2 + m, :], shu_sb[:, k, c0:c0 + n], xT[:, k, c * QW:(c + 1) * QW],
                                       start=(k == 0), stop=(k == KD - 1))
                    mm.then_inc(sh_mm, 1)
                if c == 0:
                    pe.wait_ge(gate_e, 1)
                turned(0, 0)
                if c:
                    pe.wait_ge(taken, 8 + c)
                for m, (_, n) in enumerate(HCH):
                    pe.wait_ge(sh_in, 3 * c + m + 1)
                    for t in range(TQ):
                        mm = pe.matmul(ps[:, t // 2, (t % 2) * D:(t % 2 + 1) * D], hs[0:n, m, t * P:(t + 1) * P],
                                       shd_sb[0:n, m, :], start=(m == 0 and t % 2 == 0), stop=False,
                                       skip_group_check=True)
                mm.then_inc(sh_dn, 1)
                if c == 0:
                    pe.wait_ge(w_moeb, 16 * 5)
                up(0, 0)
                with pe.Fori(0, E0 - 3, 2) as e:
                    for a in range(2):
                        turned(e + a + 1, 1 - a)
                        pe.wait_ge(up_f, 3 * (E0 * c + e + a + 1))
                        up(e + a + 1, 1 - a)
                        down(e + a, a, False)
                turned(E0 - 1, 1)
                pe.wait_ge(up_f, 3 * (E0 * c + E0 - 1))
                up(E0 - 1, 1)
                down(E0 - 2, 0, False)
                down(E0 - 1, 1, True)

            stage(5)
            for c in range(NQ):
                transposes(2, c)
            for c in range(NQ):
                pe.wait_ge(xT_in, 12)
                if c:
                    pe.wait_ge(lat_in, 2 * c)
                for i in range(2):
                    for k in range(KD):
                        mm = pe.matmul(ps[:, 2 + i, :],
                                       wl_sb[:, k, 2 * i:2 * i + 2, :].rearrange("p a l -> p (a l)"),
                                       xT[:, k, c * QW:(c + 1) * QW], start=(k == 0), stop=(k == KD - 1))
                    mm.then_inc(lat_mm, 1)
                pe.wait_ge(lat_in, 2 * c + 1)
                for i in range(4):
                    s = NPC0 + 4 * c + i
                    pe.wait_ge(pc_f, s - 1)
                    pe.matmul(ps[:, s % 2, :], wh_sb[:, i // 2, (i % 2) * P:(i % 2 + 1) * P], latqk[:, c % 2, :],
                              start=True, stop=True).then_inc(pc_mm, 1)
                pe.wait_ge(lat_in, 2 * c + 2)
                for t in range(TQ):
                    n = c * TQ + t
                    if n >= 2:
                        pe.wait_ge(v_in, 6 + n - 1)
                    pe.matmul(ps[:, 6 + n % 2, 0:D], latv[:, c % 2, t * P:(t + 1) * P], wh_sb[:, 2, :],
                              start=True, stop=True).then_inc(v_mm, 1)
            stage(6)
            attention_pe(1)
            stage(7)
            pe.wait_ge(w_pad, 16 * 8)
            project(3)
            stage(8)
            gates(es_sb, E1)
            pe.wait_ge(gate_e, 2)
            with pe.Fori(0, E1 - 1, 2) as e:
                for a in range(2):
                    pe.wait_ge(ew_in[a], 16 * (e + 2))
                    for c in range(NQ):
                        if c >= 2:
                            pe.wait_ge(ex_f, NQ * (e + a) + c - 1)
                        for k in range(KD):
                            mm = pe.matmul(ps[:, c % 2, :], ek[:, a, k, :], xT[:, k, c * QW:(c + 1) * QW],
                                           start=(k == 0), stop=(k == KD - 1))
                        mm.then_inc(ex_mm, 1)
                    for t in range(NT):
                        if t % TQ == 0:
                            pe.wait_ge(ex_f, NQ * (e + a) + t // TQ + 1)
                        if t % 2 == 0:
                            pe.wait_ge(ey_add, NT * (e + a) + t + 2)
                        mm = pe.matmul(ps[:, 4 + (t // 2) % 4, (t % 2) * D:(t % 2 + 1) * D],
                                       hx[:, a, t * P:(t + 1) * P], ev[:, a, :], start=True, stop=True)
                        if t % 2:
                            mm.then_inc(ey_mm, 1)


def kernel(x, L0_tok_emb_weight, L0_tok_lora_A, L0_tok_lora_B, L0_attn_wq, L0_attn_bq, L0_attn_wk, L0_attn_bk,
           L0_attn_wv, L0_attn_bv, L0_attn_wo, L0_attn_bo, L0_attn_wi1, L0_attn_bi1, L0_attn_wi2, L0_attn_bi2,
           L0_ffn_gate_w, L0_ffn_expert_bias, L0_ffn_w_up, L0_ffn_w_down, L0_ffn_shared_w_up, L0_ffn_shared_w_down,
           L1_attn_wq_lat, L1_attn_wk_lat, L1_attn_wv_lat, L1_attn_wq_heads, L1_attn_wk_heads, L1_attn_wv_heads,
           L1_attn_w_proj, L1_attn_b_proj, L1_ffn_expert_sel, L1_ffn_keys, L1_ffn_values):
    import numpy as np
    import concourse.bacc as bacc
    from concourse.bass_utils import run_bass_kernel_spmd

    nc = bacc.Bacc("TRN2", target_bir_lowering=False, num_devices=1)
    A = np.asarray
    arrays = {
        "ids": A(x).reshape(NT, P).T,
        "table": np.concatenate([A(L0_tok_emb_weight), A(L0_tok_lora_A).T], axis=1),
        "loraB": A(L0_tok_lora_B).T,
        "wq": A(L0_attn_wq).T, "wk": A(L0_attn_wk).T, "wv": A(L0_attn_wv).T, "wo": A(L0_attn_wo).T,
        "wi1": A(L0_attn_wi1).T, "wi2": A(L0_attn_wi2).T,
        "bq": A(L0_attn_bq).reshape(KD, P).T, "bk": A(L0_attn_bk).reshape(KD, P).T,
        "bv": A(L0_attn_bv), "bo": A(L0_attn_bo),
        "bi1": A(L0_attn_bi1).reshape(P, 1), "bi2": A(L0_attn_bi2),
        "gate_w": A(L0_ffn_gate_w).T, "e_bias": A(L0_ffn_expert_bias),
        "w_up": A(L0_ffn_w_up).transpose(2, 0, 1).reshape(D, E0 * HID),
        "w_down": A(L0_ffn_w_down).transpose(2, 0, 1).reshape(HID, E0 * D),
        "sh_up": A(L0_ffn_shared_w_up).T, "sh_down": A(L0_ffn_shared_w_down).T,
        "wq_lat": A(L1_attn_wq_lat), "wk_lat": A(L1_attn_wk_lat), "wv_lat": A(L1_attn_wv_lat),
        "wq_heads": A(L1_attn_wq_heads), "wk_heads": A(L1_attn_wk_heads), "wv_heads": A(L1_attn_wv_heads),
        "w_proj": A(L1_attn_w_proj), "b_proj": A(L1_attn_b_proj),
        "e_sel": A(L1_ffn_expert_sel).T, "e_keys": A(L1_ffn_keys), "e_values": A(L1_ffn_values),
    }
    arrays = {f"in_{k}": np.ascontiguousarray(v) for k, v in arrays.items()}
    args = [nc.dram_tensor(k, v.shape, mybir.dt.from_np(v.dtype), kind="ExternalInput").ap() for k, v in arrays.items()]
    out = nc.dram_tensor("out", (N, D), F32, kind="ExternalOutput").ap()
    order = ["ids", "table", "loraB", "wq", "wk", "wv", "wo", "wi1", "wi2", "bq", "bk", "bv", "bo", "bi1", "bi2",
             "gate_w", "e_bias", "w_up", "w_down", "sh_up", "sh_down", "wq_lat", "wk_lat", "wv_lat",
             "wq_heads", "wk_heads", "wv_heads", "w_proj", "b_proj", "e_sel", "e_keys", "e_values"]
    by_name = dict(zip([k[3:] for k in arrays], args))
    lm_tower(nc, *[by_name[k] for k in order], out)
    r = run_bass_kernel_spmd(nc, [arrays], core_ids=[0])
    return r.results[0]["out"].reshape(B, S, D)
```

```python
from contextlib import ExitStack

import concourse.bass as bass
from concourse import mybir
from concourse.bass import ds

F32 = mybir.dt.float32
F32R = mybir.dt.float32r
BF16 = mybir.dt.bfloat16
I32 = mybir.dt.int32
U32 = mybir.dt.uint32
ALU = mybir.AluOpType
ACT = mybir.ActivationFunctionType
AX = mybir.AxisListType

P = 128
B, S, D = 2, 1024, 256
N = B * S
NT = N // P
KD = D // P
QW = 512
NQ = N // QW
TQ = QW // P
R = 16
H, HD = 16, 16
G4 = 4
NU = B * H // G4
TOPK = int(S * 0.3)
CK = 103
KCH = [(c, min(CK, TOPK - c)) for c in range(0, TOPK, CK)]
QROWS = 96
E0, HID = 8, 352
HCH = [(c, min(P, HID - c)) for c in range(0, HID, P)]
LAT = 64
E1, F1, TOP1 = 32, 128, 4
NPS = 4
EPS = 1e-5
MASKED = -1.0e30
QPART = [0, 0, 1, 1, 0, 2]
KPART = [0, 1, 0, 1, 2, 0]


class Plan:

    def __init__(self, layer):
        self.layer = layer
        self.chunk = CK if layer == 0 else P
        self.nch = len(KCH) if layer == 0 else S // P
        if layer == 0:
            self.exps = [(qh, c, n, 0, QW) for qh in range(2) for c, (_, n) in enumerate(KCH)]
            self.maxes = [(qt, 0, TOPK, h, 1) for qt in range(S // P) for h in range(G4)]
            full = 4
        else:
            self.exps = []
            for qh, order in enumerate(((0, 3, 2, 1), (0, 7, 6, 5, 4, 3, 2, 1))):
                for c in order:
                    first = max(0, c * P - qh * QW)
                    self.exps.append((qh, c, P, first, QW - first))
            self.maxes = []
            for qt in range(S // P):
                for k0 in range(0, (qt + 1) * P, QW):
                    w = min(QW, (qt + 1) * P - k0)
                    per = min(G4, QW // w)
                    self.maxes += [(qt, k0, w, h, per) for h in range(0, G4, per)]
            full = 10
        self.ne, self.nm = len(self.exps), len(self.maxes)
        self.first = [min(g for g, e in enumerate(self.exps) if e[0] == qh) for qh in range(2)]
        self.last = [max(g for g, e in enumerate(self.exps) if e[0] == qh) for qh in range(2)]
        self.cuts = [g for g, e in enumerate(self.exps) if layer == 1 and e[1] * P >= e[0] * QW]
        self.steps, slots, done = [], 3 * full, 0
        for g in range(self.ne):
            rest = [("values", g - 1)] if g else [("lastvalues", self.ne - 1)]
            if g == 1:
                rest.append(("lastturn", 1))
            if g == self.last[0] + 2:
                rest.append(("turn", 0))
            for k, part in enumerate(([("scores", g, 0)], [("scores", g, 1)], rest)):
                self.steps += part
                upto = min(self.nm, (3 * g + k + 1) * self.nm // slots)
                self.steps += [("max", i) for i in range(done, upto)]
                if upto == self.nm and done < self.nm:
                    self.due = len(self.steps) + 1
                done = upto
        self.steps.insert(self.due, ("maxrow",))

    def of(self, first, last):
        return [s for s in self.steps if not (first and s[0].startswith("last"))
                and not (last and s[0].startswith("max"))] + \
            ([("values", self.ne - 1), ("turn", 1)] if last else [])

    def units(self):
        ring1 = 2 * (self.nm + 1) + 1
        per = self.nm + 3
        return ((0, 0, 0, self.nm + 1),
                lambda i, d: (3 * i + 1 + d, (1 + d) % 3, i + (1 + d) // 3, 3 * per * i + ring1 + per * d),
                (NU - 1, (NU - 1) % 3, (NU - 1) // 3, ring1 + per * (NU - 2)))


def after(unit):
    u, a, n, _ = unit
    return u + 1, (a + 1) % 3, n + (a + 1) // 3


def lm_tower(nc, ids, table, loraB, wq, wk, wv, wo, wi1, wi2, bq, bk, bv, bo, bi1, bi2,
             gate_w, e_bias, w_up, w_down, sh_up, sh_down,
             wq_lat, wk_lat, wv_lat, wq_heads, wk_heads, wv_heads, w_proj, b_proj,
             e_sel, e_keys, e_values, out):
    with ExitStack() as ctx:
        def sb(name, shape, dt=F32):
            return ctx.enter_context(nc.sbuf_tensor(name, shape, dt))

        def sem(name):
            return ctx.enter_context(nc.semaphore(name))

        ps = ctx.enter_context(nc.psum_tensor("ps", [P, 8, 512], F32))

        h = sb("h", [P, NT, D])
        xn = sb("xn", [P, NT, D])
        xT = sb("xT", [P, KD, N])
        oN = sb("oN", [P, 8, NU, G4, HD])
        with ExitStack() as early:
            vaug = early.enter_context(nc.sbuf_tensor("vaug", [P, NU, 8, G4, 32], F32))
            arena = early.enter_context(nc.sbuf_tensor("arena", [P, 16384], F32))
        xp = sb("xp", [P, 2, KD, N], F32R)
        hp = sb("hp", [P, 2, 2, N], F32R)
        ewp = sb("ewp", [P, 2, 2, 2 * D], F32R)
        spare = sb("spare", [P, 16384 - 10240])
        ks = sb("ks", [P, 3, G4, S], BF16)

        qs = arena[:, 0:6144].bitcast(BF16).rearrange("p (a h t) -> p a h t", a=3, h=G4)
        pT = arena[:, 6144:10240].rearrange("p (a h t) -> p a h t", a=2, h=G4)
        oc = arena[:, 10240:11264].rearrange("p (a t) -> p a t", a=2)
        vst = arena[:, 11264:14336].rearrange("p (a c j r) -> p a c j r", a=3, c=8, j=G4)
        rows = arena[:, 0:NT * (D + R)].rearrange("p (t d) -> p t d", t=NT)
        aT = arena[0:R, 8192:8192 + N]
        oN_flat = oN[:].rearrange("p t u j r -> p (t u j r)")
        hi = oN_flat[:, 0:1024].rearrange("p (a t) -> p a t", a=2)
        sel = oN_flat[:, 1024:1024 + 8 * TOPK].rearrange("p (t k) -> p t k", t=8)
        xcT = oN_flat[:, 3480:3480 + KD * TOPK].rearrange("p (k n) -> p k n", k=KD)
        junk = ks[:, 0, :, :]
        junk_eq = ks[:, 1, :, :].rearrange("p a (b n) -> p (a b) n", n=P)
        qf = arena[:, 6144:8192].rearrange("p (a t) -> p a t", a=NPS)
        rem = arena[:, 8192:10240].rearrange("p (a t) -> p a t", a=NPS)
        parts = arena[:, 10240:13312].bitcast(BF16).rearrange("p (a s t) -> p a s t", a=NPS, s=3)
        latqk = arena[:, 13312:14336].rearrange("p (a t) -> p a t", a=2)
        latv = arena[:, 14336:15360].rearrange("p (a t) -> p a t", a=2)
        oT = arena[:, 12288:14336].rearrange("p (a k t) -> p a k t", a=2, k=KD)
        up_sb = arena[:, 0:2816].bitcast(BF16).rearrange("p (k e f) -> p k e f", k=KD, e=E0)
        dn_sb = arena[:, 2816:5888].bitcast(BF16).rearrange("p (m e d) -> p m e d", m=3, e=E0)
        shu_sb = arena[:, 5888:6592].rearrange("p (k f) -> p k f", k=KD)
        shd_sb = arena[:, 6592:7360].rearrange("p (m d) -> p m d", m=3)
        hsf = arena[:, 7360:8896].rearrange("p (m t) -> p m t", m=3)
        hs = arena[:, 8896:10432].rearrange("p (m t) -> p m t", m=3)
        xs = arena[:, 10432:10944].bitcast(BF16).rearrange("p (t d) -> p t d", t=TQ)
        xeT = arena[:, 10944:11968].bitcast(BF16).rearrange("p (a k t) -> p a k t", a=2, k=KD)
        hr = arena[:, 11968:12736].bitcast(BF16).rearrange("p (m t) -> p m t", m=3)
        hq = arena[:, 12736:14272].bitcast(BF16).rearrange("p (a m t) -> p a m t", a=2, m=3)
        ge, sc, eq, hit = (arena[:, 14336 + 512 * i:14848 + 512 * i].rearrange("p (t e) -> p t e", t=NT)
                           for i in range(4))
        bi, mx8, ixf = (arena[:, 13312 + 128 * i:13440 + 128 * i].rearrange("p (t e) -> p t e", t=NT)
                        for i in range(3))
        ix8 = arena[:, 13696:13824].bitcast(U32).rearrange("p (t e) -> p t e", t=NT)
        ew = arena[:, 10240:11264].rearrange("p (a n) -> p a n", a=2)
        hf = arena[:, 11264:12288].rearrange("p (a t) -> p a t", a=2)
        g1 = arena[:, 12288:12800].rearrange("p (t e) -> p t e", t=NT)

        ids_sb = sb("ids_sb", [P, NT], I32)
        loraB_sb = sb("loraB_sb", [R, D])
        wq_sb = sb("wq_sb", [P, KD, D])
        wk_sb = sb("wk_sb", [P, KD, D])
        wv_sb = sb("wv_sb", [P, KD, D])
        wi1_sb = sb("wi1_sb", [P, KD, P])
        wi2_sb = sb("wi2_sb", [P, 1])
        wo_sb = sb("wo_sb", [P, KD, D])
        gw_sb = sb("gw_sb", [P, KD, E0])
        es_sb = sb("es_sb", [P, KD, E1])
        wl_sb = sb("wl_sb", [P, KD, 4, LAT])
        wh_sb = sb("wh_sb", [P, 3, D])
        bq_sb = sb("bq_sb", [P, KD])
        bq4 = sb("bq4", [P, KD])
        bk_sb = sb("bk_sb", [P, KD])
        bi1_sb = sb("bi1_sb", [P, 1])
        bi2_sb = sb("bi2_sb", [P, 1])
        bv_sb = sb("bv_sb", [P, D])
        bo_sb = sb("bo_sb", [P, D])
        bp_sb = sb("bp_sb", [P, D])
        eb_sb = sb("eb_sb", [P, E0])
        ident = sb("ident", [P, P])
        identb = sb("identb", [P, P], BF16)
        causal = sb("causal", [P, P], BF16)
        before = sb("before", [P, P])
        iota = sb("iota", [P, TOPK])
        eps = sb("eps", [P, 1])
        post = sb("post", [P, 2])
        st = sb("st", [P, TQ, 6])
        mv = sb("mv", [P, TQ, 2])
        sd = sb("sd", [P, TQ])
        rstd = sb("rstd", [P, TQ])
        impc = sb("impc", [P, B, 8])
        rkp = sb("rkp", [P, 8, 4])
        rank = sb("rank", [P, 8])
        mA = sb("mA", [P, G4, 8])
        mB = sb("mB", [P, G4, 4])
        mbf = sb("mbf", [P, G4, 8], BF16)
        mT = sb("mT", [32, 3, P], BF16)
        rden = sb("rden", [P, 2, TQ, G4])
        g0 = sb("g0", [P, NT, E0])

        qd = nc.dram_tensor("q_parts", [3, B, D, S], BF16, kind="Internal").ap()
        kd = nc.dram_tensor("k_parts", [3, B, D, S], BF16, kind="Internal").ap()

        ids_in, table_in = sem("ids_in"), [sem(f"rows_in{c}") for c in range(NQ)]
        w_emb, w_l0, w_l0b, w_proj_in, w_l1 = sem("w_emb"), sem("w_l0"), sem("w_l0b"), sem("w_proj_in"), sem("w_l1")
        w_moe, w_moeb = sem("w_moe"), sem("w_moeb")
        consts = sem("consts")
        vlink = sem("vlink")
        plink = sem("plink")
        act_left, dve_left = sem("act_left_psum"), sem("dve_left_psum")
        aT_mm, aT_sb = sem("aT_mm"), sem("aT_sb")
        prod, taken = sem("quad_product"), sem("quad_taken")
        var_in, sd_in, xn_in = sem("var_ready"), sem("sd_ready"), sem("xn_ready")
        tr_mm, xT_in = sem("xn_transposed"), sem("xT_ready")
        biased = sem("bias_in_residual")
        ih_mm, hi_in, imp_mm, imp_in = sem("ih_mm"), sem("hi_ready"), sem("imp_mm"), sem("imp_ready")
        impb_mm, sel_in, xc_mm, xc_in = sem("impb_mm"), sem("sel_ready"), sem("xc_mm"), sem("xc_ready")
        pc_mm, pc_f, pc_12, pc_3 = sem("piece_mm"), sem("piece_f"), sem("piece_12"), sem("piece_3")
        pc_out = [sem(f"piece_out{a}") for a in range(NPS)]
        v_mm, v_in = sem("v_mm"), sem("v_ready")
        lat_mm, lat_in = sem("lat_mm"), sem("lat_ready")
        gate_mm, gate_e, gate_in = sem("gate_mm"), sem("gate_e"), sem("gate_ready")
        qk_in = [[sem(f"qk_in{l}{a}") for a in range(3)] for l in range(2)]
        mrow_in = [[sem(f"mrow_in{l}{a}") for a in range(3)] for l in range(2)]
        o_mm, oT_in = sem("out_turned"), sem("out_columns")
        rden_in = [sem(f"denominators{l}") for l in range(2)]
        st_mm = [sem(f"scores_ready{l}") for l in range(2)]
        p_in = [sem(f"probs_ready{l}") for l in range(2)]
        p_cut = [sem(f"probs_masked{l}") for l in range(2)]
        p_free = [sem(f"probs_free{l}") for l in range(2)]
        o_free = [sem(f"out_bank_free{l}") for l in range(2)]
        mx_mm = [sem(f"ring_step{l}") for l in range(2)]
        mx_free = [sem(f"ring_bank_free{l}") for l in range(2)]
        m_in = [sem(f"max_ready{l}") for l in range(2)]
        mT_in = [sem(f"max_row_ready{l}") for l in range(2)]
        vst_in = [sem(f"unit_values{l}") for l in range(2)]
        sh_mm, sh_f, sh_in, sh_dn = sem("sh_mm"), sem("sh_relu"), sem("sh_square"), sem("sh_down")
        xs_in, xe_mm, xe_in = sem("xs_ready"), sem("xe_mm"), sem("xe_ready")
        up_mm, up_f, up_in, dn_mm = sem("up_mm"), sem("up_relu"), sem("up_square"), sem("down_done")
        ew_in = [sem("expert_weights0"), sem("expert_weights1")]
        xp_in, ewp_hi, ewp_in = sem("x_low"), sem("expert_weight_high"), sem("expert_weight_low")
        ex_mm, ex_f, ex_lo = sem("ex_up"), sem("ex_relu"), sem("ex_low_part")
        ey_mm, ey_add = sem("ex_down"), sem("ex_added")
        stored = sem("stored")

        NFIRST, NCONST = 2, 8
        RING = (4, 5, 7)
        PLANS = [Plan(0), Plan(1)]
        NPC0 = 12

        def kparts(w, k=KD):
            return w.rearrange("(k p) n -> p k n", k=k)

        def arena_free(eng, layer):
            eng.wait_ge(v_mm, 6 if layer == 0 else 6 + NT)
            eng.wait_ge(act_left, 2 if layer == 0 else 6)
            eng.wait_ge(dve_left, 2 if layer == 0 else 6)

        block = ctx.enter_context(nc.Block())

        @block.sync
        def _(sp):
            sp.dma_start(ids_sb[:], ids).then_inc(ids_in, 16)
            sp.dma_start(loraB_sb[:], loraB).then_inc(w_emb, 16)
            for dst, src in ((wi1_sb[:], kparts(wi1)), (wi2_sb[:], wi2), (bi1_sb[:], bi1),
                             (bi2_sb[:], bi2.partition_broadcast(P)),
                             (wq_sb[:], kparts(wq)), (bq_sb[:], bq)):
                sp.dma_start(dst, src).then_inc(w_l0, 16)
            for dst, src in ((wk_sb[:], kparts(wk)), (wv_sb[:], kparts(wv)), (bk_sb[:], bk),
                             (bv_sb[:], bv.partition_broadcast(P)),
                             (bo_sb[:], bo.partition_broadcast(P))):
                sp.dma_start(dst, src).then_inc(w_l0b, 16)
            sp.dma_start(wo_sb[:], kparts(wo)).then_inc(w_proj_in, 16)
            sp.wait_ge(consts, NCONST)
            for i, w in enumerate((wq_lat, wk_lat, wv_lat, wv_lat)):
                sp.dma_start(wl_sb[:, :, i, :], kparts(w)).then_inc(w_l1, 16)
            for i, (w, r) in enumerate(((wq_heads, 0), (wk_heads, LAT), (wv_heads, 0))):
                sp.dma_start(wh_sb[r:r + LAT, i, :], w).then_inc(w_l1, 16)
            for dst, src in ((bp_sb[:], b_proj.partition_broadcast(P)), (gw_sb[:], kparts(gate_w)),
                             (eb_sb[:], e_bias.partition_broadcast(P)), (es_sb[:], kparts(e_sel))):
                sp.dma_start(dst, src).then_inc(w_l1, 16)

            def store_pieces(first, n, where):
                for s in range(first, first + n):
                    sp.wait_ge(pc_3, s + 1)
                    sp.wait_ge(pc_12, s + 1)
                    dst, b, cg, c0, w = where(s - first)
                    sp.dma_start(dst[:, b, cg * P:(cg + 1) * P, c0:c0 + w].rearrange("s p t -> p s t"),
                                 parts[:, s % NPS, :, 0:w]).then_inc(pc_out[s % NPS], 16)

            def attention_dma(layer):
                nk = TOPK if layer == 0 else S

                def load(u, a):
                    for src, dst, sel_, w in ((qd, qs, QPART, S), (kd, ks, KPART, nk)):
                        for r, part in enumerate(sel_):
                            rows_ = src[part].rearrange("b (g j r) t -> (b g) r j t", g=G4, j=G4)
                            sp.dma_start(dst[16 * r:16 * r + 16, a, :, 0:w],
                                         rows_[ds(u, 1), :, :, 0:w].rearrange("o r j t -> (o r) j t"))\
                              .then_inc(qk_in[layer][a], 16)

                def mrow(u, a):
                    sp.wait_ge(mT_in[layer], u + 1)
                    sp.dma_start(qs[QROWS:QROWS + 1, a, :, :].rearrange("o h (q j) -> o (h q) j", j=P),
                                 mT[:, a, :]).then_inc(mrow_in[layer][a], 16)

                plan = PLANS[layer]
                arena_free(sp, layer)
                load(0, 0)
                load(1, 1)
                mrow(0, 0)
                with sp.Fori(0, (NU - 2) // 3) as i:
                    for d in range(3):
                        v = 3 * i + 2 + d
                        sp.wait_ge(p_free[layer], plan.ne * (3 * i + d) + 2)
                        load(v, (2 + d) % 3)
                        mrow(v - 1, (1 + d) % 3)
                mrow(NU - 1, (NU - 1) % 3)

            def q0(i):
                b, i = divmod(i, 6)
                return (qd, b, i // 2, (i % 2) * QW, QW) if i < 4 else (kd, b, i - 4, 0, TOPK)

            store_pieces(0, NPC0, q0)
            for a in range(NPS):
                sp.wait_ge(pc_out[a], 16 * NPC0 // NPS)
            attention_dma(0)

            sp.dma_start(wq_sb[:], kparts(w_proj)).then_inc(w_proj_in, 16)

            sp.wait_ge(dve_left, 3)
            sp.wait_ge(act_left, 3)
            sp.dma_start(shu_sb[:, :, :], kparts(sh_up)).then_inc(w_moe, 16)
            for m, (c, n) in enumerate(HCH):
                sp.dma_start(shd_sb[0:n, m, :], sh_down[c:c + n, :]).then_inc(w_moe, 16)
            def q1(i):
                c, i = divmod(i, 4)
                return (qd if i < 2 else kd, c // 2, i % 2, (c % 2) * QW, QW)

            store_pieces(NPC0, 16, q1)
            for a in range(NPS):
                sp.wait_ge(pc_out[a], 16 * (NPC0 + 16) // NPS)
            attention_dma(1)

            def expert(e, a):
                sp.dma_start(ew[:, a, 0:D].rearrange("p (k f) -> p k f", k=KD),
                             e_keys.rearrange("e (k p) f -> e p k f", k=KD)[ds(e, 1), :, :, :]
                             .rearrange("o p k f -> (o p) k f")).then_inc(ew_in[a], 16)
                sp.dma_start(ew[:, a, D:2 * D], e_values[ds(e, 1), :, :].rearrange("o p n -> (o p) n"))\
                  .then_inc(ew_in[a], 16)

            sp.wait_ge(dve_left, 7)
            sp.wait_ge(act_left, 7)
            expert(0, 0)
            expert(1, 1)
            with sp.Fori(0, E1 - 3, 2) as e:
                for a in range(2):
                    sp.wait_ge(ewp_in, e + a + 1)
                    expert(e + a + 2, a)
            for c in range(NQ):
                sp.wait_ge(ey_add, 8 + NT * (E1 - 1) + (c + 1) * TQ)
                sp.dma_start(out[c * QW:(c + 1) * QW, :].rearrange("(t p) d -> p t d", p=P),
                             h[:, c * TQ:(c + 1) * TQ, :]).then_inc(stored, 16)
            sp.wait_ge(stored, 16 * NQ)

        @block.gpsimd
        def _(pool):
            own = [0]

            def link(ins):
                own[0] += 1
                ins.then_inc(plink, 1)
                pool.wait_ge(plink, own[0])

            def constant(ins):
                ins.then_inc(consts, 1)

            link(nc.gpsimd.memset(ident[:], 0.0))
            constant(nc.gpsimd.affine_select(out=ident[:], in_=ident[:], compare_op=ALU.not_equal, fill=1.0, base=0,
                                             pattern=[[-1, P]], channel_multiplier=1))
            constant(nc.gpsimd.memset(eps[:], EPS))
            pool.wait_ge(ids_in, 16)
            for t in range(NT):
                nc.gpsimd.indirect_dma_start(
                    rows[:, t, :], None, table,
                    bass.IndirectOffsetOnAxis(ids_sb[:, t:t + 1].bitcast(U32), 0)).then_inc(table_in[t // TQ], 16)
            link(nc.gpsimd.memset(before[:], 1.0))
            constant(nc.gpsimd.affine_select(out=before[:], in_=before[:], compare_op=ALU.is_gt, fill=0.0, base=0,
                                             pattern=[[-1, P]], channel_multiplier=1))
            constant(nc.gpsimd.iota(iota[:], pattern=[[1, TOPK]], base=0, channel_multiplier=0,
                                    allow_small_or_imprecise_dtypes=True))
            constant(nc.gpsimd.tensor_copy(identb[:], ident[:]))
            link(nc.gpsimd.memset(causal[:], 0.0))
            constant(nc.gpsimd.affine_select(out=causal[:], in_=causal[:], compare_op=ALU.is_ge, fill=MASKED, base=0,
                                             pattern=[[-1, P]], channel_multiplier=1))
            constant(nc.gpsimd.memset(wh_sb[:], 0.0))
            constant(nc.gpsimd.memset(vaug[:], 1.0))

            def add_bias(first, bias):
                for c in range(NQ):
                    pool.wait_ge(xn_in, first + c + 1)
                    hc = h[:, c * TQ:(c + 1) * TQ, :]
                    nc.gpsimd.tensor_tensor(hc, hc, bias[:].unsqueeze(1).broadcast_to([P, TQ, D]), ALU.add)\
                      .then_inc(biased, 1)

            def third_parts(first, n, width):
                for s in range(first, first + n):
                    w = width(s - first)
                    pool.wait_ge(pc_12, s + 1)
                    a = s % NPS
                    if s >= NPS:
                        pool.wait_ge(pc_out[a], 16 * (s // NPS))
                    nc.gpsimd.tensor_tensor(parts[:, a, 2, 0:w], rem[:, a, 0:w], parts[:, a, 1, 0:w],
                                            ALU.subtract).then_inc(pc_3, 1)

            def attention_pool(layer):
                plan = PLANS[layer]
                ne, nch, keys, cuts = plan.ne, plan.nch, plan.chunk, plan.cuts

                def stage_values(u, a):
                    nc.gpsimd.tensor_copy(vst[0:keys, a, 0:nch, :, :].rearrange("p c j r -> p (c j r)"),
                                          vaug[0:keys, ds(u, 1), 0:nch, :, :].rearrange("p u c j r -> p (u c j r)"))\
                      .then_inc(vst_in[layer], 1)

                def cut_probs(i, u):
                    g = cuts[i]
                    pool.wait_ge(p_in[layer], 2 * ne * u + 2 * g + 2)
                    pool.wait_ge(p_cut[layer], len(cuts) * u + i + 1)
                    nc.gpsimd.tensor_tensor(post[:, 0:1], eps[:], eps[:], ALU.add)
                    d = pT[:, g % 2, :, 0:P]
                    nc.gpsimd.affine_select(out=d, in_=d, compare_op=ALU.is_ge, fill=0.0, base=0,
                                            pattern=[[0, G4], [1, P]], channel_multiplier=-1)\
                      .then_inc(p_cut[layer], 1)

                def unit(this, first=False, last=False):
                    u, _, _, _ = this
                    if cuts:
                        cut_probs(0, u)
                    if not last:
                        v, a, _ = after(this)
                        if not first:
                            pool.wait_ge(p_free[layer], ne * (u - 1) + 2)
                        stage_values(v, a)
                    for i in range(1, len(cuts)):
                        cut_probs(i, u)

                arena_free(pool, layer)
                for a in range(3):
                    nc.gpsimd.memset(ks[QROWS:QROWS + 1, a, :, :], -1.0).then_inc(vst_in[layer], 1)
                pool.sem_inc(p_cut[layer], 1)
                pool.wait_ge(vst_in[layer], 3)
                pool.wait_ge(v_in, 6 if layer == 0 else 6 + NT)
                stage_values(0, 0)
                first, middle, last = plan.units()
                unit(first, first=True)
                with pool.Fori(0, (NU - 2) // 3) as i:
                    for d in range(3):
                        unit(middle(i, d))
                unit(last, last=True)

            pool.wait_ge(w_l0b, 16 * 5)
            add_bias(0, bo_sb)
            third_parts(0, NPC0, lambda i: QW if i % 6 < 4 else TOPK)
            for a in range(NPS):
                pool.wait_ge(pc_out[a], 16 * NPC0 // NPS)
            attention_pool(0)
            pool.wait_ge(dve_left, 3)
            pool.wait_ge(act_left, 3)
            for k in range(KD):
                nc.gpsimd.dma_start(up_sb[:, k, :, :], w_up[k * P:(k + 1) * P, :].rearrange("p (e f) -> p e f", e=E0))\
                  .then_inc(w_moeb, 16)
            for m, (c, n) in enumerate(HCH):
                nc.gpsimd.dma_start(dn_sb[0:n, m, :, :], w_down[c:c + n, :].rearrange("p (e d) -> p e d", e=E0))\
                  .then_inc(w_moeb, 16)
            pool.wait_ge(w_l1, 16 * 11)
            add_bias(8, bp_sb)
            third_parts(NPC0, 16, lambda i: QW)
            for a in range(NPS):
                pool.wait_ge(pc_out[a], 16 * (NPC0 + 16) // NPS)
            attention_pool(1)

            for c in range(NQ):
                t = slice(c * QW, (c + 1) * QW)
                pool.wait_ge(xT_in, 12 + c + 1)
                nc.gpsimd.tensor_tensor(xp[:, 1, :, t], xT[:, :, t], xp[:, 0, :, t].bitcast(F32), ALU.subtract)\
                  .then_inc(xp_in, 1)

            def split_weights(e, a):
                pool.wait_ge(ewp_hi, e + 1)
                nc.gpsimd.tensor_tensor(ewp[:, a, 1, :], ew[:, a, :], ewp[:, a, 0, :].bitcast(F32), ALU.subtract)\
                  .then_inc(ewp_in, 1)

            def low_parts(e, a):
                for c in range(NQ):
                    t = slice(c * QW, (c + 1) * QW)
                    pool.wait_ge(ex_f, NQ * e + c + 1 + NQ)
                    nc.gpsimd.tensor_tensor(hp[:, a, 1, t], hf[:, c % 2, :], hp[:, a, 0, t].bitcast(F32),
                                            ALU.subtract).then_inc(ex_lo, 1)

            pool.sem_inc(ex_lo, 2)
            split_weights(0, 0)
            with pool.Fori(0, E1 - 3, 2) as e:
                for a in range(2):
                    low_parts(e + a, a)
                    split_weights(e + a + 1, 1 - a)
            low_parts(E1 - 2, 0)
            split_weights(E1 - 1, 1)
            low_parts(E1 - 1, 1)

        @block.vector
        def _(dve):
            own = [0]

            def link(ins):
                own[0] += 1
                ins.then_inc(vlink, 1)
                dve.wait_ge(vlink, own[0])

            def layernorm(i, c):
                for t in range(TQ):
                    ins = nc.vector.bn_stats(st[:, t, :], h[:, c * TQ + t, :])
                link(ins)
                for t in range(TQ):
                    ins = nc.vector.bn_aggr(mv[:, t, :], st[:, t, :])
                ins.then_inc(var_in, 1)
                dve.wait_ge(sd_in, 4 * i + c + 1)
                link(nc.vector.reciprocal(rstd[:], sd[:]))
                for t in range(TQ):
                    ins = nc.vector.tensor_scalar(xn[:, c * TQ + t, :], h[:, c * TQ + t, :], mv[:, t, 0:1],
                                                  rstd[:, t:t + 1], ALU.subtract, ALU.mult)
                ins.then_inc(xn_in, 1)

            def quad_banks(c):
                return ps[:, 2 * (c % 2):2 * (c % 2) + 2, :].rearrange("p a (b d) -> p (a b) d", d=D)

            def split_piece(s, w):
                a = s % NPS
                dve.wait_ge(pc_f, s + 1)
                if s >= NPS:
                    dve.wait_ge(pc_out[a], 16 * (s // NPS))
                    dve.wait_ge(pc_3, s - NPS + 1)
                link(nc.vector.tensor_tensor(rem[:, a, 0:w], qf[:, a, 0:w], parts[:, a, 0, 0:w], ALU.subtract))
                nc.vector.tensor_copy(parts[:, a, 1, 0:w], rem[:, a, 0:w]).then_inc(pc_12, 1)

            def attention_dve(layer):
                plan = PLANS[layer]
                nm = plan.nm

                def max_step(i, v, bank, ring):
                    qt, k0, w, hd, per = plan.maxes[i]
                    dve.wait_ge(mx_mm[layer], ring + 1)
                    if layer == 0:
                        o = mbf[:, hd:hd + per, qt]
                    else:
                        o = mA[:, hd:hd + per, qt] if k0 == 0 else mB[:, hd:hd + per, qt - 4]
                    nc.vector.tensor_reduce(o, ps[:, bank, 0:per * w].rearrange("p (j k) -> p j k", j=per),
                                            AX.X, ALU.max).then_inc(mx_free[layer], 1)
                    if i < nm - 1:
                        return
                    dve.wait_ge(mx_free[layer], ring + 4)
                    if layer == 0:
                        dve.sem_inc(m_in[layer], 1)
                    else:
                        nc.vector.tensor_copy(mbf[:, :, 0:4], mA[:, :, 0:4])
                        nc.vector.tensor_tensor(mbf[:, :, 4:8], mA[:, :, 4:8], mB[:, :, :], ALU.max)\
                          .then_inc(m_in[layer], 1)

                def max_row(a, bank, ring):
                    dve.wait_ge(mx_mm[layer], ring + 1)
                    nc.vector.tensor_copy(mT[:, a, :], ps[0:32, bank, 0:64].bitcast(BF16))\
                      .then_inc(mx_free[layer], 1)
                    dve.wait_ge(mx_free[layer], ring + 4)
                    dve.sem_inc(mT_in[layer], 1)

                def norm(u, qh, bank, ring):
                    o = ps[:, bank, :].rearrange("p (t j r) -> p t j r", t=TQ, j=G4)
                    dve.wait_ge(mx_mm[layer], ring + 1)
                    nc.vector.reciprocal(rden[:, qh, :, :].unsqueeze(3), o[:, :, :, HD:HD + 1]).then_inc(rden_in[layer], 1)
                    dve.wait_ge(rden_in[layer], 2 * u + qh + 1)
                    nc.vector.tensor_tensor(
                        oN[:, TQ * qh:TQ * qh + TQ, ds(u, 1), :, :].rearrange("p t u j r -> p (t u) j r"),
                        o[:, :, :, 0:HD], rden[:, qh, :, :].unsqueeze(3).broadcast_to([P, TQ, G4, HD]), ALU.mult)\
                      .then_inc(mx_free[layer], 1)

                def unit(this, phase, **ends):
                    u, a, _, ring = this
                    v, b, _ = after(this)
                    k = 0
                    for what, *i in plan.of(**ends):
                        at = (RING[(phase + k) % 3], ring + k)
                        if what == "max":
                            max_step(i[0], v, *at)
                        elif what == "maxrow":
                            max_row(b, *at)
                        elif what == "turn":
                            norm(u, i[0], *at)
                        elif what == "lastturn":
                            norm(u - 1, i[0], *at)
                        else:
                            continue
                        k += 1

                dve.sem_inc(mx_free[layer], 3)
                for i in range(nm):
                    max_step(i, 0, RING[i % 3], i)
                max_row(0, RING[nm % 3], nm)
                first, middle, last = plan.units()
                unit(first, first[3], first=True, last=False)
                with dve.Fori(0, (NU - 2) // 3) as i:
                    for d in range(3):
                        unit(middle(i, d), middle(0, d)[3], first=False, last=False)
                unit(last, last[3], first=False, last=True)
                dve.wait_ge(mx_free[layer], last[3] + 3 + 3)

            def pick(scores, ne, ntop, values, gates, n8):
                for t in range(NT):
                    ins = nc.vector.max(mx8[:, t, :], values[:, t, :])
                link(ins)
                for t in range(NT):
                    ins = nc.vector.max_index(ix8[:, t, :], mx8[:, t, :], values[:, t, :])
                link(ins)
                link(nc.vector.tensor_copy(ixf[:], ix8[:]))
                io = iota[:, 0:ne].unsqueeze(1).broadcast_to([P, NT, ne])
                for j in range(ntop):
                    dst = hit if j == 0 else eq
                    link(nc.vector.tensor_tensor(dst[:, :, 0:ne], io, ixf[:, :, j:j + 1].broadcast_to([P, NT, ne]),
                                                 ALU.is_equal))
                    if j:
                        link(nc.vector.tensor_tensor(hit[:, :, 0:ne], hit[:, :, 0:ne], eq[:, :, 0:ne], ALU.add))
                nc.vector.tensor_tensor(gates[:], scores, hit[:, :, 0:ne], ALU.mult).then_inc(gate_in, 1)

            for c in range(NQ):
                dve.wait_ge(table_in[c], 16 * TQ)
                dve.wait_ge(prod, c + 1)
                for half in range(2):
                    t0 = c * TQ + 2 * half
                    ins = nc.vector.scalar_tensor_tensor(
                        h[:, t0:t0 + 2, :], quad_banks(c)[:, 2 * half:2 * half + 2, :], 2.0,
                        rows[:, t0:t0 + 2, 0:D], ALU.mult, ALU.add)
                ins.then_inc(taken, 1)
                dve.wait_ge(taken, c + 1)
                layernorm(0, c)
            dve.sem_inc(dve_left, 1)

            dve.wait_ge(w_l0, 16 * 6)
            dve.wait_ge(consts, NCONST)
            link(nc.vector.tensor_scalar(bq4[:], bq_sb[:], 0.25, None, ALU.mult))
            dve.sem_inc(consts, 1)
            for b in range(B):
                dve.wait_ge(imp_mm, b + 1)
                nc.vector.tensor_scalar(impc[:, b, :], ps[:, 6 + b, 0:8], bi2_sb[:], None, ALU.add)\
                  .then_inc(imp_in, 1)
            dve.wait_ge(imp_in, B)
            dve.wait_ge(w_l0b, 16 * 5)
            for b in range(B):
                dve.wait_ge(impb_mm, b + 1)
                row = ps[:, 4:6, :].rearrange("p a n -> p (a n)")
                for t in range(8):
                    me = impc[:, b, t:t + 1]
                    lo, hi_ = t * P, (t + 1) * P
                    j = junk[:, t % G4, :]
                    if t > 0:
                        nc.vector.tensor_scalar(j[:, 0:lo], row[:, 0:lo], me, None, ALU.is_ge, ALU.add,
                                                accum_out=rkp[:, t, 0:1])
                    else:
                        nc.vector.memset(rkp[:, t, 0:1], 0.0)
                    if t < 7:
                        nc.vector.tensor_scalar(j[:, hi_:S], row[:, hi_:S], me, None, ALU.is_gt, ALU.add,
                                                accum_out=rkp[:, t, 1:2])
                    else:
                        nc.vector.memset(rkp[:, t, 1:2], 0.0)
                    nc.vector.tensor_scalar(j[:, lo:hi_], row[:, lo:hi_], me, None, ALU.is_gt, ALU.add,
                                            accum_out=rkp[:, t, 2:3])
                    ins = nc.vector.scalar_tensor_tensor(junk_eq[:, t, :], row[:, lo:hi_], me, before[:], ALU.is_equal,
                                                         ALU.mult, accum_out=rkp[:, t, 3:4])
                    if t % G4 == G4 - 1:
                        link(ins)
                link(nc.vector.tensor_reduce(rank[:], rkp[:], AX.X, ALU.add))
                if b:
                    dve.wait_ge(xc_mm, b)
                for t in range(8):
                    ins = nc.vector.tensor_scalar(sel[:, t, :], iota[:], rank[:, t:t + 1], None, ALU.is_equal)
                ins.then_inc(sel_in, 1)
                dve.wait_ge(sel_in, b + 1)
                for i in range(4):
                    split_piece(6 * b + i, QW)
                for i in range(4, 6):
                    split_piece(6 * b + i, TOPK)
                for c, (_, n) in enumerate(KCH):
                    dve.wait_ge(v_mm, 3 * b + c + 1)
                    nc.vector.tensor_tensor(
                        vaug[0:n, 4 * b:4 * b + 4, c, :, 0:HD],
                        ps[0:n, 2 + (3 * b + c) % 2, 0:D].rearrange("p (g j r) -> p g j r", g=G4, j=G4),
                        bv_sb[0:n, :].rearrange("p (g j r) -> p g j r", g=G4, j=G4), ALU.add).then_inc(v_in, 1)
            dve.wait_ge(v_in, 6)
            dve.sem_inc(dve_left, 1)

            attention_dve(0)
            dve.sem_inc(dve_left, 1)

            def project(i):
                for c in range(NQ):
                    hc = h[:, c * TQ:(c + 1) * TQ, :]
                    dve.wait_ge(prod, 4 * (i if i == 1 else 2) + c + 1)
                    dve.wait_ge(biased, 4 * (0 if i == 1 else 1) + c + 1)
                    nc.vector.tensor_tensor(hc, quad_banks(c), hc, ALU.add).then_inc(taken, 1)
                    dve.wait_ge(taken, 4 * i + c + 1)
                    layernorm(i, c)
                dve.sem_inc(dve_left, 1)

            def sigmoid(ne, n):
                dve.wait_ge(gate_e, n)
                link(nc.vector.tensor_scalar(sc[:, :, 0:ne], ge[:, :, 0:ne], 1.0, None, ALU.add))
                link(nc.vector.reciprocal(sc[:, :, 0:ne], sc[:, :, 0:ne]))

            project(1)
            sigmoid(E0, 1)
            link(nc.vector.tensor_tensor(bi[:], sc[:, :, 0:E0], eb_sb[:].unsqueeze(1).broadcast_to([P, NT, E0]), ALU.add))
            pick(sc[:, :, 0:E0], E0, 2, bi, g0, E0)
            dve.wait_ge(gate_in, 1)
            for c in range(NQ):
                def scaled(e, first):
                    if not first:
                        dve.wait_ge(xe_mm, E0 * c + e)
                    for t in range(TQ):
                        tt = c * TQ + t
                        ins = nc.vector.tensor_scalar(xs[:, t, :], xn[:, tt, :],
                                                      g0[:, tt, ds(e, 1)], None, ALU.mult)
                    ins.then_inc(xs_in, 1)

                def squares(e, a):
                    for m, (_, n) in enumerate(HCH):
                        dve.wait_ge(up_f, 3 * (E0 * c + e) + m + 1)
                        ins = nc.vector.tensor_tensor(hq[0:n, a, m, :], hr[0:n, m, :], hr[0:n, m, :], ALU.mult)
                        ins.then_inc(up_in, 1)

                for m, (_, n) in enumerate(HCH):
                    dve.wait_ge(sh_f, 3 * c + m + 1)
                    if c:
                        dve.wait_ge(sh_dn, c)
                    nc.vector.tensor_tensor(hs[0:n, m, :], hsf[0:n, m, :], hsf[0:n, m, :], ALU.mult).then_inc(sh_in, 1)
                if c:
                    dve.wait_ge(xe_mm, E0 * c)
                scaled(0, True)
                scaled(1, False)
                if c:
                    dve.wait_ge(dn_mm, E0 * c + 1)
                squares(0, 0)
                with dve.Fori(0, E0 - 3, 2) as e:
                    for a in range(2):
                        scaled(e + a + 2, False)
                        dve.wait_ge(dn_mm, E0 * c + e + a + 1)
                        squares(e + a + 1, 1 - a)
                dve.wait_ge(dn_mm, E0 * c + E0 - 1)
                squares(E0 - 1, 1)
                hc = h[:, c * TQ:(c + 1) * TQ, :]
                dve.wait_ge(dn_mm, E0 * (c + 1) + 1)
                nc.vector.tensor_tensor(hc, ps[:, 0:2, :].rearrange("p a (b d) -> p (a b) d", d=D), hc, ALU.add)\
                  .then_inc(taken, 1)
            dve.wait_ge(taken, 12)
            dve.sem_inc(dve_left, 1)

            for c in range(NQ):
                layernorm(2, c)
            for c in range(NQ):
                for i in range(4):
                    split_piece(NPC0 + 4 * c + i, QW)
                for t in range(TQ):
                    n = c * TQ + t
                    dve.wait_ge(v_mm, 6 + n + 1)
                    nc.vector.tensor_copy(
                        vaug[:, 4 * (n // 8):4 * (n // 8) + 4, n % 8, :, 0:HD],
                        ps[:, 6 + n % 2, 0:D].rearrange("p (g j r) -> p g j r", g=G4, j=G4)).then_inc(v_in, 1)
            dve.wait_ge(v_in, 6 + NT)
            dve.sem_inc(dve_left, 1)
            attention_dve(1)
            dve.sem_inc(dve_left, 1)
            project(3)
            sigmoid(E1, 2)
            pick(sc[:, :, :], E1, TOP1, sc, g1, E1)
            dve.wait_ge(gate_in, 2)
            dve.sem_inc(ey_add, 8)
            with dve.Fori(0, E1) as e:
                for t in range(NT):
                    dve.wait_ge(ey_mm, NT // 2 * e + t // 2 + 1)
                    nc.vector.scalar_tensor_tensor(h[:, t, :], ps[:, 4 + (t // 2) % 4, (t % 2) * D:(t % 2 + 1) * D],
                                                   g1[:, t, ds(e, 1)], h[:, t, :], ALU.mult, ALU.add)\
                      .then_inc(ey_add, 1)

        @block.scalar
        def _(act):
            def ln_scalar(i, c):
                act.wait_ge(var_in, 4 * i + c + 1)
                nc.scalar.activation(sd[:], mv[:, :, 1], ACT.Sqrt, bias=eps[:]).then_inc(sd_in, 1)
                act.wait_ge(tr_mm, 4 * i + c + 1)
                if i == 3:
                    nc.scalar.activation(xp[:, 0, :, c * QW:(c + 1) * QW], ps[:, 4 + 2 * (c % 2):6 + 2 * (c % 2), :],
                                         ACT.Copy)
                nc.scalar.activation(xT[:, :, c * QW:(c + 1) * QW], ps[:, 4 + 2 * (c % 2):6 + 2 * (c % 2), :],
                                     ACT.Copy).then_inc(xT_in, 1)

            def piece(s, w, scale, bias):
                a = s % NPS
                act.wait_ge(pc_mm, s + 1)
                if s >= NPS:
                    act.wait_ge(pc_12, s - NPS + 1)
                    act.wait_ge(pc_out[a], 16 * (s // NPS))
                nc.scalar.activation(qf[:, a, 0:w], ps[:, s % 2, 0:w], ACT.Identity, bias=bias, scale=scale)
                nc.scalar.activation(parts[:, a, 0, 0:w], ps[:, s % 2, 0:w], ACT.Identity, bias=bias, scale=scale)\
                  .then_inc(pc_f, 1)

            def attention_act(layer):
                plan = PLANS[layer]
                ne = plan.ne

                def evacuate(u, qh):
                    act.wait_ge(p_free[layer], ne * u + plan.last[qh] + 3)
                    nc.scalar.activation(oc[:, qh, :], ps[:, 6, :], ACT.Copy).then_inc(o_free[layer], 1)

                def unit(u, first=False):
                    for g, (qh, c, n, q0, w) in enumerate(plan.exps):
                        for pair in range(2):
                            k = 2 * g + pair
                            act.wait_ge(st_mm[layer], 2 * ne * u + k + 1)
                            if pair == 0:
                                act.wait_ge(p_free[layer], ne * u + g + 1)
                            nc.scalar.activation(pT[0:n, g % 2, 2 * pair:2 * pair + 2, 0:w],
                                                 ps[0:n, 2 * pair:2 * pair + 2, 0:w], ACT.Exp)\
                              .then_inc(p_in[layer], 1)
                        if g == 0 and not first:
                            evacuate(u - 1, 1)
                        if g == plan.last[0] + 1:
                            evacuate(u, 0)

                first, middle, last = plan.units()
                unit(first[0], first=True)
                with act.Fori(0, (NU - 2) // 3) as i:
                    for d in range(3):
                        unit(middle(i, d)[0])
                unit(last[0])
                evacuate(last[0], 1)
                act.wait_ge(o_free[layer], 1 + 2 * NU)

            def project_act(i, n):
                def out_columns(c):
                    act.wait_ge(o_mm, 4 * n + c + 1)
                    nc.scalar.activation(oT[:, c % 2, :, :], ps[:, 4 + 2 * (c % 2):6 + 2 * (c % 2), :],
                                         ACT.Copy).then_inc(oT_in, 1)

                out_columns(0)
                out_columns(1)
                for c in range(NQ):
                    ln_scalar(i, c)
                    if c + 2 < NQ:
                        out_columns(c + 2)

            act.wait_ge(consts, NFIRST)
            for c in range(NQ):
                act.wait_ge(aT_mm, c + 1)
                nc.scalar.activation(aT[:, c * QW:(c + 1) * QW], ps[0:R, 4 + c, :], ACT.Copy).then_inc(aT_sb, 1)
            for c in range(NQ):
                ln_scalar(0, c)
            act.wait_ge(xT_in, 4)
            act.sem_inc(act_left, 1)
            act.wait_ge(w_l0, 16 * 6)
            act.wait_ge(consts, NCONST + 1)
            for b in range(B):
                for c in range(2 * b, 2 * b + 2):
                    act.wait_ge(ih_mm, c + 1)
                    if c >= 2:
                        act.wait_ge(imp_mm, b)
                    nc.scalar.activation(hi[:, c % 2, :], ps[:, 2 + c % 2, :], ACT.Relu, bias=bi1_sb[:])\
                      .then_inc(hi_in, 1)
            for b in range(B):
                for i in range(4):
                    piece(6 * b + i, QW, 0.25, bq4[:, i // 2:i // 2 + 1])
                act.wait_ge(xc_mm, b + 1)
                nc.scalar.activation(xcT, ps[:, 6:8, 0:TOPK], ACT.Copy).then_inc(xc_in, 1)
                for i in range(2):
                    piece(6 * b + 4 + i, TOPK, 1.0, bk_sb[:, i:i + 1])
            act.wait_ge(pc_f, NPC0)
            act.sem_inc(act_left, 1)
            attention_act(0)
            act.sem_inc(act_left, 1)
            project_act(1, 0)
            act.wait_ge(xT_in, 8)
            act.sem_inc(act_left, 1)
            act.wait_ge(gate_mm, 1)
            nc.scalar.activation(ge[:, :, 0:E0], ps[:, 7, 0:NT * E0].rearrange("p (t e) -> p t e", e=E0),
                                 ACT.Exp, scale=-1.0).then_inc(gate_e, 1)
            for c in range(NQ):
                def relus(e, a, first=False):
                    for m, (_, n) in enumerate(HCH):
                        if c or not first:
                            act.wait_ge(up_in, 3 * (E0 * c + e - 1) + m + 1)
                        act.wait_ge(up_mm, 3 * (E0 * c + e) + m + 1)
                        nc.scalar.activation(hr[0:n, m, :], ps[0:n, 2 + m, :], ACT.Relu).then_inc(up_f, 1)

                def columns(e, a):
                    act.wait_ge(xe_mm, E0 * c + e + 1)
                    nc.scalar.activation(xeT[:, a, :, :].rearrange("p k t -> p (k t)"),
                                         ps[:, 5 + a, :].bitcast(BF16), ACT.Copy).then_inc(xe_in, 1)

                for m, (_, n) in enumerate(HCH):
                    act.wait_ge(sh_mm, 3 * c + m + 1)
                    if c:
                        act.wait_ge(sh_in, 3 * c)
                    nc.scalar.activation(hsf[0:n, m, :], ps[0:n, 2 + m, :], ACT.Relu).then_inc(sh_f, 1)
                columns(0, 0)
                relus(0, 0, True)
                columns(1, 1)
                with act.Fori(0, E0 - 3, 2) as e:
                    for a in range(2):
                        relus(e + a + 1, 1 - a)
                        columns(e + a + 2, a)
                relus(E0 - 1, 1)
            act.wait_ge(up_f, 3 * E0 * NQ)
            act.sem_inc(act_left, 1)
            for c in range(NQ):
                ln_scalar(2, c)
            for c in range(NQ):
                a = c % 2
                for i, lat in enumerate((latqk, latv)):
                    act.wait_ge(lat_mm, 2 * c + i + 1)
                    nc.scalar.activation(lat[:, a, :], ps[:, 2 + i, :], ACT.Copy).then_inc(lat_in, 1)
                for i in range(4):
                    piece(NPC0 + 4 * c + i, QW, 0.25 if i < 2 else 1.0, 0.0)
            act.wait_ge(pc_f, NPC0 + 16)
            act.sem_inc(act_left, 1)
            attention_act(1)
            act.sem_inc(act_left, 1)
            project_act(3, 1)
            act.wait_ge(xT_in, 16)
            act.sem_inc(act_left, 1)
            act.wait_ge(gate_mm, 2)
            nc.scalar.activation(ge[:, :, :], ps[:, 7, :].rearrange("p (t e) -> p t e", e=E1),
                                 ACT.Exp, scale=-1.0).then_inc(gate_e, 1)
            act.wait_ge(xn_in, 16)
            def hidden(e, a):
                for c in range(NQ):
                    act.wait_ge(ex_mm, NQ * e + c + 1)
                    act.wait_ge(ex_lo, NQ * e + c + 1)
                    nc.scalar.activation(hf[:, c % 2, :], ps[:, c, :], ACT.Relu)
                    nc.scalar.activation(hp[:, a, 0, c * QW:(c + 1) * QW], ps[:, c, :], ACT.Relu)\
                      .then_inc(ex_f, 1)

            def high_weights(e, a):
                act.wait_ge(ew_in[a], 16 * (e - a + 2))
                nc.scalar.activation(ewp[:, a, 0, :], ew[:, a, :], ACT.Copy).then_inc(ewp_hi, 1)

            high_weights(0, 0)
            act.sem_inc(ex_f, NQ)
            with act.Fori(0, E1 - 3, 2) as e:
                for a in range(2):
                    hidden(e + a, a)
                    act.wait_ge(ey_add, NT * (e + a) + 8)
                    high_weights(e + a + 1, 1 - a)
            hidden(E1 - 2, 0)
            act.wait_ge(ey_add, NT * (E1 - 2) + 8)
            high_weights(E1 - 1, 1)
            hidden(E1 - 1, 1)

        @block.tensor
        def _(pe):
            def stage(n):
                pe.wait_ge(act_left, n)
                pe.wait_ge(dve_left, n)

            def transposes(i, c):
                pe.wait_ge(xn_in, 4 * i + c + 1)
                if c >= 2:
                    pe.wait_ge(xT_in, 4 * i + c - 1)
                for t in range(TQ):
                    for k in range(KD):
                        mm = pe.transpose(ps[:, 4 + 2 * (c % 2) + k, t * P:(t + 1) * P],
                                          xn[:, c * TQ + t, k * P:(k + 1) * P], ident[:])
                mm.then_inc(tr_mm, 1)

            def attention_pe(layer):
                plan = PLANS[layer]
                ne, nm, cuts, chunk = plan.ne, plan.nm, plan.cuts, plan.chunk

                def scores(g, pair, u, a, first):
                    qh, c, n, q0, w = plan.exps[g]
                    k = 2 * g + pair
                    if not first or k >= 2:
                        pe.wait_ge(p_in[layer], 2 * ne * u + k - 1)
                    for j in range(2):
                        hd = 2 * pair + j
                        mm = pe.matmul(ps[0:n, 2 * pair + j, 0:w], ks[0:QROWS + 1, a, hd, c * chunk:c * chunk + n],
                                       qs[0:QROWS + 1, a, hd, qh * QW + q0:qh * QW + q0 + w],
                                       start=True, stop=True)
                    mm.then_inc(st_mm[layer], 1)

                def values(g, u, a):
                    qh, c, n, q0, w = plan.exps[g]
                    pe.wait_ge(p_in[layer], 2 * ne * u + 2 * g + 2)
                    if g in cuts:
                        pe.wait_ge(p_cut[layer], len(cuts) * u + cuts.index(g) + 2)
                    if g in plan.first:
                        pe.wait_ge(o_free[layer], 2 * u + qh + 1)
                    for j in range(G4):
                        mm = pe.matmul(ps[32 * j:32 * j + 32, 6, q0:q0 + w], vst[0:n, a, c, j, :],
                                       pT[0:n, g % 2, j, 0:w], start=(g in plan.first), stop=(g in plan.last),
                                       skip_group_check=True)
                    mm.then_inc(p_free[layer], 1)

                def turn(u, qh, bank, ring):
                    pe.wait_ge(o_free[layer], 2 * u + qh + 2)
                    pe.wait_ge(mx_free[layer], ring + 1)
                    for t in range(TQ):
                        mm = pe.transpose(ps[:, bank, t * P:(t + 1) * P], oc[:, qh, t * P:(t + 1) * P], ident[:])
                    mm.then_inc(mx_mm[layer], 1)

                def max_scores(i, a, bank, ring):
                    qt, k0, w, hd, per = plan.maxes[i]
                    pe.wait_ge(mx_free[layer], ring + 1)
                    diagonal = layer == 1 and k0 + w == (qt + 1) * P
                    for j in range(per):
                        mm = pe.matmul(ps[:, bank, j * w:(j + 1) * w], qs[0:QROWS, a, hd + j, qt * P:(qt + 1) * P],
                                       ks[0:QROWS, a, hd + j, k0:k0 + w], start=(j == 0),
                                       stop=not diagonal, skip_group_check=True)
                    if diagonal:
                        for j in range(per):
                            mm = pe.matmul(ps[:, bank, (j + 1) * w - P:(j + 1) * w], identb[:], causal[:],
                                           start=False, stop=True, skip_group_check=True)
                    mm.then_inc(mx_mm[layer], 1)

                def max_row(v, bank, ring):
                    pe.wait_ge(m_in[layer], v + 1)
                    pe.wait_ge(mx_free[layer], ring + 1)
                    pe.transpose(ps[0:32, bank, 0:64].bitcast(BF16), mbf[:].rearrange("p j q -> p (j q)"),
                                 identb[:]).then_inc(mx_mm[layer], 1)

                def unit(this, phase, **ends):
                    u, a, n, ring = this
                    v, b, nb = after(this)
                    pe.wait_ge(mrow_in[layer][a], 16 * n + 16)
                    if not ends["last"]:
                        pe.wait_ge(qk_in[layer][b], 192 * nb + 192)
                    k = 0
                    for what, *i in plan.of(**ends):
                        at = (RING[(phase + k) % 3], ring + k)
                        if what == "scores":
                            scores(*i, u, a, ends["first"])
                        elif what == "values":
                            if i[0] == 0:
                                pe.wait_ge(vst_in[layer], u + 4)
                            values(i[0], u, a)
                        elif what == "lastvalues":
                            values(i[0], u - 1, (a + 2) % 3)
                        else:
                            k += 1
                            if what == "max":
                                max_scores(i[0], b, *at)
                            elif what == "maxrow":
                                max_row(v, *at)
                            elif what == "turn":
                                turn(u, i[0], *at)
                            else:
                                turn(u - 1, i[0], *at)

                pe.sem_inc(p_free[layer], 2)
                pe.sem_inc(o_free[layer], 1)
                pe.wait_ge(vst_in[layer], 3)
                pe.wait_ge(qk_in[layer][0], 192)
                for i in range(nm):
                    max_scores(i, 0, RING[i % 3], i)
                max_row(0, RING[nm % 3], nm)
                first, middle, last = plan.units()
                unit(first, first[3], first=True, last=False)
                with pe.Fori(0, (NU - 2) // 3) as i:
                    for d in range(3):
                        unit(middle(i, d), middle(0, d)[3], first=False, last=False)
                unit(last, last[3], first=False, last=True)

            def project(i, w, n):
                def out_turn(c):
                    if c >= 2:
                        pe.wait_ge(xT_in, 4 * i + c - 1)
                    for t in range(TQ):
                        b, tile = divmod(c * TQ + t, 8)
                        for k in range(KD):
                            mm = pe.transpose(ps[:, 4 + 2 * (c % 2) + k, t * P:(t + 1) * P],
                                              oN[:, tile, 4 * b + 2 * k:4 * b + 2 * k + 2, :, :]
                                              .rearrange("p u j r -> p (u j r)"), ident[:])
                    mm.then_inc(o_mm, 1)

                out_turn(0)
                out_turn(1)
                for c in range(NQ):
                    pe.wait_ge(oT_in, 4 * n + c + 1)
                    if c >= 2:
                        pe.wait_ge(taken, 4 * i + c - 1)
                    for t in range(TQ):
                        for k in range(KD):
                            mm = pe.matmul(ps[:, 2 * (c % 2) + t // 2, (t % 2) * D:(t % 2 + 1) * D],
                                           oT[:, c % 2, k, t * P:(t + 1) * P], w[:, k, :],
                                           start=(k == 0), stop=(k == KD - 1))
                    mm.then_inc(prod, 1)
                    if c:
                        transposes(i, c - 1)
                        if c + 1 < NQ:
                            out_turn(c + 1)
                transposes(i, NQ - 1)

            def gates(w, ne):
                for t in range(NT):
                    for k in range(KD):
                        mm = pe.matmul(ps[:, 7, t * ne:(t + 1) * ne], xT[:, k, t * P:(t + 1) * P], w[:, k, :],
                                       start=(k == 0), stop=(k == KD - 1))
                mm.then_inc(gate_mm, 1)

            pe.wait_ge(consts, NFIRST)
            pe.wait_ge(w_emb, 16)
            for c in range(NQ):
                pe.wait_ge(table_in[c], 16 * TQ)
                for t in range(TQ):
                    mm = pe.transpose(ps[0:R, 4 + c, t * P:(t + 1) * P], rows[:, c * TQ + t, D:D + R], ident[:])
                mm.then_inc(aT_mm, 1)
            for c in range(NQ):
                pe.wait_ge(aT_sb, NQ)
                if c >= 2:
                    pe.wait_ge(taken, c - 1)
                for t in range(TQ):
                    tt = c * TQ + t
                    mm = pe.matmul(ps[:, 2 * (c % 2) + t // 2, (t % 2) * D:(t % 2 + 1) * D],
                                   aT[:, tt * P:(tt + 1) * P], loraB_sb[:], start=True, stop=True)
                mm.then_inc(prod, 1)
                if c:
                    transposes(0, c - 1)
            transposes(0, NQ - 1)

            stage(1)
            pe.wait_ge(w_l0, 16 * 6)
            pe.wait_ge(consts, NCONST)
            for b in range(B):
                for c in range(2 * b, 2 * b + 2):
                    pe.wait_ge(xT_in, c + 1)
                    if c >= 2:
                        pe.wait_ge(hi_in, c - 1)
                    for k in range(KD):
                        mm = pe.matmul(ps[:, 2 + c % 2, :], wi1_sb[:, k, :], xT[:, k, c * QW:(c + 1) * QW],
                                       start=(k == 0), stop=(k == KD - 1))
                    mm.then_inc(ih_mm, 1)
                pe.wait_ge(hi_in, 2 * b + 2)
                for t in range(8):
                    mm = pe.matmul(ps[:, 6 + b, t:t + 1], hi[:, t // 4, (t % 4) * P:(t % 4 + 1) * P],
                                   wi2_sb[:], start=True, stop=True)
                mm.then_inc(imp_mm, 1)
            pe.wait_ge(w_l0b, 16 * 5)
            for b in range(B):
                pe.wait_ge(imp_in, B)
                if b:
                    pe.wait_ge(sel_in, b)
                for t in range(8):
                    mm = pe.transpose(ps[:, 4 + t // 4, (t % 4) * P:(t % 4 + 1) * P],
                                      impc[:, b, t:t + 1].broadcast_to([P, P]), ident[:])
                mm.then_inc(impb_mm, 1)
                for i in range(4):
                    s = 6 * b + i
                    if s >= 2:
                        pe.wait_ge(pc_f, s - 1)
                    for k in range(KD):
                        mm = pe.matmul(ps[:, s % 2, :], wq_sb[:, k, (i // 2) * P:(i // 2 + 1) * P],
                                       xT[:, k, b * S + (i % 2) * QW:b * S + (i % 2 + 1) * QW],
                                       start=(k == 0), stop=(k == KD - 1))
                    mm.then_inc(pc_mm, 1)
                pe.wait_ge(sel_in, b + 1)
                for k in range(KD):
                    for t in range(8):
                        mm = pe.matmul(ps[:, 6 + k, 0:TOPK], xn[:, 8 * b + t, k * P:(k + 1) * P], sel[:, t, :],
                                       start=(t == 0), stop=(t == 7))
                mm.then_inc(xc_mm, 1)
                pe.wait_ge(xc_in, b + 1)
                for i in range(2):
                    s = 6 * b + 4 + i
                    pe.wait_ge(pc_f, s - 1)
                    for k in range(KD):
                        mm = pe.matmul(ps[:, s % 2, 0:TOPK], wk_sb[:, k, i * P:(i + 1) * P], xcT[:, k, :],
                                       start=(k == 0), stop=(k == KD - 1))
                    mm.then_inc(pc_mm, 1)
                for c, (c0, n) in enumerate(KCH):
                    if 3 * b + c >= 2:
                        pe.wait_ge(v_in, 3 * b + c - 1)
                    for k in range(KD):
                        mm = pe.matmul(ps[0:n, 2 + (3 * b + c) % 2, 0:D], xcT[:, k, c0:c0 + n], wv_sb[:, k, :],
                                       start=(k == 0), stop=(k == KD - 1))
                    mm.then_inc(v_mm, 1)

            stage(2)
            attention_pe(0)
            stage(3)
            pe.wait_ge(w_proj_in, 16 * 2)
            project(1, wo_sb, 0)
            stage(4)
            pe.wait_ge(w_l1, 16 * 11)
            gates(gw_sb, E0)
            pe.wait_ge(w_moe, 16 * 4)
            pe.sem_inc(dn_mm, 1)
            for c in range(NQ):
                def turned(e, a):
                    pe.wait_ge(xs_in, E0 * c + e + 1)
                    for t in range(TQ):
                        for k in range(KD):
                            mm = pe.transpose(ps[:, 5 + a, :].bitcast(BF16)[:, k * QW + t * P:k * QW + (t + 1) * P],
                                              xs[:, t, k * P:(k + 1) * P], identb[:])
                    mm.then_inc(xe_mm, 1)

                def up(e, a, first=False):
                    pe.wait_ge(xe_in, E0 * c + e + 1)
                    for m, (c0, n) in enumerate(HCH):
                        if not first:
                            pe.wait_ge(up_f, 3 * (E0 * c + e - 1) + m + 1)
                        for k in range(KD):
                            mm = pe.matmul(ps[0:n, 2 + m, :],
                                           up_sb[:, k, ds(e, 1), c0:c0 + n].rearrange("p e f -> p (e f)"),
                                           xeT[:, a, k, :], start=(k == 0), stop=(k == KD - 1))
                        mm.then_inc(up_mm, 1)

                def down(e, a, last):
                    for m, (_, n) in enumerate(HCH):
                        pe.wait_ge(up_in, 3 * (E0 * c + e) + m + 1)
                        for t in range(TQ):
                            mm = pe.matmul(ps[:, t // 2, (t % 2) * D:(t % 2 + 1) * D],
                                           hq[0:n, a, m, t * P:(t + 1) * P],
                                           dn_sb[0:n, m, ds(e, 1), :].rearrange("p e d -> p (e d)"),
                                           start=False, stop=last and m == 2, skip_group_check=True)
                    mm.then_inc(dn_mm, 1)

                if c:
                    pe.wait_ge(up_f, 3 * E0 * c)
                for m, (c0, n) in enumerate(HCH):
                    for k in range(KD):
                        mm = pe.matmul(ps[0:n, 2 + m, :], shu_sb[:, k, c0:c0 + n], xT[:, k, c * QW:(c + 1) * QW],
                                       start=(k == 0), stop=(k == KD - 1))
                    mm.then_inc(sh_mm, 1)
                if c == 0:
                    pe.wait_ge(gate_e, 1)
                turned(0, 0)
                if c:
                    pe.wait_ge(taken, 8 + c)
                for m, (_, n) in enumerate(HCH):
                    pe.wait_ge(sh_in, 3 * c + m + 1)
                    for t in range(TQ):
                        mm = pe.matmul(ps[:, t // 2, (t % 2) * D:(t % 2 + 1) * D], hs[0:n, m, t * P:(t + 1) * P],
                                       shd_sb[0:n, m, :], start=(m == 0 and t % 2 == 0), stop=False,
                                       skip_group_check=True)
                mm.then_inc(sh_dn, 1)
                if c == 0:
                    pe.wait_ge(w_moeb, 16 * 5)
                pe.wait_ge(sh_f, 3 * (c + 1))
                up(0, 0, True)
                turned(1, 1)
                with pe.Fori(0, E0 - 3, 2) as e:
                    for a in range(2):
                        up(e + a + 1, 1 - a)
                        turned(e + a + 2, a)
                        down(e + a, a, False)
                up(E0 - 1, 1)
                down(E0 - 2, 0, False)
                down(E0 - 1, 1, True)

            stage(5)
            for c in range(NQ):
                transposes(2, c)
            for c in range(NQ):
                pe.wait_ge(xT_in, 12)
                if c:
                    pe.wait_ge(lat_in, 2 * c)
                for i in range(2):
                    for k in range(KD):
                        mm = pe.matmul(ps[:, 2 + i, :],
                                       wl_sb[:, k, 2 * i:2 * i + 2, :].rearrange("p a l -> p (a l)"),
                                       xT[:, k, c * QW:(c + 1) * QW], start=(k == 0), stop=(k == KD - 1))
                    mm.then_inc(lat_mm, 1)
                pe.wait_ge(lat_in, 2 * c + 1)
                for i in range(4):
                    s = NPC0 + 4 * c + i
                    pe.wait_ge(pc_f, s - 1)
                    pe.matmul(ps[:, s % 2, :], wh_sb[:, i // 2, (i % 2) * P:(i % 2 + 1) * P], latqk[:, c % 2, :],
                              start=True, stop=True).then_inc(pc_mm, 1)
                pe.wait_ge(lat_in, 2 * c + 2)
                for t in range(TQ):
                    n = c * TQ + t
                    if n >= 2:
                        pe.wait_ge(v_in, 6 + n - 1)
                    pe.matmul(ps[:, 6 + n % 2, 0:D], latv[:, c % 2, t * P:(t + 1) * P], wh_sb[:, 2, :],
                              start=True, stop=True).then_inc(v_mm, 1)
            stage(6)
            attention_pe(1)
            stage(7)
            project(3, wq_sb, 1)
            stage(8)
            gates(es_sb, E1)
            pe.wait_ge(gate_e, 2)
            pe.wait_ge(xp_in, NQ)
            products = ((0, 0), (0, 1), (1, 0))
            with pe.Fori(0, E1 - 1, 2) as e:
                for a in range(2):
                    pe.wait_ge(ewp_in, e + a + 1)
                    for c in range(NQ):
                        pe.wait_ge(ex_f, NQ * (e + a) + c + 1)
                        for k in range(KD):
                            for i, (i_w, i_x) in enumerate(products):
                                mm = pe.matmul(ps[:, c, :], ewp[:, a, i_w, k * F1:(k + 1) * F1],
                                               xp[:, i_x, k, c * QW:(c + 1) * QW],
                                               start=(k == 0 and i == 0), stop=(k == KD - 1 and i == 2))
                        mm.then_inc(ex_mm, 1)
                    for t in range(NT):
                        if t % TQ == 0:
                            pe.wait_ge(ex_lo, NQ * (e + a) + t // TQ + 1 + 2)
                        if t % 2 == 0:
                            pe.wait_ge(ey_add, NT * (e + a) + t + 2)
                        for i, (i_h, i_w) in enumerate(products):
                            mm = pe.matmul(ps[:, 4 + (t // 2) % 4, (t % 2) * D:(t % 2 + 1) * D],
                                           hp[:, a, i_h, t * P:(t + 1) * P], ewp[:, a, i_w, D:2 * D],
                                           start=(i == 0), stop=(i == 2))
                        if t % 2:
                            mm.then_inc(ey_mm, 1)


def kernel(x, L0_tok_emb_weight, L0_tok_lora_A, L0_tok_lora_B, L0_attn_wq, L0_attn_bq, L0_attn_wk, L0_attn_bk,
           L0_attn_wv, L0_attn_bv, L0_attn_wo, L0_attn_bo, L0_attn_wi1, L0_attn_bi1, L0_attn_wi2, L0_attn_bi2,
           L0_ffn_gate_w, L0_ffn_expert_bias, L0_ffn_w_up, L0_ffn_w_down, L0_ffn_shared_w_up, L0_ffn_shared_w_down,
           L1_attn_wq_lat, L1_attn_wk_lat, L1_attn_wv_lat, L1_attn_wq_heads, L1_attn_wk_heads, L1_attn_wv_heads,
           L1_attn_w_proj, L1_attn_b_proj, L1_ffn_expert_sel, L1_ffn_keys, L1_ffn_values):
    import numpy as np
    import concourse.bacc as bacc
    from concourse.bass_utils import run_bass_kernel_spmd

    nc = bacc.Bacc("TRN2", target_bir_lowering=False, num_devices=1)
    A = np.asarray
    arrays = {
        "ids": A(x).reshape(NT, P).T,
        "table": np.concatenate([A(L0_tok_emb_weight), A(L0_tok_lora_A).T], axis=1),
        "loraB": A(L0_tok_lora_B).T,
        "wq": A(L0_attn_wq).T, "wk": A(L0_attn_wk).T, "wv": A(L0_attn_wv).T, "wo": A(L0_attn_wo).T,
        "wi1": A(L0_attn_wi1).T, "wi2": A(L0_attn_wi2).T,
        "bq": A(L0_attn_bq).reshape(KD, P).T, "bk": A(L0_attn_bk).reshape(KD, P).T,
        "bv": A(L0_attn_bv), "bo": A(L0_attn_bo),
        "bi1": A(L0_attn_bi1).reshape(P, 1), "bi2": A(L0_attn_bi2),
        "gate_w": A(L0_ffn_gate_w).T, "e_bias": A(L0_ffn_expert_bias),
        "w_up": A(L0_ffn_w_up).transpose(2, 0, 1).reshape(D, E0 * HID),
        "w_down": A(L0_ffn_w_down).transpose(2, 0, 1).reshape(HID, E0 * D),
        "sh_up": A(L0_ffn_shared_w_up).T, "sh_down": A(L0_ffn_shared_w_down).T,
        "wq_lat": A(L1_attn_wq_lat), "wk_lat": A(L1_attn_wk_lat), "wv_lat": A(L1_attn_wv_lat),
        "wq_heads": A(L1_attn_wq_heads), "wk_heads": A(L1_attn_wk_heads), "wv_heads": A(L1_attn_wv_heads),
        "w_proj": A(L1_attn_w_proj), "b_proj": A(L1_attn_b_proj),
        "e_sel": A(L1_ffn_expert_sel).T, "e_keys": A(L1_ffn_keys), "e_values": A(L1_ffn_values),
    }
    arrays = {f"in_{k}": np.ascontiguousarray(v) for k, v in arrays.items()}
    args = [nc.dram_tensor(k, v.shape, mybir.dt.from_np(v.dtype), kind="ExternalInput").ap() for k, v in arrays.items()]
    out = nc.dram_tensor("out", (N, D), F32, kind="ExternalOutput").ap()
    order = ["ids", "table", "loraB", "wq", "wk", "wv", "wo", "wi1", "wi2", "bq", "bk", "bv", "bo", "bi1", "bi2",
             "gate_w", "e_bias", "w_up", "w_down", "sh_up", "sh_down", "wq_lat", "wk_lat", "wv_lat",
             "wq_heads", "wk_heads", "wv_heads", "w_proj", "b_proj", "e_sel", "e_keys", "e_values"]
    by_name = dict(zip([k[3:] for k in arrays], args))
    lm_tower(nc, *[by_name[k] for k in order], out)
    r = run_bass_kernel_spmd(nc, [arrays], core_ids=[0])
    return r.results[0]["out"].reshape(B, S, D)
```

```python
from contextlib import ExitStack

import concourse.bass as bass
from concourse import mybir
from concourse.bass import ds

F32 = mybir.dt.float32
F32R = mybir.dt.float32r
BF16 = mybir.dt.bfloat16
I32 = mybir.dt.int32
U32 = mybir.dt.uint32
ALU = mybir.AluOpType
ACT = mybir.ActivationFunctionType
AX = mybir.AxisListType

P = 128
B, S, D = 2, 1024, 256
N = B * S
NT = N // P
KD = D // P
QW = 512
NQ = N // QW
TQ = QW // P
R = 16
H, HD = 16, 16
G4 = 4
NU = B * H // G4
TOPK = int(S * 0.3)
CK = 103
KCH = [(c, min(CK, TOPK - c)) for c in range(0, TOPK, CK)]
QROWS = 96
E0, HID = 8, 352
HCH = [(c, min(P, HID - c)) for c in range(0, HID, P)]
LAT = 64
E1, F1, TOP1 = 32, 128, 4
NPS = 4
EPS = 1e-5
MASKED = -1.0e30
QPART = [0, 0, 1, 1, 0, 2]
KPART = [0, 1, 0, 1, 2, 0]


class Plan:

    def __init__(self, layer):
        self.layer = layer
        self.chunk = CK if layer == 0 else P
        self.nch = len(KCH) if layer == 0 else S // P
        if layer == 0:
            self.exps = [(qh, c, n, 0, QW) for qh in range(2) for c, (_, n) in enumerate(KCH)]
            self.maxes = [(qt, 0, TOPK, h, 1) for qt in range(S // P) for h in range(G4)]
            full = 4
        else:
            self.exps = []
            for qh, order in enumerate(((0, 3, 2, 1), (0, 7, 6, 5, 4, 3, 2, 1))):
                for c in order:
                    first = max(0, c * P - qh * QW)
                    self.exps.append((qh, c, P, first, QW - first))
            self.maxes = []
            for qt in range(S // P):
                for k0 in range(0, (qt + 1) * P, QW):
                    w = min(QW, (qt + 1) * P - k0)
                    per = min(G4, QW // w)
                    self.maxes += [(qt, k0, w, h, per) for h in range(0, G4, per)]
            full = 10
        self.ne, self.nm = len(self.exps), len(self.maxes)
        self.first = [min(g for g, e in enumerate(self.exps) if e[0] == qh) for qh in range(2)]
        self.last = [max(g for g, e in enumerate(self.exps) if e[0] == qh) for qh in range(2)]
        self.cuts = [g for g, e in enumerate(self.exps) if layer == 1 and e[1] * P >= e[0] * QW]
        self.steps, slots, done = [], 3 * full, 0
        for g in range(self.ne):
            rest = [("values", g - 1)] if g else [("lastvalues", self.ne - 1)]
            if g == 1:
                rest.append(("lastturn", 1))
            if g == self.last[0] + 2:
                rest.append(("turn", 0))
            for k, part in enumerate(([("scores", g, 0)], [("scores", g, 1)], rest)):
                self.steps += part
                upto = min(self.nm, (3 * g + k + 1) * self.nm // slots)
                self.steps += [("max", i) for i in range(done, upto)]
                if upto == self.nm and done < self.nm:
                    self.due = len(self.steps) + 1
                done = upto
        self.steps.insert(self.due, ("maxrow",))

    def of(self, first, last):
        return [s for s in self.steps if not (first and s[0].startswith("last"))
                and not (last and s[0].startswith("max"))] + \
            ([("values", self.ne - 1), ("turn", 1)] if last else [])

    def units(self):
        ring1 = 2 * (self.nm + 1) + 1
        per = self.nm + 3
        return ((0, 0, 0, self.nm + 1),
                lambda i, d: (3 * i + 1 + d, (1 + d) % 3, i + (1 + d) // 3, 3 * per * i + ring1 + per * d),
                (NU - 1, (NU - 1) % 3, (NU - 1) // 3, ring1 + per * (NU - 2)))


def after(unit):
    u, a, n, _ = unit
    return u + 1, (a + 1) % 3, n + (a + 1) // 3


def lm_tower(nc, ids, table, loraB, wq, wk, wv, wo, wi1, wi2, bq, bk, bv, bo, bi1, bi2,
             gate_w, e_bias, w_up, w_down, sh_up, sh_down,
             wq_lat, wk_lat, wv_lat, wq_heads, wk_heads, wv_heads, w_proj, b_proj,
             e_sel, e_keys, e_values, out):
    with ExitStack() as ctx:
        def sb(name, shape, dt=F32):
            return ctx.enter_context(nc.sbuf_tensor(name, shape, dt))

        def sem(name):
            return ctx.enter_context(nc.semaphore(name))

        ps = ctx.enter_context(nc.psum_tensor("ps", [P, 8, 512], F32))

        h = sb("h", [P, NT, D])
        xn = sb("xn", [P, NT, D])
        xT = sb("xT", [P, KD, N])
        oN = sb("oN", [P, 8, NU, G4, HD])
        with ExitStack() as early:
            vaug = early.enter_context(nc.sbuf_tensor("vaug", [P, NU, 8, G4, 32], F32))
            arena = early.enter_context(nc.sbuf_tensor("arena", [P, 16384], F32))
        xp = sb("xp", [P, 2, KD, N], F32R)
        hp = sb("hp", [P, 2, 2, N], F32R)
        ewp = sb("ewp", [P, 2, 2, 2 * D], F32R)
        spare = sb("spare", [P, 16384 - 10240])
        ks = sb("ks", [P, 3, G4, S], BF16)

        qs = arena[:, 0:6144].bitcast(BF16).rearrange("p (a h t) -> p a h t", a=3, h=G4)
        pT = arena[:, 6144:10240].rearrange("p (a h t) -> p a h t", a=2, h=G4)
        oc = arena[:, 10240:11264].rearrange("p (a t) -> p a t", a=2)
        vst = arena[:, 11264:14336].rearrange("p (a c j r) -> p a c j r", a=3, c=8, j=G4)
        rows = arena[:, 0:NT * (D + R)].rearrange("p (t d) -> p t d", t=NT)
        aT = arena[0:R, 8192:8192 + N]
        oN_flat = oN[:].rearrange("p t u j r -> p (t u j r)")
        hi = oN_flat[:, 0:1024].rearrange("p (a t) -> p a t", a=2)
        sel = oN_flat[:, 1024:1024 + 8 * TOPK].rearrange("p (t k) -> p t k", t=8)
        xcT = oN_flat[:, 3480:3480 + KD * TOPK].rearrange("p (k n) -> p k n", k=KD)
        junk = qs[:, 2, :, :]
        junk_eq = arena[:, 13312:13824].bitcast(BF16).rearrange("p (b n) -> p b n", n=P)
        qf = arena[:, 6144:8192].rearrange("p (a t) -> p a t", a=NPS)
        rem = arena[:, 8192:10240].rearrange("p (a t) -> p a t", a=NPS)
        parts = arena[:, 10240:13312].bitcast(BF16).rearrange("p (a s t) -> p a s t", a=NPS, s=3)
        row = arena[:, 13824:15872].rearrange("p (b n) -> p b n", b=B)
        latqk = arena[:, 13312:14336].rearrange("p (a t) -> p a t", a=2)
        latv = arena[:, 14336:15360].rearrange("p (a t) -> p a t", a=2)
        oT = [arena[:, w:w + 1024].rearrange("p (k t) -> p k t", k=KD) for w in (8192, 9216, 12288, 13312)]
        up_sb = arena[:, 0:2816].bitcast(BF16).rearrange("p (k e f) -> p k e f", k=KD, e=E0)
        dn_sb = arena[:, 2816:5888].bitcast(BF16).rearrange("p (m e d) -> p m e d", m=3, e=E0)
        shu_sb = arena[:, 5888:6592].rearrange("p (k f) -> p k f", k=KD)
        shd_sb = arena[:, 6592:7360].rearrange("p (m d) -> p m d", m=3)
        hsf = arena[:, 7360:8896].rearrange("p (m t) -> p m t", m=3)
        hs = arena[:, 8896:10432].rearrange("p (m t) -> p m t", m=3)
        xs = arena[:, 10432:10944].bitcast(BF16).rearrange("p (t d) -> p t d", t=TQ)
        xeT = arena[:, 10944:11968].bitcast(BF16).rearrange("p (a k t) -> p a k t", a=2, k=KD)
        hr = arena[:, 11968:12736].bitcast(BF16).rearrange("p (m t) -> p m t", m=3)
        hq = arena[:, 12736:14272].bitcast(BF16).rearrange("p (a m t) -> p a m t", a=2, m=3)
        ge, sc, eq, hit = (arena[:, 14336 + 512 * i:14848 + 512 * i].rearrange("p (t e) -> p t e", t=NT)
                           for i in range(4))
        bi, mx8, ixf = (oN_flat[:, 128 * i:128 * i + 128].rearrange("p (t e) -> p t e", t=NT) for i in range(3))
        ix8 = oN_flat[:, 384:512].bitcast(U32).rearrange("p (t e) -> p t e", t=NT)
        ew = arena[:, 10240:11264].rearrange("p (a n) -> p a n", a=2)
        hf = arena[:, 11264:12288].rearrange("p (a t) -> p a t", a=2)
        g1 = arena[:, 12288:12800].rearrange("p (t e) -> p t e", t=NT)

        ids_sb = sb("ids_sb", [P, NT], I32)
        loraB_sb = sb("loraB_sb", [R, D])
        wq_sb = sb("wq_sb", [P, KD, D])
        wk_sb = sb("wk_sb", [P, KD, D])
        wv_sb = sb("wv_sb", [P, KD, D])
        wi1_sb = sb("wi1_sb", [P, KD, P])
        wi2_sb = sb("wi2_sb", [P, 1])
        wo_sb = sb("wo_sb", [P, KD, D])
        gw_sb = sb("gw_sb", [P, KD, E0])
        es_sb = sb("es_sb", [P, KD, E1])
        wl_sb = sb("wl_sb", [P, KD, 4, LAT])
        wh_sb = sb("wh_sb", [P, 3, D])
        bq_sb = sb("bq_sb", [P, KD])
        bq4 = sb("bq4", [P, KD])
        bk_sb = sb("bk_sb", [P, KD])
        bi1_sb = sb("bi1_sb", [P, 1])
        bi2_sb = sb("bi2_sb", [P, 1])
        bv_sb = sb("bv_sb", [P, D])
        bo_sb = sb("bo_sb", [P, D])
        bp_sb = sb("bp_sb", [P, D])
        eb_sb = sb("eb_sb", [P, E0])
        ident = sb("ident", [P, P])
        identb = sb("identb", [P, P], BF16)
        causal = sb("causal", [P, P], BF16)
        before = sb("before", [P, P])
        iota = sb("iota", [P, TOPK])
        eps = sb("eps", [P, 1])
        post = sb("post", [P, 2])
        st = sb("st", [P, TQ, 6])
        mv = sb("mv", [P, TQ, 2])
        sd = sb("sd", [P, TQ])
        rstd = sb("rstd", [P, TQ])
        impc = sb("impc", [P, B, 8])
        rkp = sb("rkp", [P, 8, 4])
        rank = sb("rank", [P, 8])
        mA = sb("mA", [P, G4, 8])
        mB = sb("mB", [P, G4, 4])
        mbf = sb("mbf", [P, G4, 8], BF16)
        mT = sb("mT", [32, 3, P], BF16)
        rden = sb("rden", [P, 2, TQ, G4])
        g0 = sb("g0", [P, NT, E0])

        qd = nc.dram_tensor("q_parts", [3, B, D, S], BF16, kind="Internal").ap()
        kd = nc.dram_tensor("k_parts", [3, B, D, S], BF16, kind="Internal").ap()

        ids_in, table_in = sem("ids_in"), [sem(f"rows_in{c}") for c in range(NQ)]
        w_emb, w_l0, w_l0b, w_proj_in, w_l1 = sem("w_emb"), sem("w_l0"), sem("w_l0b"), sem("w_proj_in"), sem("w_l1")
        w_moe, w_moeb = sem("w_moe"), sem("w_moeb")
        consts, ones_in = sem("consts"), sem("ones_ready")
        vlink = sem("vlink")
        plink = sem("plink")
        act_left, dve_left = sem("act_left_psum"), sem("dve_left_psum")
        aT_mm, aT_sb = sem("aT_mm"), sem("aT_sb")
        prod, taken = sem("quad_product"), sem("quad_taken")
        var_in, sd_in, xn_in = sem("var_ready"), sem("sd_ready"), sem("xn_ready")
        tr_mm, xT_in = sem("xn_transposed"), sem("xT_ready")
        biased = sem("bias_in_residual")
        ih_mm, hi_in, imp_mm, imp_in = sem("ih_mm"), sem("hi_ready"), sem("imp_mm"), sem("imp_ready")
        sel_in, xc_mm, xc_in = sem("sel_ready"), sem("xc_mm"), sem("xc_ready")
        pc_mm, pc_f, pc_12, pc_3 = sem("piece_mm"), sem("piece_f"), sem("piece_12"), sem("piece_3")
        pc_out = [sem(f"piece_out{a}") for a in range(NPS)]
        v_mm, v_in = sem("v_mm"), sem("v_ready")
        lat_mm, lat_in = sem("lat_mm"), sem("lat_ready")
        gate_mm, gate_e = sem("gate_mm"), sem("gate_e")
        qk_in = [[sem(f"qk_in{l}{a}") for a in range(3)] for l in range(2)]
        mrow_in = [[sem(f"mrow_in{l}{a}") for a in range(3)] for l in range(2)]
        o_mm, oT_in = sem("out_turned"), sem("out_columns")
        rden_in = [sem(f"denominators{l}") for l in range(2)]
        st_mm = [sem(f"scores_ready{l}") for l in range(2)]
        p_in = [sem(f"probs_ready{l}") for l in range(2)]
        p_cut = [sem(f"probs_masked{l}") for l in range(2)]
        p_free = [sem(f"probs_free{l}") for l in range(2)]
        o_free = [sem(f"out_bank_free{l}") for l in range(2)]
        mx_mm = [sem(f"ring_step{l}") for l in range(2)]
        mx_free = [sem(f"ring_bank_free{l}") for l in range(2)]
        m_in = [sem(f"max_ready{l}") for l in range(2)]
        mT_in = [sem(f"max_row_ready{l}") for l in range(2)]
        vst_in = [sem(f"unit_values{l}") for l in range(2)]
        sh_mm, sh_f, sh_in, sh_dn = sem("sh_mm"), sem("sh_relu"), sem("sh_square"), sem("sh_down")
        xs_in, xe_mm, xe_in = sem("xs_ready"), sem("xe_mm"), sem("xe_ready")
        up_mm, up_f, up_in, dn_mm = sem("up_mm"), sem("up_relu"), sem("up_square"), sem("down_done")
        ew_in = [sem("expert_weights0"), sem("expert_weights1")]
        xp_in, ewp_hi, ewp_in = sem("x_low"), sem("expert_weight_high"), sem("expert_weight_low")
        ex_mm, ex_f, ex_lo = sem("ex_up"), sem("ex_relu"), sem("ex_low_part")
        ey_mm, ey_add = sem("ex_down"), sem("ex_added")
        stored = sem("stored")

        NFIRST, NCONST = 2, 7
        RING = (4, 5, 7)
        PLANS = [Plan(0), Plan(1)]
        NPC0 = 12

        def kparts(w, k=KD):
            return w.rearrange("(k p) n -> p k n", k=k)

        def arena_free(eng, layer):
            eng.wait_ge(v_mm, 6 if layer == 0 else 6 + NT)
            eng.wait_ge(act_left, 2 if layer == 0 else 6)
            eng.wait_ge(dve_left, 2 if layer == 0 else 6)

        block = ctx.enter_context(nc.Block())

        @block.sync
        def _(sp):
            sp.dma_start(ids_sb[:], ids).then_inc(ids_in, 16)
            sp.dma_start(loraB_sb[:], loraB).then_inc(w_emb, 16)
            for dst, src in ((wi1_sb[:], kparts(wi1)), (wi2_sb[:], wi2), (bi1_sb[:], bi1),
                             (bi2_sb[:], bi2.partition_broadcast(P)),
                             (wq_sb[:], kparts(wq)), (bq_sb[:], bq)):
                sp.dma_start(dst, src).then_inc(w_l0, 16)
            for dst, src in ((wk_sb[:], kparts(wk)), (wv_sb[:], kparts(wv)), (bk_sb[:], bk),
                             (bv_sb[:], bv.partition_broadcast(P)),
                             (bo_sb[:], bo.partition_broadcast(P))):
                sp.dma_start(dst, src).then_inc(w_l0b, 16)
            sp.dma_start(wo_sb[:], kparts(wo)).then_inc(w_proj_in, 16)
            sp.wait_ge(consts, NCONST)
            for i, w in enumerate((wq_lat, wk_lat, wv_lat, wv_lat)):
                sp.dma_start(wl_sb[:, :, i, :], kparts(w)).then_inc(w_l1, 16)
            for i, (w, r) in enumerate(((wq_heads, 0), (wk_heads, LAT), (wv_heads, 0))):
                sp.dma_start(wh_sb[r:r + LAT, i, :], w).then_inc(w_l1, 16)
            for dst, src in ((bp_sb[:], b_proj.partition_broadcast(P)), (gw_sb[:], kparts(gate_w)),
                             (eb_sb[:], e_bias.partition_broadcast(P)), (es_sb[:], kparts(e_sel))):
                sp.dma_start(dst, src).then_inc(w_l1, 16)

            def store_pieces(first, n, where, base):
                for s in range(first, first + n):
                    sp.wait_ge(pc_3, s + 1)
                    sp.wait_ge(pc_12, s + 1)
                    dst, b, cg, c0, w = where(s - base)
                    sp.dma_start(dst[:, b, cg * P:(cg + 1) * P, c0:c0 + w].rearrange("s p t -> p s t"),
                                 parts[:, s % NPS, :, 0:w]).then_inc(pc_out[s % NPS], 16)

            def load(layer, u, a):
                nk = TOPK if layer == 0 else S
                for src, dst, sel_, w in ((qd, qs, QPART, S), (kd, ks, KPART, nk)):
                    for r, part in enumerate(sel_):
                        rows_ = src[part].rearrange("b (g j r) t -> (b g) r j t", g=G4, j=G4)
                        sp.dma_start(dst[16 * r:16 * r + 16, a, :, 0:w],
                                     rows_[ds(u, 1), :, :, 0:w].rearrange("o r j t -> (o r) j t"))\
                          .then_inc(qk_in[layer][a], 16)

            def pieces_stored(n):
                for a in range(NPS):
                    sp.wait_ge(pc_out[a], 16 * ((n - a + NPS - 1) // NPS))

            def first_loads(layer, n):
                pieces_stored(n)
                sp.wait_ge(dve_left, 1 if layer == 0 else 5)
                load(layer, 0, 0)
                load(layer, 1, 1)

            def attention_dma(layer):
                def mrow(u, a):
                    sp.wait_ge(mT_in[layer], u + 1)
                    sp.dma_start(qs[QROWS:QROWS + 1, a, :, :].rearrange("o h (q j) -> o (h q) j", j=P),
                                 mT[:, a, :]).then_inc(mrow_in[layer][a], 16)

                plan = PLANS[layer]
                arena_free(sp, layer)
                mrow(0, 0)
                with sp.Fori(0, (NU - 2) // 3) as i:
                    for d in range(3):
                        v = 3 * i + 2 + d
                        sp.wait_ge(p_free[layer], plan.ne * (3 * i + d) + 2)
                        load(layer, v, (2 + d) % 3)
                        mrow(v - 1, (1 + d) % 3)
                mrow(NU - 1, (NU - 1) % 3)

            def q0(i):
                b, i = divmod(i, 6)
                return (qd, b, i // 2, (i % 2) * QW, QW) if i < 4 else (kd, b, i - 4, 0, TOPK)

            store_pieces(0, NPC0 // B, q0, 0)
            first_loads(0, NPC0 // B)
            store_pieces(NPC0 // B, NPC0 // B, q0, 0)
            pieces_stored(NPC0)
            attention_dma(0)

            sp.dma_start(wq_sb[:], kparts(w_proj)).then_inc(w_proj_in, 16)

            sp.wait_ge(dve_left, 3)
            sp.wait_ge(act_left, 3)
            sp.dma_start(shu_sb[:, :, :], kparts(sh_up)).then_inc(w_moe, 16)
            for m, (c, n) in enumerate(HCH):
                sp.dma_start(shd_sb[0:n, m, :], sh_down[c:c + n, :]).then_inc(w_moe, 16)
            def q1(i):
                c, i = divmod(i, 4)
                return (qd if i < 2 else kd, c // 2, i % 2, (c % 2) * QW, QW)

            store_pieces(NPC0, 8, q1, NPC0)
            first_loads(1, NPC0 + 8)
            store_pieces(NPC0 + 8, 8, q1, NPC0)
            pieces_stored(NPC0 + 16)
            attention_dma(1)

            def expert(e, a):
                sp.dma_start(ew[:, a, 0:D].rearrange("p (k f) -> p k f", k=KD),
                             e_keys.rearrange("e (k p) f -> e p k f", k=KD)[ds(e, 1), :, :, :]
                             .rearrange("o p k f -> (o p) k f")).then_inc(ew_in[a], 16)
                sp.dma_start(ew[:, a, D:2 * D], e_values[ds(e, 1), :, :].rearrange("o p n -> (o p) n"))\
                  .then_inc(ew_in[a], 16)

            sp.wait_ge(dve_left, 7)
            sp.wait_ge(act_left, 7)
            expert(0, 0)
            expert(1, 1)
            with sp.Fori(0, E1 - 3, 2) as e:
                for a in range(2):
                    sp.wait_ge(ewp_in, e + a + 1)
                    expert(e + a + 2, a)
            for c in range(NQ):
                sp.wait_ge(ey_add, 8 + NT * (E1 - 1) + (c + 1) * TQ)
                sp.dma_start(out[c * QW:(c + 1) * QW, :].rearrange("(t p) d -> p t d", p=P),
                             h[:, c * TQ:(c + 1) * TQ, :]).then_inc(stored, 16)
            sp.wait_ge(stored, 16 * NQ)

        @block.gpsimd
        def _(pool):
            own = [0]

            def link(ins):
                own[0] += 1
                ins.then_inc(plink, 1)
                pool.wait_ge(plink, own[0])

            def constant(ins):
                ins.then_inc(consts, 1)

            link(nc.gpsimd.memset(ident[:], 0.0))
            constant(nc.gpsimd.affine_select(out=ident[:], in_=ident[:], compare_op=ALU.not_equal, fill=1.0, base=0,
                                             pattern=[[-1, P]], channel_multiplier=1))
            constant(nc.gpsimd.memset(eps[:], EPS))
            pool.wait_ge(ids_in, 16)
            for t in range(NT):
                nc.gpsimd.indirect_dma_start(
                    rows[:, t, :], None, table,
                    bass.IndirectOffsetOnAxis(ids_sb[:, t:t + 1].bitcast(U32), 0)).then_inc(table_in[t // TQ], 16)
            link(nc.gpsimd.memset(before[:], 1.0))
            constant(nc.gpsimd.affine_select(out=before[:], in_=before[:], compare_op=ALU.is_gt, fill=0.0, base=0,
                                             pattern=[[-1, P]], channel_multiplier=1))
            constant(nc.gpsimd.iota(iota[:], pattern=[[1, TOPK]], base=0, channel_multiplier=0,
                                    allow_small_or_imprecise_dtypes=True))
            constant(nc.gpsimd.tensor_copy(identb[:], ident[:]))
            link(nc.gpsimd.memset(causal[:], 0.0))
            constant(nc.gpsimd.affine_select(out=causal[:], in_=causal[:], compare_op=ALU.is_ge, fill=MASKED, base=0,
                                             pattern=[[-1, P]], channel_multiplier=1))
            constant(nc.gpsimd.memset(wh_sb[:], 0.0))

            def add_bias(first, bias):
                for c in range(NQ):
                    pool.wait_ge(xn_in, first + c + 1)
                    hc = h[:, c * TQ:(c + 1) * TQ, :]
                    nc.gpsimd.tensor_tensor(hc, hc, bias[:].unsqueeze(1).broadcast_to([P, TQ, D]), ALU.add)\
                      .then_inc(biased, 1)

            def third_part(s, w):
                a = s % NPS
                pool.wait_ge(pc_12, s + 1)
                if s >= NPS:
                    pool.wait_ge(pc_out[a], 16 * (s // NPS))
                nc.gpsimd.tensor_tensor(parts[:, a, 2, 0:w], rem[:, a, 0:w], parts[:, a, 1, 0:w],
                                        ALU.subtract).then_inc(pc_3, 1)

            def second_part(s, w):
                a = s % NPS
                pool.wait_ge(pc_f, s + 1)
                if s >= NPS:
                    pool.wait_ge(pc_out[a], 16 * (s // NPS))
                link(nc.gpsimd.tensor_tensor(rem[:, a, 0:w], qf[:, a, 0:w], parts[:, a, 0, 0:w], ALU.subtract))
                nc.gpsimd.tensor_copy(parts[:, a, 1, 0:w], rem[:, a, 0:w]).then_inc(pc_12, 1)

            def attention_pool(layer):
                plan = PLANS[layer]
                ne, nch, keys, cuts = plan.ne, plan.nch, plan.chunk, plan.cuts

                def stage_values(u, a):
                    nc.gpsimd.tensor_copy(vst[0:keys, a, 0:nch, :, :].rearrange("p c j r -> p (c j r)"),
                                          vaug[0:keys, ds(u, 1), 0:nch, :, :].rearrange("p u c j r -> p (u c j r)"))\
                      .then_inc(vst_in[layer], 1)

                def cut_probs(i, u):
                    g = cuts[i]
                    pool.wait_ge(p_in[layer], 2 * ne * u + 2 * g + 2)
                    pool.wait_ge(p_cut[layer], len(cuts) * u + i + 1)
                    nc.gpsimd.tensor_tensor(post[:, 0:1], eps[:], eps[:], ALU.add)
                    d = pT[:, g % 2, :, 0:P]
                    nc.gpsimd.affine_select(out=d, in_=d, compare_op=ALU.is_ge, fill=0.0, base=0,
                                            pattern=[[0, G4], [1, P]], channel_multiplier=-1)\
                      .then_inc(p_cut[layer], 1)

                def unit(this, first=False, last=False):
                    u, _, _, _ = this
                    if cuts:
                        cut_probs(0, u)
                    if not last:
                        v, a, _ = after(this)
                        if not first:
                            pool.wait_ge(p_free[layer], ne * (u - 1) + 2)
                        stage_values(v, a)
                    for i in range(1, len(cuts)):
                        cut_probs(i, u)

                arena_free(pool, layer)
                pool.sem_inc(p_cut[layer], 1)
                pool.wait_ge(v_in, 6 if layer == 0 else 6 + NT)
                stage_values(0, 0)
                first, middle, last = plan.units()
                unit(first, first=True)
                with pool.Fori(0, (NU - 2) // 3) as i:
                    for d in range(3):
                        unit(middle(i, d))
                unit(last, last=True)

            pool.wait_ge(w_l0b, 16 * 5)
            add_bias(0, bo_sb)
            nc.gpsimd.memset(vaug[:], 1.0).then_inc(ones_in, 1)
            pool.wait_ge(ones_in, 1)
            nc.gpsimd.memset(ks[QROWS:QROWS + 1, :, :, :], -1.0).then_inc(ones_in, 1)
            pool.wait_ge(ones_in, 2)
            for s in range(NPC0):
                w = QW if s % 6 < 4 else TOPK
                second_part(s, w)
                third_part(s, w)
            for a in range(NPS):
                pool.wait_ge(pc_out[a], 16 * NPC0 // NPS)
            attention_pool(0)
            pool.wait_ge(dve_left, 3)
            pool.wait_ge(act_left, 3)
            for k in range(KD):
                nc.gpsimd.dma_start(up_sb[:, k, :, :], w_up[k * P:(k + 1) * P, :].rearrange("p (e f) -> p e f", e=E0))\
                  .then_inc(w_moeb, 16)
            for m, (c, n) in enumerate(HCH):
                nc.gpsimd.dma_start(dn_sb[0:n, m, :, :], w_down[c:c + n, :].rearrange("p (e d) -> p e d", e=E0))\
                  .then_inc(w_moeb, 16)
            pool.wait_ge(w_l1, 16 * 11)
            add_bias(8, bp_sb)
            for s in range(NPC0, NPC0 + 16):
                third_part(s, QW)
            for a in range(NPS):
                pool.wait_ge(pc_out[a], 16 * (NPC0 + 16) // NPS)
            attention_pool(1)

            for c in range(NQ):
                t = slice(c * QW, (c + 1) * QW)
                pool.wait_ge(xT_in, 12 + c + 1)
                nc.gpsimd.tensor_tensor(xp[:, 1, :, t], xT[:, :, t], xp[:, 0, :, t].bitcast(F32), ALU.subtract)\
                  .then_inc(xp_in, 1)

            def split_weights(e, a):
                pool.wait_ge(ewp_hi, e + 1)
                nc.gpsimd.tensor_tensor(ewp[:, a, 1, :], ew[:, a, :], ewp[:, a, 0, :].bitcast(F32), ALU.subtract)\
                  .then_inc(ewp_in, 1)

            def low_parts(e, a):
                for c in range(NQ):
                    t = slice(c * QW, (c + 1) * QW)
                    pool.wait_ge(ex_f, NQ * e + c + 1 + NQ)
                    nc.gpsimd.tensor_tensor(hp[:, a, 1, t], hf[:, c % 2, :], hp[:, a, 0, t].bitcast(F32),
                                            ALU.subtract).then_inc(ex_lo, 1)

            pool.sem_inc(ex_lo, 2)
            split_weights(0, 0)
            with pool.Fori(0, E1 - 3, 2) as e:
                for a in range(2):
                    low_parts(e + a, a)
                    split_weights(e + a + 1, 1 - a)
            low_parts(E1 - 2, 0)
            split_weights(E1 - 1, 1)
            low_parts(E1 - 1, 1)

        @block.vector
        def _(dve):
            own = [0]

            def link(ins):
                own[0] += 1
                ins.then_inc(vlink, 1)
                dve.wait_ge(vlink, own[0])

            def layernorm(i, c):
                statistics(c)
                normalize(i, c)

            def statistics(c):
                for t in range(TQ):
                    ins = nc.vector.bn_stats(st[:, t, :], h[:, c * TQ + t, :])
                link(ins)
                for t in range(TQ):
                    ins = nc.vector.bn_aggr(mv[:, t, :], st[:, t, :])
                ins.then_inc(var_in, 1)

            def normalize(i, c):
                dve.wait_ge(sd_in, 4 * i + c + 1)
                link(nc.vector.reciprocal(rstd[:], sd[:]))
                for t in range(TQ):
                    ins = nc.vector.tensor_scalar(xn[:, c * TQ + t, :], h[:, c * TQ + t, :], mv[:, t, 0:1],
                                                  rstd[:, t:t + 1], ALU.subtract, ALU.mult)
                ins.then_inc(xn_in, 1)

            def quad_banks(c):
                return ps[:, 2 * (c % 2):2 * (c % 2) + 2, :].rearrange("p a (b d) -> p (a b) d", d=D)

            def split_piece(s, w):
                a = s % NPS
                dve.wait_ge(pc_f, s + 1)
                if s >= NPS:
                    dve.wait_ge(pc_out[a], 16 * (s // NPS))
                    dve.wait_ge(pc_3, s - NPS + 1)
                link(nc.vector.tensor_tensor(rem[:, a, 0:w], qf[:, a, 0:w], parts[:, a, 0, 0:w], ALU.subtract))
                nc.vector.tensor_copy(parts[:, a, 1, 0:w], rem[:, a, 0:w]).then_inc(pc_12, 1)

            def attention_dve(layer):
                plan = PLANS[layer]
                nm = plan.nm

                def max_step(i, v, bank, ring):
                    qt, k0, w, hd, per = plan.maxes[i]
                    dve.wait_ge(mx_mm[layer], ring + 1)
                    if layer == 0:
                        o = mbf[:, hd:hd + per, qt]
                    else:
                        o = mA[:, hd:hd + per, qt] if k0 == 0 else mB[:, hd:hd + per, qt - 4]
                    nc.vector.tensor_reduce(o, ps[:, bank, 0:per * w].rearrange("p (j k) -> p j k", j=per),
                                            AX.X, ALU.max).then_inc(mx_free[layer], 1)
                    if i < nm - 1:
                        return
                    dve.wait_ge(mx_free[layer], ring + 4)
                    if layer == 0:
                        dve.sem_inc(m_in[layer], 1)
                    else:
                        nc.vector.tensor_copy(mbf[:, :, 0:4], mA[:, :, 0:4])
                        nc.vector.tensor_tensor(mbf[:, :, 4:8], mA[:, :, 4:8], mB[:, :, :], ALU.max)\
                          .then_inc(m_in[layer], 1)

                def max_row(a, bank, ring):
                    dve.wait_ge(mx_mm[layer], ring + 1)
                    nc.vector.tensor_copy(mT[:, a, :], ps[0:32, bank, 0:64].bitcast(BF16))\
                      .then_inc(mx_free[layer], 1)
                    dve.wait_ge(mx_free[layer], ring + 4)
                    dve.sem_inc(mT_in[layer], 1)

                def norm(u, qh, bank, ring):
                    o = ps[:, bank, :].rearrange("p (t j r) -> p t j r", t=TQ, j=G4)
                    dve.wait_ge(mx_mm[layer], ring + 1)
                    nc.vector.reciprocal(rden[:, qh, :, :].unsqueeze(3), o[:, :, :, HD:HD + 1]).then_inc(rden_in[layer], 1)
                    dve.wait_ge(rden_in[layer], 2 * u + qh + 1)
                    nc.vector.tensor_tensor(
                        oN[:, TQ * qh:TQ * qh + TQ, ds(u, 1), :, :].rearrange("p t u j r -> p (t u) j r"),
                        o[:, :, :, 0:HD], rden[:, qh, :, :].unsqueeze(3).broadcast_to([P, TQ, G4, HD]), ALU.mult)\
                      .then_inc(mx_free[layer], 1)

                def unit(this, phase, **ends):
                    u, a, _, ring = this
                    v, b, _ = after(this)
                    k = 0
                    for what, *i in plan.of(**ends):
                        at = (RING[(phase + k) % 3], ring + k)
                        if what == "max":
                            max_step(i[0], v, *at)
                        elif what == "maxrow":
                            max_row(b, *at)
                        elif what == "turn":
                            norm(u, i[0], *at)
                        elif what == "lastturn":
                            norm(u - 1, i[0], *at)
                        else:
                            continue
                        k += 1

                dve.sem_inc(mx_free[layer], 3)
                for i in range(nm):
                    max_step(i, 0, RING[i % 3], i)
                max_row(0, RING[nm % 3], nm)
                first, middle, last = plan.units()
                unit(first, first[3], first=True, last=False)
                with dve.Fori(0, (NU - 2) // 3) as i:
                    for d in range(3):
                        unit(middle(i, d), middle(0, d)[3], first=False, last=False)
                unit(last, last[3], first=False, last=True)
                dve.wait_ge(mx_free[layer], last[3] + 3 + 3)

            def pick(tiles, scores, ne, ntop, values, gates):
                span = slice(tiles[0], tiles[-1] + 1)
                for t in tiles:
                    ins = nc.vector.max(mx8[:, t, :], values[:, t, :])
                link(ins)
                for t in tiles:
                    ins = nc.vector.max_index(ix8[:, t, :], mx8[:, t, :], values[:, t, :])
                link(ins)
                link(nc.vector.tensor_copy(ixf[:, span, :], ix8[:, span, :]))
                io = iota[:, 0:ne].unsqueeze(1).broadcast_to([P, len(tiles), ne])
                for j in range(ntop):
                    dst = hit if j == 0 else eq
                    link(nc.vector.tensor_tensor(dst[:, span, 0:ne], io,
                                                 ixf[:, span, j:j + 1].broadcast_to([P, len(tiles), ne]),
                                                 ALU.is_equal))
                    if j:
                        link(nc.vector.tensor_tensor(hit[:, span, 0:ne], hit[:, span, 0:ne], eq[:, span, 0:ne],
                                                     ALU.add))
                link(nc.vector.tensor_tensor(gates[:, span, :], scores[:, span, 0:ne], hit[:, span, 0:ne], ALU.mult))

            for c in range(NQ):
                dve.wait_ge(table_in[c], 16 * TQ)
                dve.wait_ge(prod, c + 1)
                for half in range(2):
                    t0 = c * TQ + 2 * half
                    ins = nc.vector.scalar_tensor_tensor(
                        h[:, t0:t0 + 2, :], quad_banks(c)[:, 2 * half:2 * half + 2, :], 2.0,
                        rows[:, t0:t0 + 2, 0:D], ALU.mult, ALU.add)
                ins.then_inc(taken, 1)
                dve.wait_ge(taken, c + 1)
                layernorm(0, c)
            dve.sem_inc(dve_left, 1)

            dve.wait_ge(w_l0, 16 * 6)
            dve.wait_ge(consts, NCONST)
            link(nc.vector.tensor_scalar(bq4[:], bq_sb[:], 0.25, None, ALU.mult))
            dve.sem_inc(consts, 1)
            dve.wait_ge(w_l0b, 16 * 5)
            for b in range(B):
                dve.wait_ge(imp_in, 2 * b + 2)
                for t in range(8):
                    ins = nc.vector.scalar_tensor_tensor(junk_eq[:, t, :], row[:, b, t * P:(t + 1) * P], 1.0, ident[:],
                                                         ALU.mult, ALU.mult, accum_out=impc[:, b, t:t + 1])
                link(ins)
                for t in range(8):
                    me = impc[:, b, t:t + 1]
                    lo, hi_ = t * P, (t + 1) * P
                    j = junk[:, t % G4, :]
                    if t > 0:
                        nc.vector.tensor_scalar(j[:, 0:lo], row[:, b, 0:lo], me, None, ALU.is_ge, ALU.add,
                                                accum_out=rkp[:, t, 0:1])
                    else:
                        nc.vector.memset(rkp[:, t, 0:1], 0.0)
                    if t < 7:
                        nc.vector.tensor_scalar(j[:, hi_:S], row[:, b, hi_:S], me, None, ALU.is_gt, ALU.add,
                                                accum_out=rkp[:, t, 1:2])
                    else:
                        nc.vector.memset(rkp[:, t, 1:2], 0.0)
                    nc.vector.tensor_scalar(j[:, lo:hi_], row[:, b, lo:hi_], me, None, ALU.is_gt, ALU.add,
                                            accum_out=rkp[:, t, 2:3])
                    ins = nc.vector.scalar_tensor_tensor(junk_eq[:, t, :], row[:, b, lo:hi_], me, before[:], ALU.is_equal,
                                                         ALU.mult, accum_out=rkp[:, t, 3:4])
                    if t % G4 == G4 - 1:
                        link(ins)
                link(nc.vector.tensor_reduce(rank[:], rkp[:], AX.X, ALU.add))
                if b:
                    dve.wait_ge(xc_mm, b)
                for t in range(8):
                    ins = nc.vector.tensor_scalar(sel[:, t, :], iota[:], rank[:, t:t + 1], None, ALU.is_equal)
                ins.then_inc(sel_in, 1)
                dve.wait_ge(sel_in, b + 1)
            dve.wait_ge(ones_in, 1)
            for b in range(B):
                for c, (_, n) in enumerate(KCH):
                    dve.wait_ge(v_mm, 3 * b + c + 1)
                    nc.vector.tensor_tensor(
                        vaug[0:n, 4 * b:4 * b + 4, c, :, 0:HD],
                        ps[0:n, 2 + (3 * b + c) % 2, 0:D].rearrange("p (g j r) -> p g j r", g=G4, j=G4),
                        bv_sb[0:n, :].rearrange("p (g j r) -> p g j r", g=G4, j=G4), ALU.add).then_inc(v_in, 1)
            dve.wait_ge(v_in, 6)
            dve.sem_inc(dve_left, 1)

            attention_dve(0)
            dve.sem_inc(dve_left, 1)

            def project(i):
                for c in range(NQ):
                    hc = h[:, c * TQ:(c + 1) * TQ, :]
                    dve.wait_ge(prod, 4 * (i if i == 1 else 2) + c + 1)
                    dve.wait_ge(biased, 4 * (0 if i == 1 else 1) + c + 1)
                    nc.vector.tensor_tensor(hc, quad_banks(c), hc, ALU.add).then_inc(taken, 1)
                    dve.wait_ge(taken, 4 * i + c + 1)
                    layernorm(i, c)
                dve.sem_inc(dve_left, 1)

            def sigmoid(half, ne, n):
                dve.wait_ge(gate_e, n)
                t = slice(8 * half, 8 * half + 8)
                link(nc.vector.tensor_scalar(sc[:, t, 0:ne], ge[:, t, 0:ne], 1.0, None, ALU.add))
                link(nc.vector.reciprocal(sc[:, t, 0:ne], sc[:, t, 0:ne]))

            def biased_scores(half):
                t = slice(8 * half, 8 * half + 8)
                link(nc.vector.tensor_tensor(bi[:, t, :], sc[:, t, 0:E0], eb_sb[:].unsqueeze(1).broadcast_to([P, 8, E0]),
                                             ALU.add))

            project(1)
            sigmoid(0, E0, 1)
            biased_scores(0)
            pick(range(TQ), sc, E0, 2, bi, g0)
            for c in range(NQ):
                def scaled(e, first):
                    if not first:
                        dve.wait_ge(xe_mm, E0 * c + e)
                    for t in range(TQ):
                        tt = c * TQ + t
                        ins = nc.vector.tensor_scalar(xs[:, t, :], xn[:, tt, :],
                                                      g0[:, tt, ds(e, 1)], None, ALU.mult)
                    ins.then_inc(xs_in, 1)

                def squares(e, a):
                    for m, (_, n) in enumerate(HCH):
                        dve.wait_ge(up_f, 3 * (E0 * c + e) + m + 1)
                        ins = nc.vector.tensor_tensor(hq[0:n, a, m, :], hr[0:n, m, :], hr[0:n, m, :], ALU.mult)
                        ins.then_inc(up_in, 1)

                if c:
                    dve.wait_ge(xe_mm, E0 * c)
                scaled(0, True)
                for m, (_, n) in enumerate(HCH):
                    dve.wait_ge(sh_f, 3 * c + m + 1)
                    if c:
                        dve.wait_ge(sh_dn, c)
                    nc.vector.tensor_tensor(hs[0:n, m, :], hsf[0:n, m, :], hsf[0:n, m, :], ALU.mult).then_inc(sh_in, 1)
                scaled(1, False)
                if c == 1:
                    sigmoid(1, E0, 2)
                    biased_scores(1)
                if c + 1 < NQ:
                    pick(range(TQ * (c + 1), TQ * (c + 2)), sc, E0, 2, bi, g0)
                if c:
                    dve.wait_ge(taken, 8 + c)
                    statistics(c - 1)
                    dve.wait_ge(dn_mm, E0 * c + 1)
                squares(0, 0)
                if c:
                    normalize(2, c - 1)
                with dve.Fori(0, E0 - 3, 2) as e:
                    for a in range(2):
                        scaled(e + a + 2, False)
                        dve.wait_ge(dn_mm, E0 * c + e + a + 1)
                        squares(e + a + 1, 1 - a)
                dve.wait_ge(dn_mm, E0 * c + E0 - 1)
                squares(E0 - 1, 1)
                hc = h[:, c * TQ:(c + 1) * TQ, :]
                dve.wait_ge(dn_mm, E0 * (c + 1) + 1)
                nc.vector.tensor_tensor(hc, ps[:, 0:2, :].rearrange("p a (b d) -> p (a b) d", d=D), hc, ALU.add)\
                  .then_inc(taken, 1)
            dve.wait_ge(taken, 12)
            dve.sem_inc(dve_left, 1)

            layernorm(2, NQ - 1)
            for c in range(NQ):
                for i in range(4):
                    split_piece(NPC0 + 4 * c + i, QW)
                for t in range(TQ):
                    n = c * TQ + t
                    dve.wait_ge(v_mm, 6 + n + 1)
                    nc.vector.tensor_copy(
                        vaug[:, 4 * (n // 8):4 * (n // 8) + 4, n % 8, :, 0:HD],
                        ps[:, 6 + n % 2, 0:D].rearrange("p (g j r) -> p g j r", g=G4, j=G4)).then_inc(v_in, 1)
            dve.wait_ge(v_in, 6 + NT)
            dve.sem_inc(dve_left, 1)
            attention_dve(1)
            dve.sem_inc(dve_left, 1)
            project(3)
            for half in range(2):
                sigmoid(half, E1, 3 + half)
                pick(range(8 * half, 8 * half + 8), sc, E1, TOP1, sc, g1)
            dve.sem_inc(ey_add, 8)
            with dve.Fori(0, E1) as e:
                for t in range(NT):
                    dve.wait_ge(ey_mm, NT // 2 * e + t // 2 + 1)
                    nc.vector.scalar_tensor_tensor(h[:, t, :], ps[:, 4 + (t // 2) % 4, (t % 2) * D:(t % 2 + 1) * D],
                                                   g1[:, t, ds(e, 1)], h[:, t, :], ALU.mult, ALU.add)\
                      .then_inc(ey_add, 1)

        @block.scalar
        def _(act):
            def ln_sd(i, c):
                act.wait_ge(var_in, 4 * i + c + 1)
                nc.scalar.activation(sd[:], mv[:, :, 1], ACT.Sqrt, bias=eps[:]).then_inc(sd_in, 1)

            def ln_columns(i, c):
                act.wait_ge(tr_mm, 4 * i + c + 1)
                if i == 3:
                    nc.scalar.activation(xp[:, 0, :, c * QW:(c + 1) * QW], ps[:, 4 + 2 * (c % 2):6 + 2 * (c % 2), :],
                                         ACT.Copy)
                nc.scalar.activation(xT[:, :, c * QW:(c + 1) * QW], ps[:, 4 + 2 * (c % 2):6 + 2 * (c % 2), :],
                                     ACT.Copy).then_inc(xT_in, 1)

            def ln_scalar(i, c):
                ln_sd(i, c)
                ln_columns(i, c)

            def piece(s, w, scale, bias):
                a = s % NPS
                act.wait_ge(pc_mm, s + 1)
                if s >= NPS:
                    act.wait_ge(pc_12, s - NPS + 1)
                    act.wait_ge(pc_out[a], 16 * (s // NPS))
                nc.scalar.activation(qf[:, a, 0:w], ps[:, s % 2, 0:w], ACT.Identity, bias=bias, scale=scale)
                nc.scalar.activation(parts[:, a, 0, 0:w], ps[:, s % 2, 0:w], ACT.Identity, bias=bias, scale=scale)\
                  .then_inc(pc_f, 1)

            def attention_act(layer):
                plan = PLANS[layer]
                ne = plan.ne

                def evacuate(u, qh):
                    act.wait_ge(p_free[layer], ne * u + plan.last[qh] + 3)
                    nc.scalar.activation(oc[:, qh, :], ps[:, 6, :], ACT.Copy).then_inc(o_free[layer], 1)

                def unit(u, first=False):
                    for g, (qh, c, n, q0, w) in enumerate(plan.exps):
                        for pair in range(2):
                            k = 2 * g + pair
                            act.wait_ge(st_mm[layer], 2 * ne * u + k + 1)
                            if pair == 0:
                                act.wait_ge(p_free[layer], ne * u + g + 1)
                            nc.scalar.activation(pT[0:n, g % 2, 2 * pair:2 * pair + 2, 0:w],
                                                 ps[0:n, 2 * pair:2 * pair + 2, 0:w], ACT.Exp)\
                              .then_inc(p_in[layer], 1)
                        if g == 0 and not first:
                            evacuate(u - 1, 1)
                        if g == plan.last[0] + 1:
                            evacuate(u, 0)

                first, middle, last = plan.units()
                unit(first[0], first=True)
                with act.Fori(0, (NU - 2) // 3) as i:
                    for d in range(3):
                        unit(middle(i, d)[0])
                unit(last[0])
                evacuate(last[0], 1)
                act.wait_ge(o_free[layer], 1 + 2 * NU)

            def project_act(i, n, ne):
                def out_columns(c):
                    act.wait_ge(o_mm, 4 * n + c + 1)
                    nc.scalar.activation(oT[c], ps[:, 4 + 2 * (c % 2):6 + 2 * (c % 2), :],
                                         ACT.Copy).then_inc(oT_in, 1)

                out_columns(0)
                out_columns(1)
                out_columns(2)
                ln_sd(i, 0)
                out_columns(3)
                ln_columns(i, 0)
                ln_scalar(i, 1)
                ln_scalar(i, 2)
                ln_sd(i, 3)
                for half in range(2):
                    if half:
                        ln_columns(i, 3)
                    act.wait_ge(gate_mm, 4 * n + 2 * half + 2)
                    nc.scalar.activation(ge[:, 8 * half:8 * half + 8, 0:ne],
                                         ps[:, 2 * half, 0:8 * ne].rearrange("p (t e) -> p t e", e=ne),
                                         ACT.Exp, scale=-1.0).then_inc(gate_e, 1)

            act.wait_ge(consts, NFIRST)
            for c in range(NQ):
                act.wait_ge(aT_mm, c + 1)
                nc.scalar.activation(aT[:, c * QW:(c + 1) * QW], ps[0:R, 2 * (c % 2), :], ACT.Copy).then_inc(aT_sb, 1)
                if c:
                    ln_scalar(0, c - 1)
            ln_scalar(0, NQ - 1)
            act.wait_ge(xT_in, 4)
            act.sem_inc(act_left, 1)
            act.wait_ge(w_l0, 16 * 6)
            act.wait_ge(consts, NCONST + 1)
            def hidden_importance(c):
                act.wait_ge(ih_mm, c + 1)
                if c >= 2:
                    act.wait_ge(imp_mm, c - 1)
                nc.scalar.activation(hi[:, c % 2, :], ps[:, 2 + c % 2, :], ACT.Relu, bias=bi1_sb[:]).then_inc(hi_in, 1)

            hidden_importance(0)
            for c in range(NQ):
                if c + 1 < NQ:
                    hidden_importance(c + 1)
                act.wait_ge(imp_mm, c + 1)
                nc.scalar.activation(row[:, c // 2, (c % 2) * QW:(c % 2 + 1) * QW], ps[:, 4 + c, :],
                                     ACT.Identity, bias=bi2_sb[:]).then_inc(imp_in, 1)
            for b in range(B):
                for i in range(4):
                    piece(6 * b + i, QW, 0.25, bq4[:, i // 2:i // 2 + 1])
                act.wait_ge(xc_mm, b + 1)
                nc.scalar.activation(xcT, ps[:, 6:8, 0:TOPK], ACT.Copy).then_inc(xc_in, 1)
                for i in range(2):
                    piece(6 * b + 4 + i, TOPK, 1.0, bk_sb[:, i:i + 1])
            act.wait_ge(pc_f, NPC0)
            act.sem_inc(act_left, 1)
            attention_act(0)
            act.sem_inc(act_left, 1)
            project_act(1, 0, E0)
            act.wait_ge(xT_in, 8)
            act.sem_inc(act_left, 1)
            for c in range(NQ):
                def relus(e, a, first=False):
                    for m, (_, n) in enumerate(HCH):
                        if c or not first:
                            act.wait_ge(up_in, 3 * (E0 * c + e - 1) + m + 1)
                        act.wait_ge(up_mm, 3 * (E0 * c + e) + m + 1)
                        nc.scalar.activation(hr[0:n, m, :], ps[0:n, 2 + m, :], ACT.Relu).then_inc(up_f, 1)

                def columns(e, a):
                    act.wait_ge(xe_mm, E0 * c + e + 1)
                    nc.scalar.activation(xeT[:, a, :, :].rearrange("p k t -> p (k t)"),
                                         ps[:, 5 + a, :].bitcast(BF16), ACT.Copy).then_inc(xe_in, 1)

                for m, (_, n) in enumerate(HCH):
                    act.wait_ge(sh_mm, 3 * c + m + 1)
                    if c:
                        act.wait_ge(sh_in, 3 * c)
                    nc.scalar.activation(hsf[0:n, m, :], ps[0:n, 2 + m, :], ACT.Relu).then_inc(sh_f, 1)
                columns(0, 0)
                if c:
                    ln_sd(2, c - 1)
                relus(0, 0, True)
                columns(1, 1)
                with act.Fori(0, E0 - 3, 2) as e:
                    for a in range(2):
                        relus(e + a + 1, 1 - a)
                        columns(e + a + 2, a)
                relus(E0 - 1, 1)
            act.wait_ge(up_f, 3 * E0 * NQ)
            act.sem_inc(act_left, 1)
            ln_sd(2, NQ - 1)
            for c in range(NQ - 1):
                ln_columns(2, c)
            for c in range(NQ):
                a = c % 2
                for i, lat in enumerate((latqk, latv)):
                    act.wait_ge(lat_mm, 2 * c + i + 1)
                    nc.scalar.activation(lat[:, a, :], ps[:, 2 + i, :], ACT.Copy).then_inc(lat_in, 1)
                for i in range(4):
                    piece(NPC0 + 4 * c + i, QW, 0.25 if i < 2 else 1.0, 0.0)
                if c == 0:
                    ln_columns(2, NQ - 1)
            act.wait_ge(pc_f, NPC0 + 16)
            act.sem_inc(act_left, 1)
            attention_act(1)
            act.sem_inc(act_left, 1)
            project_act(3, 1, E1)
            act.wait_ge(xT_in, 16)
            act.sem_inc(act_left, 1)
            act.wait_ge(xn_in, 16)
            def hidden(e, a):
                for c in range(NQ):
                    act.wait_ge(ex_mm, NQ * e + c + 1)
                    act.wait_ge(ex_lo, NQ * e + c + 1)
                    nc.scalar.activation(hf[:, c % 2, :], ps[:, c, :], ACT.Relu)
                    nc.scalar.activation(hp[:, a, 0, c * QW:(c + 1) * QW], ps[:, c, :], ACT.Relu)\
                      .then_inc(ex_f, 1)

            def high_weights(e, a):
                act.wait_ge(ew_in[a], 16 * (e - a + 2))
                nc.scalar.activation(ewp[:, a, 0, :], ew[:, a, :], ACT.Copy).then_inc(ewp_hi, 1)

            high_weights(0, 0)
            act.sem_inc(ex_f, NQ)
            with act.Fori(0, E1 - 3, 2) as e:
                for a in range(2):
                    hidden(e + a, a)
                    act.wait_ge(ey_add, NT * (e + a) + 8)
                    high_weights(e + a + 1, 1 - a)
            hidden(E1 - 2, 0)
            act.wait_ge(ey_add, NT * (E1 - 2) + 8)
            high_weights(E1 - 1, 1)
            hidden(E1 - 1, 1)

        @block.tensor
        def _(pe):
            def stage(n):
                pe.wait_ge(act_left, n)
                pe.wait_ge(dve_left, n)

            def transposes(i, c):
                pe.wait_ge(xn_in, 4 * i + c + 1)
                if c >= 2:
                    pe.wait_ge(xT_in, 4 * i + c - 1)
                for t in range(TQ):
                    for k in range(KD):
                        mm = pe.transpose(ps[:, 4 + 2 * (c % 2) + k, t * P:(t + 1) * P],
                                          xn[:, c * TQ + t, k * P:(k + 1) * P], ident[:])
                mm.then_inc(tr_mm, 1)

            def attention_pe(layer):
                plan = PLANS[layer]
                ne, nm, cuts, chunk = plan.ne, plan.nm, plan.cuts, plan.chunk

                def scores(g, pair, u, a, first):
                    qh, c, n, q0, w = plan.exps[g]
                    k = 2 * g + pair
                    if not first or k >= 2:
                        pe.wait_ge(p_in[layer], 2 * ne * u + k - 1)
                    for j in range(2):
                        hd = 2 * pair + j
                        mm = pe.matmul(ps[0:n, 2 * pair + j, 0:w], ks[0:QROWS + 1, a, hd, c * chunk:c * chunk + n],
                                       qs[0:QROWS + 1, a, hd, qh * QW + q0:qh * QW + q0 + w],
                                       start=True, stop=True)
                    mm.then_inc(st_mm[layer], 1)

                def values(g, u, a):
                    qh, c, n, q0, w = plan.exps[g]
                    pe.wait_ge(p_in[layer], 2 * ne * u + 2 * g + 2)
                    if g in cuts:
                        pe.wait_ge(p_cut[layer], len(cuts) * u + cuts.index(g) + 2)
                    if g in plan.first:
                        pe.wait_ge(o_free[layer], 2 * u + qh + 1)
                    for j in range(G4):
                        mm = pe.matmul(ps[32 * j:32 * j + 32, 6, q0:q0 + w], vst[0:n, a, c, j, :],
                                       pT[0:n, g % 2, j, 0:w], start=(g in plan.first), stop=(g in plan.last),
                                       skip_group_check=True)
                    mm.then_inc(p_free[layer], 1)

                def turn(u, qh, bank, ring):
                    pe.wait_ge(o_free[layer], 2 * u + qh + 2)
                    pe.wait_ge(mx_free[layer], ring + 1)
                    for t in range(TQ):
                        mm = pe.transpose(ps[:, bank, t * P:(t + 1) * P], oc[:, qh, t * P:(t + 1) * P], ident[:])
                    mm.then_inc(mx_mm[layer], 1)

                def max_scores(i, a, bank, ring):
                    qt, k0, w, hd, per = plan.maxes[i]
                    pe.wait_ge(mx_free[layer], ring + 1)
                    diagonal = layer == 1 and k0 + w == (qt + 1) * P
                    for j in range(per):
                        mm = pe.matmul(ps[:, bank, j * w:(j + 1) * w], qs[0:QROWS, a, hd + j, qt * P:(qt + 1) * P],
                                       ks[0:QROWS, a, hd + j, k0:k0 + w], start=(j == 0),
                                       stop=not diagonal, skip_group_check=True)
                    if diagonal:
                        for j in range(per):
                            mm = pe.matmul(ps[:, bank, (j + 1) * w - P:(j + 1) * w], identb[:], causal[:],
                                           start=False, stop=True, skip_group_check=True)
                    mm.then_inc(mx_mm[layer], 1)

                def max_row(v, bank, ring):
                    pe.wait_ge(m_in[layer], v + 1)
                    pe.wait_ge(mx_free[layer], ring + 1)
                    pe.transpose(ps[0:32, bank, 0:64].bitcast(BF16), mbf[:].rearrange("p j q -> p (j q)"),
                                 identb[:]).then_inc(mx_mm[layer], 1)

                def unit(this, phase, **ends):
                    u, a, n, ring = this
                    v, b, nb = after(this)
                    pe.wait_ge(mrow_in[layer][a], 16 * n + 16)
                    if not ends["last"]:
                        pe.wait_ge(qk_in[layer][b], 192 * nb + 192)
                    k = 0
                    for what, *i in plan.of(**ends):
                        at = (RING[(phase + k) % 3], ring + k)
                        if what == "scores":
                            scores(*i, u, a, ends["first"])
                        elif what == "values":
                            if i[0] == 0:
                                pe.wait_ge(vst_in[layer], u + 1)
                            values(i[0], u, a)
                        elif what == "lastvalues":
                            values(i[0], u - 1, (a + 2) % 3)
                        else:
                            k += 1
                            if what == "max":
                                max_scores(i[0], b, *at)
                            elif what == "maxrow":
                                max_row(v, *at)
                            elif what == "turn":
                                turn(u, i[0], *at)
                            else:
                                turn(u - 1, i[0], *at)

                pe.sem_inc(p_free[layer], 2)
                pe.sem_inc(o_free[layer], 1)
                pe.wait_ge(ones_in, 2)
                pe.wait_ge(qk_in[layer][0], 192)
                for i in range(nm):
                    max_scores(i, 0, RING[i % 3], i)
                max_row(0, RING[nm % 3], nm)
                first, middle, last = plan.units()
                unit(first, first[3], first=True, last=False)
                with pe.Fori(0, (NU - 2) // 3) as i:
                    for d in range(3):
                        unit(middle(i, d), middle(0, d)[3], first=False, last=False)
                unit(last, last[3], first=False, last=True)

            def project(i, w, n, wg, ne):
                def out_turn(c):
                    for t in range(TQ):
                        b, tile = divmod(c * TQ + t, 8)
                        for k in range(KD):
                            mm = pe.transpose(ps[:, 4 + 2 * (c % 2) + k, t * P:(t + 1) * P],
                                              oN[:, tile, 4 * b + 2 * k:4 * b + 2 * k + 2, :, :]
                                              .rearrange("p u j r -> p (u j r)"), ident[:])
                    mm.then_inc(o_mm, 1)

                def product(c):
                    pe.wait_ge(oT_in, 4 * n + c + 1)
                    if c >= 2:
                        pe.wait_ge(taken, 4 * i + c - 1)
                    for t in range(TQ):
                        for k in range(KD):
                            mm = pe.matmul(ps[:, 2 * (c % 2) + t // 2, (t % 2) * D:(t % 2 + 1) * D],
                                           oT[c][:, k, t * P:(t + 1) * P], w[:, k, :],
                                           start=(k == 0), stop=(k == KD - 1))
                    mm.then_inc(prod, 1)

                def gates(c):
                    pe.wait_ge(xT_in, 4 * i + c + 1)
                    pe.wait_ge(taken, 4 * i + c // 2 + 3)
                    for t in range(TQ):
                        tt = c * TQ + t
                        for k in range(KD):
                            mm = pe.matmul(ps[:, 2 * (c // 2), (tt % 8) * ne:(tt % 8 + 1) * ne],
                                           xT[:, k, tt * P:(tt + 1) * P], wg[:, k, :],
                                           start=(k == 0), stop=(k == KD - 1))
                    mm.then_inc(gate_mm, 1)

                out_turn(0)
                out_turn(1)
                for c in range(NQ):
                    product(c)
                    if c < 2:
                        out_turn(c + 2)
                    if c >= 1:
                        pe.wait_ge(oT_in, 4 * n + min(c + 2, NQ))
                        transposes(i, c - 1)
                gates(0)
                gates(1)
                transposes(i, 3)
                gates(2)
                gates(3)

            pe.wait_ge(consts, NFIRST)
            pe.wait_ge(w_emb, 16)
            for c in range(NQ):
                pe.wait_ge(table_in[c], 16 * TQ)
                if c >= 2:
                    pe.wait_ge(taken, c - 1)
                for t in range(TQ):
                    mm = pe.transpose(ps[0:R, 2 * (c % 2), t * P:(t + 1) * P], rows[:, c * TQ + t, D:D + R], ident[:])
                mm.then_inc(aT_mm, 1)
                pe.wait_ge(aT_sb, c + 1)
                for t in range(TQ):
                    tt = c * TQ + t
                    mm = pe.matmul(ps[:, 2 * (c % 2) + t // 2, (t % 2) * D:(t % 2 + 1) * D],
                                   aT[:, tt * P:(tt + 1) * P], loraB_sb[:], start=True, stop=True)
                mm.then_inc(prod, 1)
                if c:
                    transposes(0, c - 1)
            transposes(0, NQ - 1)

            stage(1)
            pe.wait_ge(w_l0, 16 * 6)
            pe.wait_ge(consts, NCONST)
            for c in range(NQ + 1):
                if c < NQ:
                    pe.wait_ge(xT_in, c + 1)
                    if c >= 2:
                        pe.wait_ge(hi_in, c - 1)
                    for k in range(KD):
                        mm = pe.matmul(ps[:, 2 + c % 2, :], wi1_sb[:, k, :], xT[:, k, c * QW:(c + 1) * QW],
                                       start=(k == 0), stop=(k == KD - 1))
                    mm.then_inc(ih_mm, 1)
                if c:
                    pe.wait_ge(hi_in, c)
                    pe.matmul(ps[:, 3 + c, :], wi2_sb[:].broadcast_to([P, P]), hi[:, (c - 1) % 2, :],
                              start=True, stop=True).then_inc(imp_mm, 1)
            pe.wait_ge(w_l0b, 16 * 5)

            for b in range(B):
                for i in range(4):
                    s = 6 * b + i
                    if s >= 2:
                        pe.wait_ge(pc_f, s - 1)
                    for k in range(KD):
                        mm = pe.matmul(ps[:, s % 2, :], wq_sb[:, k, (i // 2) * P:(i // 2 + 1) * P],
                                       xT[:, k, b * S + (i % 2) * QW:b * S + (i % 2 + 1) * QW],
                                       start=(k == 0), stop=(k == KD - 1))
                    mm.then_inc(pc_mm, 1)
                pe.wait_ge(sel_in, b + 1)
                pe.wait_ge(imp_in, NQ)
                for k in range(KD):
                    for t in range(8):
                        mm = pe.matmul(ps[:, 6 + k, 0:TOPK], xn[:, 8 * b + t, k * P:(k + 1) * P], sel[:, t, :],
                                       start=(t == 0), stop=(t == 7))
                mm.then_inc(xc_mm, 1)
                pe.wait_ge(xc_in, b + 1)
                for i in range(2):
                    s = 6 * b + 4 + i
                    pe.wait_ge(pc_f, s - 1)
                    for k in range(KD):
                        mm = pe.matmul(ps[:, s % 2, 0:TOPK], wk_sb[:, k, i * P:(i + 1) * P], xcT[:, k, :],
                                       start=(k == 0), stop=(k == KD - 1))
                    mm.then_inc(pc_mm, 1)
                for c, (c0, n) in enumerate(KCH):
                    if 3 * b + c >= 2:
                        pe.wait_ge(v_in, 3 * b + c - 1)
                    for k in range(KD):
                        mm = pe.matmul(ps[0:n, 2 + (3 * b + c) % 2, 0:D], xcT[:, k, c0:c0 + n], wv_sb[:, k, :],
                                       start=(k == 0), stop=(k == KD - 1))
                    mm.then_inc(v_mm, 1)

            stage(2)
            attention_pe(0)
            stage(3)
            pe.wait_ge(w_proj_in, 16 * 2)
            pe.wait_ge(w_l1, 16 * 11)
            project(1, wo_sb, 0, gw_sb, E0)
            stage(4)
            pe.wait_ge(w_moe, 16 * 4)
            pe.sem_inc(dn_mm, 1)
            for c in range(NQ):
                def turned(e, a):
                    pe.wait_ge(xs_in, E0 * c + e + 1)
                    for t in range(TQ):
                        for k in range(KD):
                            mm = pe.transpose(ps[:, 5 + a, :].bitcast(BF16)[:, k * QW + t * P:k * QW + (t + 1) * P],
                                              xs[:, t, k * P:(k + 1) * P], identb[:])
                    mm.then_inc(xe_mm, 1)

                def up(e, a, first=False):
                    pe.wait_ge(xe_in, E0 * c + e + 1)
                    for m, (c0, n) in enumerate(HCH):
                        if not first:
                            pe.wait_ge(up_f, 3 * (E0 * c + e - 1) + m + 1)
                        for k in range(KD):
                            mm = pe.matmul(ps[0:n, 2 + m, :],
                                           up_sb[:, k, ds(e, 1), c0:c0 + n].rearrange("p e f -> p (e f)"),
                                           xeT[:, a, k, :], start=(k == 0), stop=(k == KD - 1))
                        mm.then_inc(up_mm, 1)

                def down(e, a, last):
                    for m, (_, n) in enumerate(HCH):
                        pe.wait_ge(up_in, 3 * (E0 * c + e) + m + 1)
                        for t in range(TQ):
                            mm = pe.matmul(ps[:, t // 2, (t % 2) * D:(t % 2 + 1) * D],
                                           hq[0:n, a, m, t * P:(t + 1) * P],
                                           dn_sb[0:n, m, ds(e, 1), :].rearrange("p e d -> p (e d)"),
                                           start=False, stop=last and m == 2, skip_group_check=True)
                    mm.then_inc(dn_mm, 1)

                if c:
                    pe.wait_ge(up_f, 3 * E0 * c)
                else:
                    pe.wait_ge(gate_e, 2)
                for m, (c0, n) in enumerate(HCH):
                    for k in range(KD):
                        mm = pe.matmul(ps[0:n, 2 + m, :], shu_sb[:, k, c0:c0 + n], xT[:, k, c * QW:(c + 1) * QW],
                                       start=(k == 0), stop=(k == KD - 1))
                    mm.then_inc(sh_mm, 1)
                turned(0, 0)
                if c:
                    pe.wait_ge(taken, 8 + c)
                for m, (_, n) in enumerate(HCH):
                    pe.wait_ge(sh_in, 3 * c + m + 1)
                    for t in range(TQ):
                        mm = pe.matmul(ps[:, t // 2, (t % 2) * D:(t % 2 + 1) * D], hs[0:n, m, t * P:(t + 1) * P],
                                       shd_sb[0:n, m, :], start=(m == 0 and t % 2 == 0), stop=False,
                                       skip_group_check=True)
                mm.then_inc(sh_dn, 1)
                if c == 0:
                    pe.wait_ge(w_moeb, 16 * 5)
                pe.wait_ge(sh_f, 3 * (c + 1))
                up(0, 0, True)
                turned(1, 1)
                with pe.Fori(0, E0 - 3, 2) as e:
                    for a in range(2):
                        up(e + a + 1, 1 - a)
                        turned(e + a + 2, a)
                        down(e + a, a, False)
                up(E0 - 1, 1)
                down(E0 - 2, 0, False)
                down(E0 - 1, 1, True)

            stage(5)
            for c in range(NQ - 1):
                transposes(2, c)
            for c in range(NQ):
                pe.wait_ge(xT_in, 8 + c + 1)
                if c:
                    pe.wait_ge(lat_in, 2 * c)
                for i in range(2):
                    for k in range(KD):
                        mm = pe.matmul(ps[:, 2 + i, :],
                                       wl_sb[:, k, 2 * i:2 * i + 2, :].rearrange("p a l -> p (a l)"),
                                       xT[:, k, c * QW:(c + 1) * QW], start=(k == 0), stop=(k == KD - 1))
                    mm.then_inc(lat_mm, 1)
                pe.wait_ge(lat_in, 2 * c + 1)
                for i in range(4):
                    s = NPC0 + 4 * c + i
                    pe.wait_ge(pc_f, s - 1)
                    pe.matmul(ps[:, s % 2, :], wh_sb[:, i // 2, (i % 2) * P:(i % 2 + 1) * P], latqk[:, c % 2, :],
                              start=True, stop=True).then_inc(pc_mm, 1)
                if c == 0:
                    transposes(2, NQ - 1)
                    pe.wait_ge(xT_in, 12)
                pe.wait_ge(lat_in, 2 * c + 2)
                for t in range(TQ):
                    n = c * TQ + t
                    if n >= 2:
                        pe.wait_ge(v_in, 6 + n - 1)
                    pe.matmul(ps[:, 6 + n % 2, 0:D], latv[:, c % 2, t * P:(t + 1) * P], wh_sb[:, 2, :],
                              start=True, stop=True).then_inc(v_mm, 1)
            stage(6)
            attention_pe(1)
            stage(7)
            project(3, wq_sb, 1, es_sb, E1)
            stage(8)
            pe.wait_ge(gate_e, 4)
            pe.wait_ge(xp_in, NQ)
            products = ((0, 0), (0, 1), (1, 0))
            with pe.Fori(0, E1 - 1, 2) as e:
                for a in range(2):
                    pe.wait_ge(ewp_in, e + a + 1)
                    for c in range(NQ):
                        pe.wait_ge(ex_f, NQ * (e + a) + c + 1)
                        for k in range(KD):
                            for i, (i_w, i_x) in enumerate(products):
                                mm = pe.matmul(ps[:, c, :], ewp[:, a, i_w, k * F1:(k + 1) * F1],
                                               xp[:, i_x, k, c * QW:(c + 1) * QW],
                                               start=(k == 0 and i == 0), stop=(k == KD - 1 and i == 2))
                        mm.then_inc(ex_mm, 1)
                    for t in range(NT):
                        if t % TQ == 0:
                            pe.wait_ge(ex_lo, NQ * (e + a) + t // TQ + 1 + 2)
                        if t % 2 == 0:
                            pe.wait_ge(ey_add, NT * (e + a) + t + 2)
                        for i, (i_h, i_w) in enumerate(products):
                            mm = pe.matmul(ps[:, 4 + (t // 2) % 4, (t % 2) * D:(t % 2 + 1) * D],
                                           hp[:, a, i_h, t * P:(t + 1) * P], ewp[:, a, i_w, D:2 * D],
                                           start=(i == 0), stop=(i == 2))
                        if t % 2:
                            mm.then_inc(ey_mm, 1)


def kernel(x, L0_tok_emb_weight, L0_tok_lora_A, L0_tok_lora_B, L0_attn_wq, L0_attn_bq, L0_attn_wk, L0_attn_bk,
           L0_attn_wv, L0_attn_bv, L0_attn_wo, L0_attn_bo, L0_attn_wi1, L0_attn_bi1, L0_attn_wi2, L0_attn_bi2,
           L0_ffn_gate_w, L0_ffn_expert_bias, L0_ffn_w_up, L0_ffn_w_down, L0_ffn_shared_w_up, L0_ffn_shared_w_down,
           L1_attn_wq_lat, L1_attn_wk_lat, L1_attn_wv_lat, L1_attn_wq_heads, L1_attn_wk_heads, L1_attn_wv_heads,
           L1_attn_w_proj, L1_attn_b_proj, L1_ffn_expert_sel, L1_ffn_keys, L1_ffn_values):
    import numpy as np
    import concourse.bacc as bacc
    from concourse.bass_utils import run_bass_kernel_spmd

    nc = bacc.Bacc("TRN2", target_bir_lowering=False, num_devices=1)
    A = np.asarray
    arrays = {
        "ids": A(x).reshape(NT, P).T,
        "table": np.concatenate([A(L0_tok_emb_weight), A(L0_tok_lora_A).T], axis=1),
        "loraB": A(L0_tok_lora_B).T,
        "wq": A(L0_attn_wq).T, "wk": A(L0_attn_wk).T, "wv": A(L0_attn_wv).T, "wo": A(L0_attn_wo).T,
        "wi1": A(L0_attn_wi1).T, "wi2": A(L0_attn_wi2).T,
        "bq": A(L0_attn_bq).reshape(KD, P).T, "bk": A(L0_attn_bk).reshape(KD, P).T,
        "bv": A(L0_attn_bv), "bo": A(L0_attn_bo),
        "bi1": A(L0_attn_bi1).reshape(P, 1), "bi2": A(L0_attn_bi2),
        "gate_w": A(L0_ffn_gate_w).T, "e_bias": A(L0_ffn_expert_bias),
        "w_up": A(L0_ffn_w_up).transpose(2, 0, 1).reshape(D, E0 * HID),
        "w_down": A(L0_ffn_w_down).transpose(2, 0, 1).reshape(HID, E0 * D),
        "sh_up": A(L0_ffn_shared_w_up).T, "sh_down": A(L0_ffn_shared_w_down).T,
        "wq_lat": A(L1_attn_wq_lat), "wk_lat": A(L1_attn_wk_lat), "wv_lat": A(L1_attn_wv_lat),
        "wq_heads": A(L1_attn_wq_heads), "wk_heads": A(L1_attn_wk_heads), "wv_heads": A(L1_attn_wv_heads),
        "w_proj": A(L1_attn_w_proj), "b_proj": A(L1_attn_b_proj),
        "e_sel": A(L1_ffn_expert_sel).T, "e_keys": A(L1_ffn_keys), "e_values": A(L1_ffn_values),
    }
    arrays = {f"in_{k}": np.ascontiguousarray(v) for k, v in arrays.items()}
    args = [nc.dram_tensor(k, v.shape, mybir.dt.from_np(v.dtype), kind="ExternalInput").ap() for k, v in arrays.items()]
    out = nc.dram_tensor("out", (N, D), F32, kind="ExternalOutput").ap()
    order = ["ids", "table", "loraB", "wq", "wk", "wv", "wo", "wi1", "wi2", "bq", "bk", "bv", "bo", "bi1", "bi2",
             "gate_w", "e_bias", "w_up", "w_down", "sh_up", "sh_down", "wq_lat", "wk_lat", "wv_lat",
             "wq_heads", "wk_heads", "wv_heads", "w_proj", "b_proj", "e_sel", "e_keys", "e_values"]
    by_name = dict(zip([k[3:] for k in arrays], args))
    lm_tower(nc, *[by_name[k] for k in order], out)
    r = run_bass_kernel_spmd(nc, [arrays], core_ids=[0])
    return r.results[0]["out"].reshape(B, S, D)
```
